# Optimizing a Trainium2 kernel written in Bass

```python
import numpy as np
import jax
import jax.numpy as jnp

def _softmax(x, axis=-1):
    return jax.nn.softmax(x, axis=axis)

def _gelu(x):
    return jax.nn.gelu(x, approximate=True)

def _silu(x):
    return jax.nn.silu(x)

def _sigmoid(x):
    return jax.nn.sigmoid(x)

def _layernorm(x, axis=-1, eps=1e-05):
    m = jnp.mean(x, axis=axis, keepdims=True)
    v = jnp.var(x, axis=axis, keepdims=True)
    return (x - m) / jnp.sqrt(v + eps)

def _scatter_add(tgt, idx, src, axis=0):
    return tgt.at[idx].add(src)

def _segment_sum(src, seg, n):
    return jax.ops.segment_sum(src, seg, n)
kernel_name = 'mk_audio_tower_d1_tok_audfeat512_r4_7c9cd6'

def setup_inputs(seed: int=0):
    np.random.seed(seed)
    _w = jnp.asarray

    def _rec_inputs():
        import jax
        import jax.numpy as jnp
        _rk = jax.random.key(seed)
        x = -7.10856e-05 + 0.999911 * jax.random.normal(jax.random.fold_in(_rk, 1), (8, 750, 128), jnp.float32)
        return x
    x = _rec_inputs()

    def _L0_tok_setup():
        import jax, jax.numpy as jnp
        import numpy as np
        EPS = 1e-05

        def conv1d(x, w, b, stride=1, padding=0):
            out = jax.lax.conv_general_dilated(x, w, window_strides=(stride,), padding=[(padding, padding)], dimension_numbers=('NCH', 'OIH', 'NCH'))
            return out + b[None, :, None]

        def layer_norm(x, g, b):
            mu = jnp.mean(x, axis=-1, keepdims=True)
            var = jnp.mean(jnp.square(x - mu), axis=-1, keepdims=True)
            return (x - mu) * jax.lax.rsqrt(var + EPS) * g + b
        key = jax.random.key(seed)
        ks = jax.random.split(key, 16)
        B, T, H = (64, 512, 128)
        Bn = H // 2
        s = 0.02
        return {'x': jax.random.normal(ks[0], (B, T, H), dtype=jnp.float32), 'w_compress': jax.random.normal(ks[1], (Bn, H, 1), dtype=jnp.float32) * s, 'b_compress': jnp.zeros((Bn,), dtype=jnp.float32), 'w_main': jax.random.normal(ks[2], (Bn, Bn, 3), dtype=jnp.float32) * s, 'b_main': jnp.zeros((Bn,), dtype=jnp.float32), 'w_expand': jax.random.normal(ks[3], (H, Bn, 1), dtype=jnp.float32) * s, 'b_expand': jnp.zeros((H,), dtype=jnp.float32), 'g_conv_norm': jnp.ones((H,), dtype=jnp.float32), 'b_conv_norm': jnp.zeros((H,), dtype=jnp.float32), 'w_ff1': jax.random.normal(ks[4], (Bn, H), dtype=jnp.float32) * s, 'b_ff1': jnp.zeros((Bn,), dtype=jnp.float32), 'w_ff2': jax.random.normal(ks[5], (H, Bn), dtype=jnp.float32) * s, 'b_ff2': jnp.zeros((H,), dtype=jnp.float32), 'g_ff_norm': jnp.ones((H,), dtype=jnp.float32), 'b_ff_norm': jnp.zeros((H,), dtype=jnp.float32)}
    _L0_tok_all = _L0_tok_setup()
    _L0_tok_in = {k: v for k, v in _L0_tok_all.items() if k in ('w_compress', 'b_compress', 'w_main', 'b_main', 'w_expand', 'b_expand', 'g_conv_norm', 'b_conv_norm', 'w_ff1', 'b_ff1', 'w_ff2', 'b_ff2', 'g_ff_norm', 'b_ff_norm')}
    del _L0_tok_all

    def _L0_attn_setup():
        import jax, jax.numpy as jnp
        import numpy as np
        import math
        D_MODEL = 128
        NUM_HEADS = 8
        B, L = (2, 1024)
        EPS_NORM = 1e-08
        PLASTICITY = 1.0

        def _hebbian_forward(x, qkv_w, qkv_b, out_w, out_b, decay_w, decay_b, norm_scale):
            Bsz, Lsz, D = x.shape
            H = NUM_HEADS
            E = D // H
            qkv = x @ qkv_w.T + qkv_b
            q, k, v = jnp.split(qkv, 3, axis=-1)
            q = q.reshape(Bsz, Lsz, H, E)
            k = k.reshape(Bsz, Lsz, H, E)
            v = v.reshape(Bsz, Lsz, H, E)
            q = (jax.nn.elu(q) + 1.0) / math.sqrt(E)
            k = jax.nn.elu(k) + 1.0
            decay_logits = x @ decay_w.T + decay_b
            lambdas = (0.9 + 0.1 * jax.nn.sigmoid(decay_logits)) * PLASTICITY
            log_lambdas = jnp.log(jnp.clip(lambdas, 1e-06))[..., None]
            log_lambda_cum = jnp.clip(jnp.cumsum(log_lambdas, axis=1), -50.0, 50.0)
            decay_k = jnp.exp(-log_lambda_cum)
            decay_q = jnp.exp(log_lambda_cum)
            k_decayed = k * decay_k
            q_decayed = q * decay_q
            kv = jnp.einsum('blhe,blhf->blhef', k_decayed, v)
            memory_state = jnp.cumsum(kv, axis=1)
            k_sum_decayed = jnp.cumsum(k_decayed, axis=1)
            num = jnp.einsum('blhe,blhef->blhf', q_decayed, memory_state)
            den = jnp.einsum('blhe,blhe->blh', q_decayed, k_sum_decayed)[..., None] + 1e-06
            out = (num / den).reshape(Bsz, Lsz, D)
            out = out @ out_w.T + out_b
            rnorm = jax.lax.rsqrt(jnp.mean(out * out, axis=-1, keepdims=True) + EPS_NORM)
            return out * rnorm * norm_scale
        key = jax.random.key(seed)
        ks = jax.random.split(key, 6)
        D, H = (D_MODEL, NUM_HEADS)
        std = 1.0 / math.sqrt(D)
        x = jax.random.normal(ks[0], (B, L, D), dtype=jnp.float32)
        qkv_w = jax.random.normal(ks[1], (3 * D, D), dtype=jnp.float32) * std
        qkv_b = jnp.zeros((3 * D,), dtype=jnp.float32)
        out_w = jax.random.normal(ks[2], (D, D), dtype=jnp.float32) * std
        out_b = jnp.zeros((D,), dtype=jnp.float32)
        decay_w = jax.random.normal(ks[3], (H, D), dtype=jnp.float32) * 0.02
        decay_b = jnp.full((H,), 4.0, dtype=jnp.float32)
        norm_scale = jnp.ones((D,), dtype=jnp.float32)
        return {'x': x, 'qkv_w': qkv_w, 'qkv_b': qkv_b, 'out_w': out_w, 'out_b': out_b, 'decay_w': decay_w, 'decay_b': decay_b, 'norm_scale': norm_scale}
    _L0_attn_all = _L0_attn_setup()
    _L0_attn_in = {k: v for k, v in _L0_attn_all.items() if k in ('qkv_w', 'qkv_b', 'out_w', 'out_b', 'decay_w', 'decay_b', 'norm_scale')}
    del _L0_attn_all

    def _L0_ffn_setup():
        import jax, jax.numpy as jnp
        import numpy as np
        B, T, C = (8, 256, 128)
        H = 256
        G, EG = (2, 4)
        E = G * EG
        K = 2
        LN_EPS = 1e-05

        def _swiglu(x):
            a, b = jnp.split(x, 2, axis=-1)
            return jax.nn.silu(a) * b
        key = jax.random.key(seed)
        ks = jax.random.split(key, 8)
        n = lambda k, shape, s: jax.random.normal(k, shape, dtype=jnp.float32) * s
        return {'x': n(ks[0], (B, T, C), 1.0), 'ln_scale': jnp.ones((C,), jnp.float32), 'ln_bias': jnp.zeros((C,), jnp.float32), 'shared_in_w': n(ks[1], (2 * H, C), 0.02), 'shared_out_w': n(ks[2], (C, H), 0.02), 'shared_out_b': jnp.zeros((C,), jnp.float32), 'expert_in_w': n(ks[3], (2 * H, C), 0.02), 'expert_out_weight': n(ks[4], (E, C, H), 0.02), 'expert_out_bias': jnp.zeros((E, C), jnp.float32), 'group_gate_w': n(ks[5], (G, C), 0.02), 'expert_gate_w': n(ks[6], (E, C), 0.02), 'group_bias': jnp.zeros((G,), jnp.float32), 'expert_bias': jnp.zeros((E,), jnp.float32)}
    _L0_ffn_all = _L0_ffn_setup()
    _L0_ffn_in = {k: v for k, v in _L0_ffn_all.items() if k in ('ln_scale', 'ln_bias', 'shared_in_w', 'shared_out_w', 'shared_out_b', 'expert_in_w', 'expert_out_weight', 'expert_out_bias', 'group_gate_w', 'expert_gate_w', 'group_bias', 'expert_bias')}
    del _L0_ffn_all
    return {'x': x, 'L0_tok_w_compress': _L0_tok_in['w_compress'], 'L0_tok_b_compress': _L0_tok_in['b_compress'], 'L0_tok_w_main': _L0_tok_in['w_main'], 'L0_tok_b_main': _L0_tok_in['b_main'], 'L0_tok_w_expand': _L0_tok_in['w_expand'], 'L0_tok_b_expand': _L0_tok_in['b_expand'], 'L0_tok_g_conv_norm': _L0_tok_in['g_conv_norm'], 'L0_tok_b_conv_norm': _L0_tok_in['b_conv_norm'], 'L0_tok_w_ff1': _L0_tok_in['w_ff1'], 'L0_tok_b_ff1': _L0_tok_in['b_ff1'], 'L0_tok_w_ff2': _L0_tok_in['w_ff2'], 'L0_tok_b_ff2': _L0_tok_in['b_ff2'], 'L0_tok_g_ff_norm': _L0_tok_in['g_ff_norm'], 'L0_tok_b_ff_norm': _L0_tok_in['b_ff_norm'], 'L0_attn_qkv_w': _L0_attn_in['qkv_w'], 'L0_attn_qkv_b': _L0_attn_in['qkv_b'], 'L0_attn_out_w': _L0_attn_in['out_w'], 'L0_attn_out_b': _L0_attn_in['out_b'], 'L0_attn_decay_w': _L0_attn_in['decay_w'], 'L0_attn_decay_b': _L0_attn_in['decay_b'], 'L0_attn_norm_scale': _L0_attn_in['norm_scale'], 'L0_ffn_ln_scale': _L0_ffn_in['ln_scale'], 'L0_ffn_ln_bias': _L0_ffn_in['ln_bias'], 'L0_ffn_shared_in_w': _L0_ffn_in['shared_in_w'], 'L0_ffn_shared_out_w': _L0_ffn_in['shared_out_w'], 'L0_ffn_shared_out_b': _L0_ffn_in['shared_out_b'], 'L0_ffn_expert_in_w': _L0_ffn_in['expert_in_w'], 'L0_ffn_expert_out_weight': _L0_ffn_in['expert_out_weight'], 'L0_ffn_expert_out_bias': _L0_ffn_in['expert_out_bias'], 'L0_ffn_group_gate_w': _L0_ffn_in['group_gate_w'], 'L0_ffn_expert_gate_w': _L0_ffn_in['expert_gate_w'], 'L0_ffn_group_bias': _L0_ffn_in['group_bias'], 'L0_ffn_expert_bias': _L0_ffn_in['expert_bias']}

def reference(x, L0_tok_w_compress, L0_tok_b_compress, L0_tok_w_main, L0_tok_b_main, L0_tok_w_expand, L0_tok_b_expand, L0_tok_g_conv_norm, L0_tok_b_conv_norm, L0_tok_w_ff1, L0_tok_b_ff1, L0_tok_w_ff2, L0_tok_b_ff2, L0_tok_g_ff_norm, L0_tok_b_ff_norm, L0_attn_qkv_w, L0_attn_qkv_b, L0_attn_out_w, L0_attn_out_b, L0_attn_decay_w, L0_attn_decay_b, L0_attn_norm_scale, L0_ffn_ln_scale, L0_ffn_ln_bias, L0_ffn_shared_in_w, L0_ffn_shared_out_w, L0_ffn_shared_out_b, L0_ffn_expert_in_w, L0_ffn_expert_out_weight, L0_ffn_expert_out_bias, L0_ffn_group_gate_w, L0_ffn_expert_gate_w, L0_ffn_group_bias, L0_ffn_expert_bias):
    import jax
    import jax.numpy as jnp

    def _L0_tok_ref(x, w_compress, b_compress, w_main, b_main, w_expand, b_expand, g_conv_norm, b_conv_norm, w_ff1, b_ff1, w_ff2, b_ff2, g_ff_norm, b_ff_norm):
        import jax, jax.numpy as jnp
        import numpy as np
        EPS = 1e-05

        def conv1d(x, w, b, stride=1, padding=0):
            out = jax.lax.conv_general_dilated(x, w, window_strides=(stride,), padding=[(padding, padding)], dimension_numbers=('NCH', 'OIH', 'NCH'))
            return out + b[None, :, None]

        def layer_norm(x, g, b):
            mu = jnp.mean(x, axis=-1, keepdims=True)
            var = jnp.mean(jnp.square(x - mu), axis=-1, keepdims=True)
            return (x - mu) * jax.lax.rsqrt(var + EPS) * g + b
        xt = jnp.transpose(x, (0, 2, 1))
        identity = xt
        h = jax.nn.silu(conv1d(xt, w_compress, b_compress))
        h = jax.nn.silu(conv1d(h, w_main, b_main, stride=1, padding=1))
        h = conv1d(h, w_expand, b_expand)
        h = jnp.transpose(h, (0, 2, 1))
        identity = jnp.transpose(identity, (0, 2, 1))
        y = layer_norm(h + identity, g_conv_norm, b_conv_norm)
        ff = jnp.einsum('bth,oh->bto', y, w_ff1) + b_ff1
        ff = jax.nn.gelu(ff, approximate=False)
        ff = jnp.einsum('bto,ho->bth', ff, w_ff2) + b_ff2
        y = layer_norm(ff + y, g_ff_norm, b_ff_norm)
        yt = jnp.transpose(y, (0, 2, 1))
        pooled = jax.lax.reduce_window(yt, -jnp.inf, jax.lax.max, (1, 1, 3), (1, 1, 1), 'VALID')
        return jnp.transpose(pooled, (0, 2, 1))

    def _L0_attn_ref(x, qkv_w, qkv_b, out_w, out_b, decay_w, decay_b, norm_scale):
        import jax, jax.numpy as jnp
        import numpy as np
        import math
        D_MODEL = 128
        NUM_HEADS = 8
        B, L = (2, 1024)
        EPS_NORM = 1e-08
        PLASTICITY = 1.0

        def _hebbian_forward(x, qkv_w, qkv_b, out_w, out_b, decay_w, decay_b, norm_scale):
            Bsz, Lsz, D = x.shape
            H = NUM_HEADS
            E = D // H
            qkv = x @ qkv_w.T + qkv_b
            q, k, v = jnp.split(qkv, 3, axis=-1)
            q = q.reshape(Bsz, Lsz, H, E)
            k = k.reshape(Bsz, Lsz, H, E)
            v = v.reshape(Bsz, Lsz, H, E)
            q = (jax.nn.elu(q) + 1.0) / math.sqrt(E)
            k = jax.nn.elu(k) + 1.0
            decay_logits = x @ decay_w.T + decay_b
            lambdas = (0.9 + 0.1 * jax.nn.sigmoid(decay_logits)) * PLASTICITY
            log_lambdas = jnp.log(jnp.clip(lambdas, 1e-06))[..., None]
            log_lambda_cum = jnp.clip(jnp.cumsum(log_lambdas, axis=1), -50.0, 50.0)
            decay_k = jnp.exp(-log_lambda_cum)
            decay_q = jnp.exp(log_lambda_cum)
            k_decayed = k * decay_k
            q_decayed = q * decay_q
            kv = jnp.einsum('blhe,blhf->blhef', k_decayed, v)
            memory_state = jnp.cumsum(kv, axis=1)
            k_sum_decayed = jnp.cumsum(k_decayed, axis=1)
            num = jnp.einsum('blhe,blhef->blhf', q_decayed, memory_state)
            den = jnp.einsum('blhe,blhe->blh', q_decayed, k_sum_decayed)[..., None] + 1e-06
            out = (num / den).reshape(Bsz, Lsz, D)
            out = out @ out_w.T + out_b
            rnorm = jax.lax.rsqrt(jnp.mean(out * out, axis=-1, keepdims=True) + EPS_NORM)
            return out * rnorm * norm_scale
        return _hebbian_forward(x, qkv_w, qkv_b, out_w, out_b, decay_w, decay_b, norm_scale)

    def _L0_ffn_ref(x, ln_scale, ln_bias, shared_in_w, shared_out_w, shared_out_b, expert_in_w, expert_out_weight, expert_out_bias, group_gate_w, expert_gate_w, group_bias, expert_bias):
        import jax, jax.numpy as jnp
        import numpy as np
        B, T, C = (8, 256, 128)
        H = 256
        G, EG = (2, 4)
        E = G * EG
        K = 2
        LN_EPS = 1e-05

        def _swiglu(x):
            a, b = jnp.split(x, 2, axis=-1)
            return jax.nn.silu(a) * b
        Bx, Tx, Cx = x.shape
        S = Bx * Tx
        flat = x.reshape(S, Cx)
        mu = flat.mean(-1, keepdims=True)
        var = ((flat - mu) ** 2).mean(-1, keepdims=True)
        flat = (flat - mu) * jax.lax.rsqrt(var + LN_EPS) * ln_scale + ln_bias
        h_shared = _swiglu(flat @ shared_in_w.T)
        out_shared = h_shared @ shared_out_w.T + shared_out_b
        g_logits = flat @ group_gate_w.T + group_bias
        g_idx = jnp.argmax(g_logits, axis=-1)
        e_logits = (flat @ expert_gate_w.T).reshape(S, G, EG)
        e_sel = jnp.take_along_axis(e_logits, g_idx[:, None, None], axis=1)[:, 0, :]
        e_sel = e_sel + expert_bias.reshape(G, EG)[g_idx]
        e_probs = jax.nn.softmax(e_sel, axis=-1)
        topv, topi = jax.lax.top_k(e_probs, K)
        topv = topv / (topv.sum(-1, keepdims=True) + 1e-08)
        disp = g_idx[:, None] * EG + topi
        h_expert = _swiglu(flat @ expert_in_w.T)
        rows = jnp.arange(S)[:, None]
        comb = jnp.zeros((S, E), flat.dtype).at[rows, disp].add(topv)
        cnt = jnp.zeros((S, E), flat.dtype).at[rows, disp].add(1.0)
        routed = cnt @ expert_out_bias
        for e in range(E):
            routed = routed + comb[:, e:e + 1] * (h_expert @ expert_out_weight[e].T)
        return (out_shared + routed).reshape(Bx, Tx, Cx)
    h = _L0_tok_ref(x, L0_tok_w_compress, L0_tok_b_compress, L0_tok_w_main, L0_tok_b_main, L0_tok_w_expand, L0_tok_b_expand, L0_tok_g_conv_norm, L0_tok_b_conv_norm, L0_tok_w_ff1, L0_tok_b_ff1, L0_tok_w_ff2, L0_tok_b_ff2, L0_tok_g_ff_norm, L0_tok_b_ff_norm)
    h = h + _L0_attn_ref(_layernorm(h, axis=-1), L0_attn_qkv_w, L0_attn_qkv_b, L0_attn_out_w, L0_attn_out_b, L0_attn_decay_w, L0_attn_decay_b, L0_attn_norm_scale)
    h = h + _L0_ffn_ref(_layernorm(h, axis=-1), L0_ffn_ln_scale, L0_ffn_ln_bias, L0_ffn_shared_in_w, L0_ffn_shared_out_w, L0_ffn_shared_out_b, L0_ffn_expert_in_w, L0_ffn_expert_out_weight, L0_ffn_expert_out_bias, L0_ffn_group_gate_w, L0_ffn_expert_gate_w, L0_ffn_group_bias, L0_ffn_expert_bias)
    return h

_drawn_inputs = setup_inputs


def setup_inputs(seed=0):
    import zlib

    import numpy as np

    out = dict(_drawn_inputs(seed))
    spreads = {'L0_tok_b_compress': (0.0, 0.8),
     'L0_tok_b_main': (0.0, 0.304),
     'L0_tok_b_expand': (0.0, 0.1),
     'L0_tok_g_conv_norm': (1.0, 0.2),
     'L0_tok_b_conv_norm': (0.0, 0.1),
     'L0_tok_b_ff1': (0.0, 0.367),
     'L0_tok_b_ff2': (0.0, 0.1),
     'L0_tok_g_ff_norm': (1.0, 0.2),
     'L0_tok_b_ff_norm': (0.0, 0.1),
     'L0_attn_qkv_b': (0.0, 0.1),
     'L0_attn_out_b': (0.0, 0.1),
     'L0_attn_decay_b': (4.0, 0.2),
     'L0_attn_norm_scale': (1.0, 0.2),
     'L0_ffn_ln_scale': (1.0, 0.2),
     'L0_ffn_ln_bias': (0.0, 0.1),
     'L0_ffn_shared_out_b': (0.0, 0.637),
     'L0_ffn_expert_out_bias': (0.0, 0.402),
     'L0_ffn_group_bias': (0.0, 0.1),
     'L0_ffn_expert_bias': (0.0, 0.1)}
    factors = {'L0_tok_w_compress': 8.0,
     'L0_tok_w_main': 8.0,
     'L0_tok_w_ff1': 2.934,
     'L0_attn_decay_w': 6.251,
     'L0_ffn_shared_in_w': 8.0,
     'L0_ffn_shared_out_w': 8.0,
     'L0_ffn_expert_in_w': 8.0,
     'L0_ffn_expert_out_weight': 8.0}
    for name, (base, spread) in spreads.items():
        noise = np.random.default_rng([zlib.crc32(name.encode()), seed]).standard_normal(out[name].shape)
        drawn = base * np.exp(spread * noise) if base else spread * noise
        out[name] = jnp.asarray(drawn.astype(out[name].dtype))
    for name, factor in factors.items():
        out[name] = (out[name] * factor).astype(out[name].dtype)
    return out
```

```python
from contextlib import ExitStack

import concourse.bass as bass
from concourse import mybir

F32 = mybir.dt.float32
ALU = mybir.AluOpType
ACT = mybir.ActivationFunctionType
AX = mybir.AxisListType

NSEQ, SEQ, D = 8, 750, 128
POOL = 3
OUT_LEN = SEQ - POOL + 1
PAIRS = NSEQ // 2
TOK = 125
NT = SEQ // TOK
NCH = 2
TPC = NT // NCH
CH = TPC * TOK
LAST = OUT_LEN - (NT - 1) * TOK
HALF = D // 2
HEADS, HD = 8, 16
HE = HD + 1
NV = HEADS * HE
HID = 256
EXP = 8
GROUPS, EG = 2, 4
NG = GROUPS + EXP
BANKS, BANK = 8, 512
EPS = 1e-5

WCOLS = {}


def _layout():
    at = 0
    for name, width in [
        ("ident", D), ("compress", HALF), ("conv", 3 * D), ("expand", D), ("ff1", HALF), ("ff2", D), ("vecs", 16),
        ("q", D), ("k", D), ("v", D + HEADS), ("out", D), ("tri", TOK), ("ones", TOK), ("blocks", NV), ("parity", 2),
        ("row_v", D + HEADS), ("row_out", D), ("row_scale", D), ("row_gate", NG), ("before", 16), ("after", 16),
        ("halfneg", NT), ("eps", NT), ("eps_rms", NT), ("scale_two", NT), ("eps_two", NT), ("shared_in", 2 * HID), ("expert_in", 2 * HID), ("shared_out", 2 * D),
        ("expert_out", 2 * EXP * D), ("gate", NG), ("bias_rows", D),
    ]:
        WCOLS[name] = (at, at + width)
        at += width
    return at


NW = _layout()
W_FIRST = WCOLS["q"][0]
VECS = ["compress", "main", "expand", "conv_g", "conv_b", "ff1", "ff2", "ff_g", "ff_b", "q", "k", "ln_g", "ln_b"]

PER_PAIR = dict(
    small=12, scaled=2, ms_ready=2, h1_ready=2, h2_ready=2, r1_ready=4, y_ready=4, g_ready=2, r2_ready=4, z_ready=4, pooled=4,
    n3_ready=4, in_exp=8, in_relu=8, q_ready=4, k_ready=4, q_split=4, v_ready=4, ktm_ready=4, lam_exp=2, lam_ready=2,
    log_ready=2, cum_clipped=2, dk_ready=2, vd_ready=2, masked=24, den_ready=4, at_ready=4,
    atc_ready=4, o_ready=4, sq_ready=2, rms_ready=2, o2_ready=2, r3_ready=4, f_ready=4, gl_ready=2,
    route_exp=1, route=19, cnt_ready=1, cnt_t=4, silu_ready=16, h_ready=16, acc=108, tile_out=12, state_copied=10,
    stats=16, var_ready=8, rstd_ready=8, norm=16, eps_added=8,
    pe_compress=2, pe_conv=2, pe_expand=4, pe_t=16, pe_back=16, pe_ff1=2, pe_ff2=4, pe_q=4, pe_k=4, pe_v=4, pe_tk=4,
    pe_cum=2, pe_s=24, pe_num=12, pe_state=10, pe_tat=4, pe_o=4, pe_gate=2, pe_cnt=2, pe_in=16, pe_out=12,
)


def build(nc, wpack, x, out):
    with ExitStack() as ctx:
        def sb(name, shape):
            return ctx.enter_context(nc.sbuf_tensor(name, shape, F32))

        W = sb("weights", [D, NW])

        def w(name, a=0, b=None, p=D):
            lo, hi = WCOLS[name]
            return W[0:p, lo + a:(hi if b is None else lo + b)]

        def vec(name, p0=0, p1=D):
            c = WCOLS["vecs"][0] + VECS.index(name)
            return W[p0:p1, c:c + 1]

        xs = [sb(f"x{s}", [D, SEQ]) for s in range(2)]
        h1 = sb("conv1", [D, SEQ + 2])
        h2 = sb("conv2", [D, SEQ])
        g = sb("g", [D, SEQ])
        r = [sb(f"r{s}", [D, SEQ]) for s in range(2)]
        ntm = [sb(f"ntm{s}", [D, NT, D]) for s in range(2)]
        y = [sb(f"y{s}", [D, SEQ]) for s in range(2)]
        z = [sb(f"z{s}", [D, SEQ]) for s in range(2)]
        m2 = h2
        h = [sb(f"h{s}", [D, SEQ]) for s in range(2)]
        st = [sb(f"st{s}", [D, NT, 6]) for s in range(2)]
        mv = [sb(f"mv{s}", [D, NT, 2]) for s in range(2)]
        ve = [sb(f"ve{s}", [D, NT]) for s in range(2)]
        rstd = [sb(f"rstd{s}", [D, NT]) for s in range(2)]
        e_in = [sb(f"e_in{i}", [D, CH]) for i in range(4)]
        r_in = [sb(f"r_in{i}", [D, CH]) for i in range(4)]
        q = r
        k = [sb(f"k{s}", [D, SEQ]) for s in range(2)]
        q2 = [sb(f"q2{s}", [D, 2, SEQ]) for s in range(2)]
        ktm = [sb(f"ktm{s}", [D, NT, D]) for s in range(2)]
        v = [sb(f"v{s}", [D, NT, D + HEADS]) for s in range(2)]
        lam = [sb(f"lam{s}", [D, NT, HEADS]) for s in range(2)]
        lam2 = [sb(f"lam2{s}", [D, NT, HEADS]) for s in range(2)]
        logl = [sb(f"logl{s}", [D, NT, HEADS]) for s in range(2)]
        cum = [sb(f"cum{s}", [D, NT, HEADS]) for s in range(2)]
        dk = [sb(f"dk{s}", [D, NT, HEADS]) for s in range(2)]
        dk4 = [sb(f"dk4{s}", [D, NT, HEADS]) for s in range(2)]
        vd = [sb(f"vd{s}", [D, NT, HEADS, HE]) for s in range(2)]
        sm = [sb(f"sm{s}", [D, 4, 2, TOK]) for s in range(2)]
        state = [sb(f"state{s}", [D, NV]) for s in range(2)]
        den = [sb(f"den{s}", [D, TPC, HEADS]) for s in range(2)]
        rden = [sb(f"rden{s}", [D, TPC, HEADS]) for s in range(2)]
        at = [sb(f"at{s}", [D, NT, HEADS, HD]) for s in range(2)]
        atc = k
        o = [sb(f"o{s}", [D, NT, D]) for s in range(2)]
        ss = [sb(f"ss{s}", [D, NT]) for s in range(2)]
        ms = [sb(f"ms{s}", [D, NT]) for s in range(2)]
        rrms = [sb(f"rrms{s}", [D, NT]) for s in range(2)]
        o2 = [sb(f"o2{s}", [D, NT, D]) for s in range(2)]
        r3 = [sb(f"r3{s}", [D, NT, D]) for s in range(2)]
        gl = sb("gl", [D, 2 * NT, NG])
        gind = sb("gind", [D, 2 * NT, GROUPS])
        rt = [sb(f"rt{i}", [D, 2 * NT, GROUPS, EG]) for i in range(7)]
        rr = [sb(f"rr{i}", [D, 2 * NT * GROUPS]) for i in range(5)]
        pair4 = [sb(f"pair4{i}", [D, 2 * NT * GROUPS, EG, EG]) for i in range(2)]
        cmp8 = sb("cmp8", [D, 2 * NT * GROUPS, EG, 2 * EG])
        comb = sb("comb", [D, 2 * NT, GROUPS, EG])
        cnt9 = sb("cnt9", [D, 2 * NT, EXP + 1])
        cnt_t = sb("cnt_t", [EXP + 1, 2, SEQ])
        sil = [sb(f"sil{i}", [D, CH]) for i in range(2)]
        H = [[[sb(f"H{s}{gg}{hh}", [D, SEQ]) for hh in range(2)] for gg in range(2)] for s in range(2)]
        acc = [[sb(f"acc{i}{j}", [D, D]) for j in range(2)] for i in range(2)]
        res = [sb(f"res{s}", [D, NT, D]) for s in range(2)]
        scratch = sb("scratch", [1, 10])
        PS = ctx.enter_context(nc.psum_tensor("PS", [D, BANKS, BANK], F32))

        S = {n: ctx.enter_context(nc.semaphore(n)) for n in PER_PAIR}
        N = PER_PAIR
        w_first = ctx.enter_context(nc.semaphore("w_first"))
        w_rest = ctx.enter_context(nc.semaphore("w_rest"))
        x_in = ctx.enter_context(nc.semaphore("x_in"))
        stored = ctx.enter_context(nc.semaphore("stored"))
        cleared = ctx.enter_context(nc.semaphore("cleared"))

        def sc(s, c):
            return 2 * s + c

        def tiles_of(c):
            return range(c * TPC, (c + 1) * TPC)

        def cols(c):
            return slice(c * CH, (c + 1) * CH)

        def tile(i):
            return slice(i * TOK, (i + 1) * TOK)

        def tm_bank(b, width=D, p=TOK):
            return PS[0:p, b, 0:TPC * width].rearrange("p (t n) -> p t n", t=TPC)

        block = ctx.enter_context(nc.Block())

        @block.sync
        def _(sp):
            sp.dma_start(W[:, 0:W_FIRST], wpack[:, 0:W_FIRST]).then_inc(w_first, 16)

            def load(pair):
                for s in range(2):
                    sp.dma_start(xs[s][:, :], x[:, bass.ds((2 * pair + s) * SEQ, SEQ)]).then_inc(x_in, 16)

            def store(pair):
                for s in range(2):
                    sp.wait_ge(S["tile_out"], pair * N["tile_out"] + NT * (s + 1) + 1)
                    dst = out[bass.ds(2 * pair + s, 1), :, :].rearrange("o l d -> (o l) d")
                    full = (NT - 1) * TOK
                    sp.dma_start(dst[0:full, :].rearrange("(t p) d -> p t d", p=TOK),
                                 res[s][0:TOK, 0:NT - 1, :]).then_inc(stored, 16)
                    sp.dma_start(dst[full:OUT_LEN, :], res[s][0:LAST, NT - 1, :]).then_inc(stored, 16)

            load(0)
            with sp.Fori(0, PAIRS - 1) as it:
                sp.wait_ge(S["r1_ready"], it * N["r1_ready"] + 4)
                load(it + 1)
                store(it)
            store(PAIRS - 1)
            sp.wait_ge(stored, PAIRS * 4 * 16 + 16)

        @block.gpsimd
        def _(pool):
            pool.dma_start(W[:, W_FIRST:NW], wpack[:, W_FIRST:NW]).then_inc(w_rest, 16)
            nc.gpsimd.memset(h1[:, 0:1], 0.0).then_inc(cleared, 1)
            nc.gpsimd.memset(h1[:, SEQ + 1:SEQ + 2], 0.0).then_inc(cleared, 1)
            for s in range(2):
                nc.gpsimd.memset(h[s][:, OUT_LEN:SEQ], 0.0).then_inc(cleared, 1)
            nc.gpsimd.memset(cnt9[0:TOK, :, EXP:EXP + 1], 1.0).then_inc(cleared, 1)
            nc.gpsimd.memset(scratch[0:1, 8:9], 0.0).then_inc(S["tile_out"], 1)
            nc.gpsimd.memset(scratch[0:1, 9:10], 0.0).then_inc(stored, 16)
            pool.wait_ge(w_rest, 16)

            with pool.Fori(0, PAIRS) as it:
                def power(norm, s):
                    pool.wait_ge(S["var_ready"], it * N["var_ready"] + 2 * norm + s + 1)
                    var, eps = mv[s][0:TOK, :, 1], "eps"
                    if norm == 3:
                        nc.gpsimd.tensor_tensor(ms[s][0:TOK, :], var, w("scale_two", p=TOK), ALU.mult).then_inc(S["scaled"], 1)
                        pool.wait_ge(S["scaled"], it * N["scaled"] + s + 1)
                        var, eps = ms[s][0:TOK, :], "eps_two"
                    nc.gpsimd.tensor_tensor(ve[s][0:TOK, :], var, w(eps, p=TOK), ALU.add).then_inc(S["eps_added"], 1)
                    pool.wait_ge(S["eps_added"], it * N["eps_added"] + 2 * norm + s + 1)
                    nc.gpsimd.tensor_tensor(rstd[s][0:TOK, :], ve[s][0:TOK, :], w("halfneg", p=TOK), ALU.pow).then_inc(S["rstd_ready"], 1)

                for norm in range(3):
                    for s in range(2):
                        power(norm, s)
                for s in range(2):
                    for c in range(NCH):
                        pool.wait_ge(S["q_ready"], it * N["q_ready"] + sc(s, c) + 1)
                        for par in range(2):
                            last = nc.gpsimd.tensor_tensor(q2[s][:, par, cols(c)], q[s][:, cols(c)],
                                                           w("parity", par, par + 1).broadcast_to([D, CH]), ALU.mult)
                        last.then_inc(S["q_split"], 1)
                for s in range(2):
                    pool.wait_ge(S["sq_ready"], it * N["sq_ready"] + s + 1)
                    nc.gpsimd.tensor_tensor(ms[s][0:TOK, :], ss[s][0:TOK, :], w("eps_rms", p=TOK), ALU.add).then_inc(S["ms_ready"], 1)
                    pool.wait_ge(S["ms_ready"], it * N["ms_ready"] + s + 1)
                    nc.gpsimd.tensor_tensor(rrms[s][0:TOK, :], ms[s][0:TOK, :], w("halfneg", p=TOK), ALU.pow).then_inc(S["rms_ready"], 1)
                for s in range(2):
                    power(3, s)

        @block.tensor
        def _(pe):
            mm = nc.tensor.matmul

            def transpose_in(it, src, s, c, n):
                for j, i in enumerate(tiles_of(c)):
                    last = nc.tensor.transpose(PS[0:TOK, sc(s, c), j * D:(j + 1) * D], src[s][:, tile(i)], w("ident"))
                last.then_inc(S["pe_t"], 1)

            def transpose_back(it, src, s, c):
                for j, i in enumerate(tiles_of(c)):
                    last = nc.tensor.transpose(PS[:, 4 + sc(s, c), tile(j)], src[s][0:TOK, i, :],
                                               w("ident", 0, TOK, TOK))
                return last

            pe.wait_ge(w_first, 16)
            with pe.Fori(0, PAIRS) as it:
                pe.wait_ge(S["tile_out"], it * N["tile_out"] + 1)
                pe.wait_ge(x_in, it * 32 + 32)
                for c in range(NCH):
                    for s in range(2):
                        last = mm(PS[HALF * s:HALF * (s + 1), c, 0:CH], w("compress"), xs[s][:, cols(c)],
                                  start=True, stop=True)
                    last.then_inc(S["pe_compress"], 1)
                pe.wait_ge(S["h1_ready"], it * N["h1_ready"] + 2)
                for c in range(NCH):
                    for tap in range(3):
                        last = mm(PS[:, 2 + c, 0:CH], w("conv", tap * D, (tap + 1) * D),
                                  h1[:, c * CH + tap:c * CH + tap + CH], start=tap == 0, stop=tap == 2)
                    last.then_inc(S["pe_conv"], 1)
                pe.wait_ge(S["h2_ready"], it * N["h2_ready"] + 2)
                for s in range(2):
                    for c in range(NCH):
                        rows = slice(HALF * s, HALF * (s + 1))
                        lo, hi = WCOLS["expand"]
                        mm(PS[:, 4 + sc(s, c), 0:CH], W[rows, lo:hi], h2[rows, cols(c)], start=True, stop=True).then_inc(S["pe_expand"], 1)
                for s in range(2):
                    for c in range(NCH):
                        pe.wait_ge(S["r1_ready"], it * N["r1_ready"] + sc(s, c) + 1)
                        transpose_in(it, r, s, c, 0)
                for s in range(2):
                    for c in range(NCH):
                        pe.wait_ge(S["norm"], it * N["norm"] + sc(s, c) + 1)
                        transpose_back(it, ntm, s, c).then_inc(S["pe_back"], 1)
                pe.wait_ge(S["y_ready"], it * N["y_ready"] + 4)
                for c in range(NCH):
                    for s in range(2):
                        last = mm(PS[HALF * s:HALF * (s + 1), c, 0:CH], w("ff1"), y[s][:, cols(c)],
                                  start=True, stop=True)
                    last.then_inc(S["pe_ff1"], 1)
                pe.wait_ge(S["g_ready"], it * N["g_ready"] + 2)
                for s in range(2):
                    for c in range(NCH):
                        rows = slice(HALF * s, HALF * (s + 1))
                        lo, hi = WCOLS["ff2"]
                        mm(PS[:, 4 + sc(s, c), 0:CH], W[rows, lo:hi], g[rows, cols(c)], start=True, stop=True).then_inc(S["pe_ff2"], 1)
                for s in range(2):
                    for c in range(NCH):
                        pe.wait_ge(S["r2_ready"], it * N["r2_ready"] + sc(s, c) + 1)
                        transpose_in(it, r, s, c, 1)
                for s in range(2):
                    for c in range(NCH):
                        pe.wait_ge(S["norm"], it * N["norm"] + 4 + sc(s, c) + 1)
                        transpose_back(it, ntm, s, c).then_inc(S["pe_back"], 1)
                for s in range(2):
                    pe.wait_ge(S["pooled"], it * N["pooled"] + 2 * s + 2)
                    for c in range(NCH):
                        transpose_in(it, h, s, c, 2)
                for s in range(2):
                    for c in range(NCH):
                        pe.wait_ge(S["norm"], it * N["norm"] + 8 + sc(s, c) + 1)
                        transpose_back(it, ntm, s, c).then_inc(S["pe_back"], 1)
                pe.wait_ge(w_rest, 16)
                for s in range(2):
                    for c in range(NCH):
                        pe.wait_ge(S["n3_ready"], it * N["n3_ready"] + sc(s, c) + 1)
                        mm(PS[:, sc(s, c), 0:CH], w("q"), y[s][:, cols(c)], start=True, stop=True).then_inc(S["pe_q"], 1)
                for s in range(2):
                    for c in range(NCH):
                        pe.wait_ge(S["n3_ready"], it * N["n3_ready"] + 4)
                        mm(PS[:, 4 + sc(s, c), 0:CH], w("k"), y[s][:, cols(c)], start=True, stop=True).then_inc(S["pe_k"], 1)
                for s in range(2):
                    for c in range(NCH):
                        pe.wait_ge(S["in_relu"], it * N["in_relu"] + sc(s, c) + 1)
                        for j, i in enumerate(tiles_of(c)):
                            last = mm(PS[0:TOK, sc(s, c), j * (D + HEADS):(j + 1) * (D + HEADS)], y[s][:, tile(i)],
                                      w("v"), start=True, stop=True)
                        last.then_inc(S["pe_v"], 1)
                for s in range(2):
                    for c in range(NCH):
                        pe.wait_ge(S["k_ready"], it * N["k_ready"] + sc(s, c) + 1)
                        for j, i in enumerate(tiles_of(c)):
                            last = nc.tensor.transpose(PS[0:TOK, 4 + sc(s, c), j * D:(j + 1) * D], k[s][:, tile(i)],
                                                       w("ident"))
                        last.then_inc(S["pe_tk"], 1)
                for s in range(2):
                    pe.wait_ge(S["log_ready"], it * N["log_ready"] + s + 1)
                    if s == 0:
                        pe.wait_ge(S["v_ready"], it * N["v_ready"] + 4)
                    dst = PS[0:TOK, s, 0:NT * HEADS].rearrange("p (t n) -> p t n", t=NT)
                    mm(dst, w("tri", p=TOK), logl[s][0:TOK, :, :], start=True, stop=False)
                    for back in range(1, NT):
                        last = mm(dst[:, back:NT, :], w("ones", p=TOK), logl[s][0:TOK, 0:NT - back, :],
                                  start=False, stop=back == NT - 1)
                    last.then_inc(S["pe_cum"], 1)

                def scores(i, s):
                    for half in range(2):
                        u = 4 * i + 2 * s + half
                        if u < 2:
                            pe.wait_ge(S["q_split"], it * N["q_split"] + 4)
                            pe.wait_ge(S["ktm_ready"], it * N["ktm_ready"] + 4)
                            pe.wait_ge(S["cum_clipped"], it * N["cum_clipped"] + 2)
                        else:
                            pe.wait_ge(S["masked"], it * N["masked"] + u - 1)
                        for b in (2 * half, 2 * half + 1):
                            rows = slice(32 * b, 32 * b + 32)
                            last = mm(PS[0:TOK, b, 0:2 * TOK].rearrange("p (a n) -> p a n", a=2), k[s][rows, tile(i)],
                                      q2[s][rows, :, tile(i)], start=True, stop=True, tile_position=(32 * b, 0))
                        last.then_inc(S["pe_s"], 1)

                def attend(i, s):
                    t = 2 * i + s
                    j = i % TPC
                    if i == 0:
                        pe.wait_ge(S["vd_ready"], it * N["vd_ready"] + s + 1)
                    if i == TPC:
                        pe.wait_ge(S["at_ready"], it * N["at_ready"] + s + 1)
                    base = j * NV
                    if i > 0:
                        pe.wait_ge(S["state_copied"], it * N["state_copied"] + 2 * (i - 1) + s + 1)
                        mm(PS[0:TOK, 4 + s, base:base + NV], q[s][:, tile(i)], state[s][:, :],
                           start=True, stop=False, skip_group_check=True)
                    pe.wait_ge(S["masked"], it * N["masked"] + 4 * i + 2 * s + 2)
                    for hd in range(HEADS):
                        last = mm(PS[0:TOK, 4 + s, base + hd * HE:base + (hd + 1) * HE],
                                  sm[s][0:TOK, hd // 2, hd % 2, :], vd[s][0:TOK, i, hd, :],
                                  start=(i == 0 and hd == 0), stop=hd == HEADS - 1, skip_group_check=True)
                    last.then_inc(S["pe_num"], 1)
                    if i < NT - 1:
                        mm(PS[:, 6 + s, 0:NV], ktm[s][0:TOK, i, :],
                               vd[s][0:TOK, i, :, :].rearrange("p a b -> p (a b)"),
                               start=i == 0, stop=True, skip_group_check=True).then_inc(S["pe_state"], 1)

                steps = [(i, s) for i in range(NT) for s in range(2)]
                for n, (i, s) in enumerate(steps):
                    scores(i, s)
                    if n:
                        attend(*steps[n - 1])
                attend(*steps[-1])
                pe.wait_ge(S["masked"], it * N["masked"] + 24)
                for s in range(2):
                    for c in range(NCH):
                        pe.wait_ge(S["at_ready"], it * N["at_ready"] + 2 * c + s + 1)
                        for j, i in enumerate(tiles_of(c)):
                            last = nc.tensor.transpose(PS[:, sc(s, c), tile(j)],
                                                       at[s][0:TOK, i, :, :].rearrange("p a b -> p (a b)"),
                                                       w("ident", 0, TOK, TOK))
                        last.then_inc(S["pe_tat"], 1)
                pe.wait_ge(S["state_copied"], it * N["state_copied"] + 10)
                for s in range(2):
                    for c in range(NCH):
                        pe.wait_ge(S["atc_ready"], it * N["atc_ready"] + sc(s, c) + 1)
                        for j, i in enumerate(tiles_of(c)):
                            last = mm(PS[0:TOK, 4 + sc(s, c), j * D:(j + 1) * D], atc[s][:, tile(i)], w("out"),
                                      start=True, stop=True)
                        last.then_inc(S["pe_o"], 1)
                for s in range(2):
                    for c in range(NCH):
                        transpose_in(it, h, s, c, 3)
                for s in range(2):
                    for c in range(NCH):
                        pe.wait_ge(S["norm"], it * N["norm"] + 12 + sc(s, c) + 1)
                        transpose_back(it, ntm, s, c).then_inc(S["pe_back"], 1)
                for s in range(2):
                    pe.wait_ge(S["f_ready"], it * N["f_ready"] + 2 * s + 2)
                    for i in range(NT):
                        last = mm(PS[0:TOK, s, i * NG:(i + 1) * NG], z[s][:, tile(i)], w("gate"), start=True,
                                  stop=True)
                    last.then_inc(S["pe_gate"], 1)
                n = 0
                for s in range(2):
                    for c in range(NCH):
                        for gname in ("shared_in", "expert_in"):
                            for hh in range(2):
                                b = 4 + 2 * (n % 2)
                                if n == 0:
                                    pe.wait_ge(S["f_ready"], it * N["f_ready"] + 4)
                                if n >= 2:
                                    pe.wait_ge(S["h_ready"], it * N["h_ready"] + n - 1)
                                mm(PS[:, b, 0:CH], w(gname, hh * D, (hh + 1) * D), z[s][:, cols(c)],
                                   start=True, stop=True)
                                mm(PS[:, b + 1, 0:CH], w(gname, HID + hh * D, HID + (hh + 1) * D),
                                       z[s][:, cols(c)], start=True, stop=True).then_inc(S["pe_in"], 1)
                                n += 1
                pe.wait_ge(S["cnt_ready"], it * N["cnt_ready"] + 1)
                pe.wait_ge(S["h_ready"], it * N["h_ready"] + 16)
                for s in range(2):
                    if s:
                        pe.wait_ge(S["cnt_t"], it * N["cnt_t"] + 2)
                    for i in range(NT):
                        last = nc.tensor.transpose(PS[0:EXP + 1, 6 + i // TPC, tile(i % TPC)],
                                                   cnt9[0:TOK, s * NT + i, :], w("ident", 0, TOK, TOK))
                    last.then_inc(S["pe_cnt"], 1)
                for s in range(2):
                    for i in range(NT):
                        t = s * NT + i
                        if i == 0:
                            pe.wait_ge(S["cnt_t"], it * N["cnt_t"] + 2 * s + 2)
                        if t >= 2:
                            pe.wait_ge(S["tile_out"], it * N["tile_out"] + t - 1 + 1)
                        b = 4 + t % 2
                        for hh in range(2):
                            mm(PS[0:TOK, b, 0:D], H[s][0][hh][:, tile(i)], w("shared_out", hh * D, (hh + 1) * D),
                               start=hh == 0, stop=False)
                        mm(PS[0:TOK, b, 0:D], cnt_t[0:EXP + 1, s, tile(i)], w("bias_rows", p=EXP + 1), start=False,
                           stop=True)
                        b = 2 * (t % 2)
                        for half in range(2):
                            for hh in range(2):
                                at0 = hh * EXP * D + half * BANK
                                last = mm(PS[0:TOK, b + half, :], H[s][1][hh][:, tile(i)],
                                          w("expert_out", at0, at0 + BANK), start=hh == 0, stop=hh == 1)
                        last.then_inc(S["pe_out"], 1)

        @block.scalar
        def _(act):
            A = nc.scalar.activation
            with act.Fori(0, PAIRS) as it:
                act.wait_ge(w_first, 16)
                act.wait_ge(cleared, 5)
                for c in range(NCH):
                    act.wait_ge(S["pe_compress"], it * N["pe_compress"] + c + 1)
                    A(h1[:, 1 + c * CH:1 + (c + 1) * CH], PS[:, c, 0:CH], ACT.Silu, bias=vec("compress")).then_inc(S["h1_ready"], 1)
                for c in range(NCH):
                    act.wait_ge(S["pe_conv"], it * N["pe_conv"] + c + 1)
                    A(h2[:, cols(c)], PS[:, 2 + c, 0:CH], ACT.Silu, bias=vec("main")).then_inc(S["h2_ready"], 1)
                for s in range(2):
                    for c in range(NCH):
                        act.wait_ge(S["pe_back"], it * N["pe_back"] + sc(s, c) + 1)
                        A(y[s][:, cols(c)], PS[:, 4 + sc(s, c), 0:CH], ACT.Identity, bias=vec("conv_b"),
                              scale=vec("conv_g")).then_inc(S["y_ready"], 1)
                for c in range(NCH):
                    act.wait_ge(S["pe_ff1"], it * N["pe_ff1"] + c + 1)
                    A(g[:, cols(c)], PS[:, c, 0:CH], ACT.Gelu, bias=vec("ff1")).then_inc(S["g_ready"], 1)
                for s in range(2):
                    for c in range(NCH):
                        act.wait_ge(S["pe_back"], it * N["pe_back"] + 4 + sc(s, c) + 1)
                        A(z[s][:, cols(c)], PS[:, 4 + sc(s, c), 0:CH], ACT.Identity, bias=vec("ff_b"),
                              scale=vec("ff_g")).then_inc(S["z_ready"], 1)
                nc.scalar.preload_act_table_set("natural_log_exp_and_others")
                for s in range(2):
                    for c in range(NCH):
                        act.wait_ge(S["pe_back"], it * N["pe_back"] + 8 + sc(s, c) + 1)
                        act.wait_ge(S["r2_ready"], it * N["r2_ready"] + 4)
                        A(y[s][:, cols(c)], PS[:, 4 + sc(s, c), 0:CH], ACT.Identity).then_inc(S["n3_ready"], 1)
                act.wait_ge(w_rest, 16)
                for n, (name, projected) in enumerate((("q", S["pe_q"]), ("k", S["pe_k"]))):
                    for s in range(2):
                        for c in range(NCH):
                            act.wait_ge(projected, it * N["pe_q"] + sc(s, c) + 1)
                            if n:
                                act.wait_ge(S["q_ready"], it * N["q_ready"] + sc(s, c) + 1)
                            src = PS[:, 4 * n + sc(s, c), 0:CH]
                            A(e_in[sc(s, c)][:, :], src, ACT.Exp, bias=vec(name)).then_inc(S["in_exp"], 1)
                            A(r_in[sc(s, c)][:, :], src, ACT.Relu, bias=vec(name)).then_inc(S["in_relu"], 1)
                for s in range(2):
                    act.wait_ge(S["v_ready"], it * N["v_ready"] + 2 * s + 2)
                    A(lam[s][0:TOK, :, :], v[s][0:TOK, :, D:D + HEADS], ACT.Exp, scale=-1.0).then_inc(S["lam_exp"], 1)
                for s in range(2):
                    act.wait_ge(S["lam_ready"], it * N["lam_ready"] + s + 1)
                    A(logl[s][0:TOK, :, :], lam[s][0:TOK, :, :], ACT.Ln).then_inc(S["log_ready"], 1)
                for s in range(2):
                    for c in range(NCH):
                        act.wait_ge(S["pe_tk"], it * N["pe_tk"] + sc(s, c) + 1)
                        A(ktm[s][0:TOK, c * TPC:(c + 1) * TPC, :], tm_bank(4 + sc(s, c)), ACT.Identity).then_inc(S["ktm_ready"], 1)
                for s in range(2):
                    act.wait_ge(S["cum_clipped"], it * N["cum_clipped"] + s + 1)
                    A(dk[s][0:TOK, :, :], cum[s][0:TOK, :, :], ACT.Exp, scale=-1.0).then_inc(S["dk_ready"], 1)
                for s in range(2):
                    for c in range(NCH):
                        act.wait_ge(S["pe_tat"], it * N["pe_tat"] + sc(s, c) + 1)
                        A(atc[s][:, cols(c)], PS[:, sc(s, c), 0:CH], ACT.Identity).then_inc(S["atc_ready"], 1)
                for s in range(2):
                    act.wait_ge(S["o_ready"], it * N["o_ready"] + 2 * s + 2)
                    for i in range(NT):
                        last = A(q2[s][0:TOK].rearrange("p a n -> p (a n)")[:, i * D:(i + 1) * D], o[s][0:TOK, i, :], ACT.Square, scale=D ** -0.5,
                                 accum_out=ss[s][0:TOK, i:i + 1])
                    last.then_inc(S["sq_ready"], 1)
                for s in range(2):
                    for c in range(NCH):
                        act.wait_ge(S["pe_back"], it * N["pe_back"] + 12 + sc(s, c) + 1)
                        A(z[s][:, cols(c)], PS[:, 4 + sc(s, c), 0:CH], ACT.Identity, bias=vec("ln_b"),
                              scale=vec("ln_g")).then_inc(S["f_ready"], 1)
                act.wait_ge(S["route"], it * N["route"] + 4)
                A(rt[1][0:TOK], rt[0][0:TOK], ACT.Exp).then_inc(S["route_exp"], 1)
                for n in range(16):
                    act.wait_ge(S["pe_in"], it * N["pe_in"] + n + 1)
                    if n >= 2:
                        act.wait_ge(S["h_ready"], it * N["h_ready"] + n - 1)
                    A(sil[n % 2][:, :], PS[:, 4 + 2 * (n % 2), 0:CH], ACT.Silu).then_inc(S["silu_ready"], 1)
                for s in range(2):
                    act.wait_ge(S["pe_cnt"], it * N["pe_cnt"] + s + 1)
                    for c in range(NCH):
                        A(cnt_t[0:EXP + 1, s, cols(c)], PS[0:EXP + 1, 6 + c, 0:CH], ACT.Identity).then_inc(S["cnt_t"], 1)

        @block.vector
        def _(dve):
            V = nc.vector
            dve.wait_ge(w_first, 16)
            dve.wait_ge(cleared, 5)
            with dve.Fori(0, PAIRS) as it:
                smalls = [0]

                def small(ins):
                    ins.then_inc(S["small"], 1)
                    smalls[0] += 1
                    dve.wait_ge(S["small"], it * N["small"] + smalls[0])

                def statistics(norm, s, c, src):
                    u = 4 * norm + sc(s, c) + 1
                    for j, i in enumerate(tiles_of(c)):
                        last = V.bn_stats(st[s][0:TOK, i, :], src(j, i))
                    last.then_inc(S["stats"], 1)
                    if c == 1:
                        dve.wait_ge(S["stats"], it * N["stats"] + u)
                        n = 2 * norm + s
                        V.memset(scratch[0:1, n:n + 1], 0.0)
                        for i in range(NT):
                            last = V.bn_aggr(mv[s][0:TOK, i, :], st[s][0:TOK, i, :])
                        last.then_inc(S["var_ready"], 1)

                def normalise(norm, s, c, src):
                    if c == 0:
                        dve.wait_ge(S["rstd_ready"], it * N["rstd_ready"] + 2 * norm + s + 1)
                    for j, i in enumerate(tiles_of(c)):
                        last = V.tensor_scalar(ntm[s][0:TOK, i, :], src(j, i), mv[s][0:TOK, i, 0:1],
                                               rstd[s][0:TOK, i:i + 1], ALU.subtract, ALU.mult)
                    last.then_inc(S["norm"], 1)

                def norm_from_psum(norm):
                    for s in range(2):
                        for c in range(NCH):
                            dve.wait_ge(S["pe_t"], it * N["pe_t"] + 4 * norm + sc(s, c) + 1)
                            statistics(norm, s, c, lambda j, i: PS[0:TOK, sc(s, c), j * D:(j + 1) * D])
                    for s in range(2):
                        for c in range(NCH):
                            normalise(norm, s, c, lambda j, i: PS[0:TOK, sc(s, c), j * D:(j + 1) * D])

                for s in range(2):
                    for c in range(NCH):
                        dve.wait_ge(S["pe_expand"], it * N["pe_expand"] + sc(s, c) + 1)
                        ins = V.scalar_tensor_tensor(r[s][:, cols(c)], PS[:, 4 + sc(s, c), 0:CH], vec("expand"),
                                                     xs[s][:, cols(c)], ALU.add, ALU.add)
                        ins.then_inc(S["r1_ready"], 1)
                norm_from_psum(0)
                for s in range(2):
                    for c in range(NCH):
                        dve.wait_ge(S["pe_ff2"], it * N["pe_ff2"] + sc(s, c) + 1)
                        V.scalar_tensor_tensor(r[s][:, cols(c)], PS[:, 4 + sc(s, c), 0:CH], vec("ff2"),
                                                   y[s][:, cols(c)], ALU.add, ALU.add).then_inc(S["r2_ready"], 1)
                norm_from_psum(1)
                for s in range(2):
                    dve.wait_ge(S["z_ready"], it * N["z_ready"] + 2 * s + 2)
                    if s:
                        dve.wait_ge(S["pooled"], it * N["pooled"] + 2)
                    V.tensor_tensor(m2[:, 0:SEQ - 1], z[s][:, 0:SEQ - 1], z[s][:, 1:SEQ], ALU.max).then_inc(S["pooled"], 1)
                    dve.wait_ge(S["pooled"], it * N["pooled"] + 2 * s + 1)
                    V.tensor_tensor(h[s][:, 0:OUT_LEN], m2[:, 0:OUT_LEN], z[s][:, 2:SEQ], ALU.max).then_inc(S["pooled"], 1)
                norm_from_psum(2)
                for ready, dst, n in ((S["q_ready"], q, 0), (S["k_ready"], k, 4)):
                    for s in range(2):
                        for c in range(NCH):
                            dve.wait_ge(S["in_relu"], it * N["in_relu"] + n + sc(s, c) + 1)
                            V.scalar_tensor_tensor(dst[s][:, cols(c)], e_in[sc(s, c)][:, :], 1.0,
                                                       r_in[sc(s, c)][:, :], ALU.min, ALU.add).then_inc(ready, 1)
                dve.wait_ge(w_rest, 16)
                for s in range(2):
                    for c in range(NCH):
                        dve.wait_ge(S["pe_v"], it * N["pe_v"] + sc(s, c) + 1)
                        bias = w("row_v", p=TOK).unsqueeze(1).broadcast_to([TOK, TPC, D + HEADS])
                        V.tensor_tensor(v[s][0:TOK, c * TPC:(c + 1) * TPC, :], tm_bank(sc(s, c), D + HEADS),
                                            bias, ALU.add).then_inc(S["v_ready"], 1)
                for s in range(2):
                    dve.wait_ge(S["lam_exp"], it * N["lam_exp"] + s + 1)
                    small(V.tensor_scalar_add(lam2[s][0:TOK, :, :], lam[s][0:TOK, :, :], 1.0))
                    small(V.reciprocal(lam[s][0:TOK, :, :], lam2[s][0:TOK, :, :]))
                    small(V.tensor_scalar(lam2[s][0:TOK, :, :], lam[s][0:TOK, :, :], 0.1, 0.9, ALU.mult, ALU.add))
                    V.tensor_scalar_max(lam[s][0:TOK, :, :], lam2[s][0:TOK, :, :], 1e-6).then_inc(S["lam_ready"], 1)
                for s in range(2):
                    dve.wait_ge(S["pe_cum"], it * N["pe_cum"] + s + 1)
                    V.tensor_scalar(cum[s][0:TOK, :, :], PS[0:TOK, s, 0:NT * HEADS].rearrange(
                        "p (t n) -> p t n", t=NT), 50.0, -50.0, ALU.min, ALU.max).then_inc(S["cum_clipped"], 1)
                for s in range(2):
                    dve.wait_ge(S["dk_ready"], it * N["dk_ready"] + s + 1)
                    small(V.tensor_scalar_mul(dk4[s][0:TOK, :, :], dk[s][0:TOK, :, :], HD ** -0.5))
                    V.tensor_copy(vd[s][0:TOK, :, :, HD:HE], dk4[s][0:TOK, :, :].unsqueeze(3))
                    V.tensor_tensor(vd[s][0:TOK, :, :, 0:HD],
                                        v[s][0:TOK, :, 0:D].rearrange("p t (a b) -> p t a b", a=HEADS),
                                        dk4[s][0:TOK, :, :].unsqueeze(3).broadcast_to([TOK, NT, HEADS, HD]),
                                        ALU.mult).then_inc(S["vd_ready"], 1)

                def mask(i, s):
                    for half in range(2):
                        dve.wait_ge(S["pe_s"], it * N["pe_s"] + 4 * i + 2 * s + half + 1)
                        if i > 0:
                            dve.wait_ge(S["pe_num"], it * N["pe_num"] + 2 * (i - 1) + s + 1)
                        causal = w("tri", p=TOK).unsqueeze(1).unsqueeze(1).broadcast_to([TOK, 2, 2, TOK])
                        src = PS[0:TOK, 2 * half:2 * half + 2, 0:2 * TOK].rearrange("p b (a n) -> p b a n", a=2)
                        V.tensor_tensor(sm[s][0:TOK, 2 * half:2 * half + 2, :, :], src, causal, ALU.mult).then_inc(S["masked"], 1)

                def copy_state(i, s):
                    dve.wait_ge(S["pe_state"], it * N["pe_state"] + 2 * i + s + 1)
                    V.tensor_tensor(state[s][:, :], PS[:, 6 + s, 0:NV], w("blocks"), ALU.mult).then_inc(S["state_copied"], 1)

                def divide(c, s):
                    dve.wait_ge(S["pe_num"], it * N["pe_num"] + 2 * (TPC * (c + 1) - 1) + s + 1)
                    nd = PS[0:TOK, 4 + s, 0:TPC * NV].rearrange("p (t a b) -> p t a b", t=TPC, a=HEADS)
                    small(V.scalar_tensor_tensor(den[s][0:TOK, :, :], dk4[s][0:TOK, c * TPC:(c + 1) * TPC, :],
                                                 1e-6 * HD ** 0.5, nd[:, :, :, HD], ALU.mult, ALU.add))
                    V.reciprocal(rden[s][0:TOK, :, :], den[s][0:TOK, :, :]).then_inc(S["den_ready"], 1)
                    dve.wait_ge(S["den_ready"], it * N["den_ready"] + 2 * c + s + 1)
                    V.tensor_tensor(at[s][0:TOK, c * TPC:(c + 1) * TPC, :, :], nd[:, :, :, 0:HD],
                                        rden[s][0:TOK, :, :].unsqueeze(3).broadcast_to([TOK, TPC, HEADS, HD]),
                                        ALU.mult).then_inc(S["at_ready"], 1)

                steps = [(i, s) for i in range(NT) for s in range(2)]
                for n, (i, s) in enumerate(steps):
                    mask(i, s)
                    if n:
                        pi, psq = steps[n - 1]
                        if pi < NT - 1:
                            copy_state(pi, psq)
                        if pi == TPC - 1:
                            divide(0, psq)
                        if pi == NT - 1:
                            divide(1, psq)
                divide(1, 1)
                for s in range(2):
                    for c in range(NCH):
                        dve.wait_ge(S["pe_o"], it * N["pe_o"] + sc(s, c) + 1)
                        bias = w("row_out", p=TOK).unsqueeze(1).broadcast_to([TOK, TPC, D])
                        V.tensor_tensor(o[s][0:TOK, c * TPC:(c + 1) * TPC, :], tm_bank(4 + sc(s, c)), bias,
                                            ALU.add).then_inc(S["o_ready"], 1)
                for s in range(2):
                    dve.wait_ge(S["rms_ready"], it * N["rms_ready"] + s + 1)
                    for i in range(NT):
                        last = V.scalar_tensor_tensor(o2[s][0:TOK, i, :], o[s][0:TOK, i, :], rrms[s][0:TOK, i:i + 1],
                                                      w("row_scale", p=TOK), ALU.mult, ALU.mult)
                    last.then_inc(S["o2_ready"], 1)
                    dve.wait_ge(S["o2_ready"], it * N["o2_ready"] + s + 1)
                    for c in range(NCH):
                        dve.wait_ge(S["pe_t"], it * N["pe_t"] + 12 + sc(s, c) + 1)
                        V.tensor_tensor(r3[s][0:TOK, c * TPC:(c + 1) * TPC, :], tm_bank(sc(s, c)),
                                            o2[s][0:TOK, c * TPC:(c + 1) * TPC, :], ALU.add).then_inc(S["r3_ready"], 1)
                    for c in range(NCH):
                        dve.wait_ge(S["r3_ready"], it * N["r3_ready"] + sc(s, c) + 1)
                        statistics(3, s, c, lambda j, i: r3[s][0:TOK, i, :])
                for s in range(2):
                    for c in range(NCH):
                        normalise(3, s, c, lambda j, i: r3[s][0:TOK, i, :])

                routes = [0]

                def step(ins):
                    ins.then_inc(S["route"], 1)
                    routes[0] += 1
                    dve.wait_ge(S["route"], it * N["route"] + routes[0])

                G2 = 2 * NT * GROUPS
                for s in range(2):
                    dve.wait_ge(S["pe_gate"], it * N["pe_gate"] + s + 1)
                    src = PS[0:TOK, s, 0:NT * NG].rearrange("p (t n) -> p t n", t=NT)
                    V.tensor_tensor(gl[0:TOK, s * NT:(s + 1) * NT, :], src,
                                        w("row_gate", p=TOK).unsqueeze(1).broadcast_to([TOK, NT, NG]), ALU.add).then_inc(S["gl_ready"], 1)
                dve.wait_ge(S["gl_ready"], it * N["gl_ready"] + 2)
                logits = gl[0:TOK, :, GROUPS:NG].rearrange("p t (a b) -> p t a b", a=GROUPS)
                step(V.tensor_tensor(gind[0:TOK, :, 1:2], gl[0:TOK, :, 1:2], gl[0:TOK, :, 0:1], ALU.is_gt))
                step(V.tensor_scalar(gind[0:TOK, :, 0:1], gind[0:TOK, :, 1:2], -1.0, 1.0, ALU.mult, ALU.add))
                mx = rr[0][0:TOK, :].rearrange("p (t a) -> p t a", a=GROUPS)
                step(V.tensor_reduce(mx, logits, AX.X, ALU.max))
                step(V.tensor_tensor(rt[0][0:TOK], logits, mx.unsqueeze(3).broadcast_to([TOK, 2 * NT, GROUPS, EG]),
                                     ALU.subtract))
                dve.wait_ge(S["route_exp"], it * N["route_exp"] + 1)

                def flat(t):
                    return t[0:TOK].rearrange("p t a b -> p (t a) b")

                def over4(col):
                    return col[0:TOK, :].unsqueeze(2).broadcast_to([TOK, G2, EG])

                step(V.tensor_reduce(rr[1][0:TOK, :], flat(rt[1]), AX.X, ALU.add))
                step(V.reciprocal(rr[2][0:TOK, :], rr[1][0:TOK, :]))
                step(V.tensor_tensor(flat(rt[2]), flat(rt[1]), over4(rr[2]), ALU.mult))
                prob = flat(rt[2])
                other = prob.unsqueeze(2).broadcast_to([TOK, G2, EG, EG])
                own = prob.unsqueeze(3).broadcast_to([TOK, G2, EG, EG])
                step(V.tensor_tensor(pair4[0][0:TOK], other, own, ALU.is_gt))
                step(V.tensor_tensor(pair4[1][0:TOK], other, own, ALU.is_ge))

                def table(name):
                    return w(name, p=TOK).rearrange("p (a b) -> p a b", a=EG).unsqueeze(1).broadcast_to(
                        [TOK, G2, EG, EG])

                step(V.tensor_tensor(cmp8[0:TOK, :, :, 0:EG], pair4[0][0:TOK], table("after"), ALU.mult))
                step(V.tensor_tensor(cmp8[0:TOK, :, :, EG:2 * EG], pair4[1][0:TOK], table("before"), ALU.mult))
                step(V.tensor_reduce(flat(rt[3]), cmp8[0:TOK], AX.X, ALU.add))
                step(V.tensor_scalar(flat(rt[4]), flat(rt[3]), 1.5, None, ALU.is_lt))
                step(V.tensor_tensor(flat(rt[5]), prob, flat(rt[4]), ALU.mult))
                step(V.tensor_reduce(rr[3][0:TOK, :], flat(rt[5]), AX.X, ALU.add))
                step(V.tensor_scalar_add(rr[4][0:TOK, :], rr[3][0:TOK, :], 1e-8))
                step(V.reciprocal(rr[0][0:TOK, :], rr[4][0:TOK, :]))
                step(V.tensor_tensor(flat(rt[6]), flat(rt[5]), over4(rr[0]), ALU.mult))
                chosen = gind[0:TOK].unsqueeze(3).broadcast_to([TOK, 2 * NT, GROUPS, EG])
                step(V.tensor_tensor(comb[0:TOK], rt[6][0:TOK], chosen, ALU.mult))
                V.tensor_tensor(cnt9[0:TOK, :, 0:EXP].rearrange("p t (a b) -> p t a b", a=GROUPS), rt[4][0:TOK],
                                    chosen, ALU.mult).then_inc(S["cnt_ready"], 1)

                n = 0
                for s in range(2):
                    for c in range(NCH):
                        for gg in range(2):
                            for hh in range(2):
                                dve.wait_ge(S["silu_ready"], it * N["silu_ready"] + n + 1)
                                V.tensor_tensor(H[s][gg][hh][:, cols(c)], sil[n % 2][:, :],
                                                    PS[:, 5 + 2 * (n % 2), 0:CH], ALU.mult).then_inc(S["h_ready"], 1)
                                n += 1
                n = 0
                for s in range(2):
                    if s == 0:
                        dve.wait_ge(stored, it * 64 + 16)
                    for i in range(NT):
                        t = s * NT + i
                        dve.wait_ge(S["pe_out"], it * N["pe_out"] + t + 1)
                        a = acc[t % 2]
                        share = comb[0:TOK].rearrange("p t a b -> p t (a b)")
                        V.tensor_tensor(a[0][0:TOK, :], PS[0:TOK, 4 + t % 2, 0:D], r3[s][0:TOK, i, :], ALU.add).then_inc(S["acc"], 1)
                        for e in range(EXP):
                            src = PS[0:TOK, 2 * (t % 2) + e // 4, (e % 4) * D:(e % 4 + 1) * D]
                            dst = a[(e + 1) % 2][0:TOK, :]
                            if e == 0:
                                V.tensor_scalar(dst, src, share[:, t, e:e + 1], None, ALU.mult).then_inc(S["acc"], 1)
                            else:
                                dve.wait_ge(S["acc"], it * N["acc"] + n + e)
                                V.scalar_tensor_tensor(dst, src, share[:, t, e:e + 1], dst, ALU.mult, ALU.add).then_inc(S["acc"], 1)
                        dve.wait_ge(S["acc"], it * N["acc"] + n + 9)
                        V.tensor_tensor(res[s][0:TOK, i, :], a[0][0:TOK, :], a[1][0:TOK, :], ALU.add).then_inc(S["tile_out"], 1)
                        n += 9


def kernel(**inputs):
    import numpy as np
    import concourse.bacc as bacc
    from concourse.bass_utils import run_bass_kernel_spmd

    a = {n.replace("L0_", ""): np.asarray(t) for n, t in inputs.items()}
    pack = np.zeros((D, NW), np.float32)

    def put(name, block, row=0, col=0):
        block = np.asarray(block, np.float32)
        at = WCOLS[name][0] + col
        pack[row:row + block.shape[0], at:at + block.shape[1]] = block

    put("ident", np.eye(D))
    put("compress", a["tok_w_compress"][:, :, 0].T)
    for tap in range(3):
        for s in range(2):
            put("conv", a["tok_w_main"][:, :, tap].T, HALF * s, tap * D + HALF * s)
    for s in range(2):
        put("expand", a["tok_w_expand"][:, :, 0].T, HALF * s)
        put("ff2", a["tok_w_ff2"].T, HALF * s)
    put("ff1", a["tok_w_ff1"].T)
    for name, source in [("compress", "tok_b_compress"), ("main", "tok_b_main"), ("ff1", "tok_b_ff1")]:
        for s in range(2):
            put("vecs", a[source][:, None], HALF * s, VECS.index(name))
    qkv_b = a["attn_qkv_b"].reshape(3, D)
    for name, column in [("expand", a["tok_b_expand"]), ("conv_g", a["tok_g_conv_norm"]),
                         ("conv_b", a["tok_b_conv_norm"]), ("ff2", a["tok_b_ff2"]), ("ff_g", a["tok_g_ff_norm"]),
                         ("ff_b", a["tok_b_ff_norm"]), ("q", qkv_b[0]), ("k", qkv_b[1]), ("ln_g", a["ffn_ln_scale"]),
                         ("ln_b", a["ffn_ln_bias"])]:
        put("vecs", column[:, None], 0, VECS.index(name))
    qkv_w = a["attn_qkv_w"].reshape(3, D, D)
    put("q", qkv_w[0].T)
    put("k", qkv_w[1].T)
    put("v", qkv_w[2].T)
    put("v", a["attn_decay_w"].T, 0, D)
    put("out", a["attn_out_w"].T)
    put("tri", np.triu(np.ones((TOK, TOK))))
    put("ones", np.ones((TOK, TOK)))
    put("blocks", np.kron(np.eye(HEADS), np.ones((HD, HE))))
    put("parity", np.kron(np.ones((D // (2 * HD), 1)), np.kron(np.eye(2), np.ones((HD, 1)))))
    put("row_v", np.broadcast_to(qkv_b[2], (D, D)))
    put("row_v", np.broadcast_to(a["attn_decay_b"], (D, HEADS)), 0, D)
    put("row_out", np.broadcast_to(a["attn_out_b"], (D, D)))
    put("row_scale", np.broadcast_to(a["attn_norm_scale"], (D, D)))
    put("row_gate", np.broadcast_to(a["ffn_group_bias"], (D, GROUPS)))
    put("row_gate", np.broadcast_to(a["ffn_expert_bias"], (D, EXP)), 0, GROUPS)
    before = np.tril(np.ones((EG, EG)), -1)
    put("before", np.broadcast_to(before.reshape(-1), (D, EG * EG)))
    put("after", np.broadcast_to((1.0 - before).reshape(-1), (D, EG * EG)))
    put("halfneg", np.full((D, NT), -0.5))
    for name, value in [("eps", EPS), ("eps_rms", 1e-8), ("scale_two", 1.0 + EPS), ("eps_two", EPS * EPS)]:
        put(name, np.full((D, NT), value))
    put("shared_in", a["ffn_shared_in_w"].T)
    put("expert_in", a["ffn_expert_in_w"].T)
    for half in range(2):
        rows = slice(half * D, (half + 1) * D)
        put("shared_out", a["ffn_shared_out_w"].T[rows], 0, half * D)
        put("expert_out", a["ffn_expert_out_weight"].transpose(2, 0, 1).reshape(HID, EXP * D)[rows], 0,
            half * EXP * D)
    put("gate", a["ffn_group_gate_w"].T)
    put("gate", a["ffn_expert_gate_w"].T, 0, GROUPS)
    put("bias_rows", a["ffn_expert_out_bias"])
    put("bias_rows", a["ffn_shared_out_b"][None, :], EXP)

    arrays = {
        "wpack": pack,
        "x_cm": np.ascontiguousarray(a["x"].transpose(2, 0, 1).reshape(D, NSEQ * SEQ)),
    }
    nc = bacc.Bacc("TRN2", target_bir_lowering=False, num_devices=1)
    args = [nc.dram_tensor(n, t.shape, mybir.dt.from_np(t.dtype), kind="ExternalInput").ap()
            for n, t in arrays.items()]
    args.append(nc.dram_tensor("out", (NSEQ, OUT_LEN, D), F32, kind="ExternalOutput").ap())
    build(nc, *args)
    got = run_bass_kernel_spmd(nc, [arrays], core_ids=[0])
    return got.results[0]["out"]
```

```python
from contextlib import ExitStack

import concourse.bass as bass
from concourse import mybir

F32 = mybir.dt.float32
F32R = mybir.dt.float32r
ALU = mybir.AluOpType
ACT = mybir.ActivationFunctionType
AX = mybir.AxisListType

NSEQ, SEQ, D = 8, 750, 128
POOL = 3
OUT_LEN = SEQ - POOL + 1
PAIRS = NSEQ // 2
TOK = 125
NT = SEQ // TOK
NCH = 2
TPC = NT // NCH
CH = TPC * TOK
LAST = OUT_LEN - (NT - 1) * TOK
HALF = D // 2
HEADS, HD = 8, 16
HE = HD + 1
NV = HEADS * HE
HID = 256
EXP = 8
GROUPS, EG = 2, 4
NG = GROUPS + EXP
BANKS, BANK = 8, 512
EPS = 1e-5

WCOLS = {}


def _layout():
    at = 0
    for name, width in [
        ("ident", D), ("compress", HALF), ("conv", 3 * D), ("expand", D), ("ff1", HALF), ("ff2", D), ("vecs", 16),
        ("q", D), ("k", D), ("v", D + HEADS), ("out", D), ("tri", TOK), ("ones", TOK), ("blocks", NV), ("parity", 2),
        ("row_v", D + HEADS), ("row_out", D), ("row_scale", D), ("row_gate", NG), ("gate", NG), ("bias_rows", D), ("shared_out", 2 * D), ("before", 16), ("after", 16),
        ("halfneg", NT), ("eps", NT), ("eps_rms", NT), ("scale_two", NT), ("eps_two", NT),
    ]:
        WCOLS[name] = (at, at + width)
        at += width
    return at


NW = _layout()
W_FIRST = WCOLS["q"][0]
VECS = ["compress", "main", "expand", "conv_g", "conv_b", "ff1", "ff2", "ff_g", "ff_b", "q", "k", "ln_g", "ln_b"]

SPLIT = {"shared_in": (0, 2 * HID), "expert_in": (2 * HID, 4 * HID), "expert_out": (4 * HID, 4 * HID + 2 * EXP * D)}
NSPLIT = 4 * HID + 2 * EXP * D

PARTS = [slice(2 * TOK * p, 2 * TOK * (p + 1)) for p in range(NT // 2)]
HIDDEN_UNITS = 2 * len(PARTS) * 4
SHARED_UNITS = 2 * NCH * 2
EXPERT_UNITS = 2 * NT * 2
BACK = HIDDEN_UNITS + SHARED_UNITS + EXPERT_UNITS

FILLS = dict(
    compress=2, conv=2, expand0=1, expand1=1, y_tm00=1, y_tm01=1, y_tm10=1, y_tm11=1, y_wait=2, y_cm00=1, y_cm01=1,
    y_cm10=1, y_cm11=1, ff1=2, ff20=1, ff21=1, z_tm0=1, z_tm1=1, z_wait=2, z_cm0=1, z_cm1=1, pool=1, h_tm0=1, h_tm1=1,
    n3_cm=0, q=1, k=0, v=0, k_tm0=1, k_tm1=1, cum=1,
    s0=1, a0=1, s1=1, a1=1, s2=1, a2=1, s3=1, a3=1, s4=1, a4=1, s5=1, a5=1, s6=1, a6=1, s7=1, a7=1, s8=1, a8=1,
    s9=1, a9=0, s10=1, a10=0, s11=1, a11=0, at_cm=1, out=1, rms=0,
    h_res=0, f_norm=0, f_cm=0,
)
assert sum(FILLS.values()) == BACK


def units_of(stage, lag=0):
    names = list(FILLS)
    first = sum(FILLS[n] for n in names[:names.index(stage)])
    last = first + FILLS[stage]
    return range(max(first - lag, 0), BACK if stage == names[-1] else max(last - lag, 0))


PER_PAIR = dict(
    small=12, scaled=2, ms_ready=2, h1_ready=2, h2_ready=2, r1_ready=4, y_ready=4, g_ready=2, r2_ready=4, z_ready=4,
    pooled=4, n3_ready=4, in_exp=8, in_relu=8, q_ready=4, k_ready=4, q_split=4, v_ready=4, ktm_ready=4, lam_exp=2,
    lam_ready=2, log_ready=2, cum_clipped=2, dk_ready=2, vd_ready=2, masked=24, den_ready=4, at_ready=4,
    atc_ready=4, o_ready=4, sq_ready=2, rms_ready=2, o2_ready=2, r3_ready=4, f_ready=4, f_high=4, f_low=4, gl_ready=2,
    route_exp=1, route=19, cnt_ready=1, cnt_t=4, silu_ready=24, hidden_ready=24, high_ready=12, low_ready=12,
    shared_added=4, acc=96, chunk_done=4, state_copied=10, stats=16, var_ready=8, rstd_ready=8, norm=16, eps_added=8,
    pe_compress=2, pe_conv=2, pe_expand=4, pe_t=16, pe_back=16, pe_ff1=2, pe_ff2=4, pe_q=4, pe_k=4, pe_v=4, pe_tk=4,
    pe_cum=2, pe_s=24, pe_num=12, pe_state=10, pe_tat=4, pe_o=4, pe_gate=2, pe_cnt=4, pe_in=24, pe_shared=4,
    pe_exp=24,
)


def build(nc, wpack, wsplit, x, out):
    with ExitStack() as ctx:
        def sb(name, shape, dtype=F32):
            return ctx.enter_context(nc.sbuf_tensor(name, shape, dtype))

        W = sb("weights", [D, NW])

        def w(name, a=0, b=None, p=D):
            lo, hi = WCOLS[name]
            return W[0:p, lo + a:(hi if b is None else lo + b)]

        def vec(name, p0=0, p1=D):
            c = WCOLS["vecs"][0] + VECS.index(name)
            return W[p0:p1, c:c + 1]

        xs = [sb(f"x{s}", [D, SEQ]) for s in range(2)]
        h1 = sb("conv1", [D, SEQ + 2])
        h2 = sb("conv2", [D, SEQ])
        g = sb("g", [D, SEQ])
        r = [sb(f"r{s}", [D, SEQ]) for s in range(2)]
        ntm = [sb(f"ntm{s}", [D, NT, D]) for s in range(2)]
        y = [sb(f"y{s}", [D, SEQ]) for s in range(2)]
        z = [sb(f"z{s}", [D, SEQ]) for s in range(2)]
        m2 = h2
        h = [sb(f"h{s}", [D, SEQ]) for s in range(2)]
        st = [sb(f"st{s}", [D, NT, 6]) for s in range(2)]
        mv = [sb(f"mv{s}", [D, NT, 2]) for s in range(2)]
        ve = [sb(f"ve{s}", [D, NT]) for s in range(2)]
        rstd = [sb(f"rstd{s}", [D, NT]) for s in range(2)]
        e_in = [z[i // 2][:, (i % 2) * CH:(i % 2 + 1) * CH] for i in range(4)]
        r_in = [(h2, g)[i // 2][:, (i % 2) * CH:(i % 2 + 1) * CH] for i in range(4)]
        q = r
        k = [sb(f"k{s}", [D, SEQ]) for s in range(2)]
        q2 = [sb(f"q2{s}", [D, 2, SEQ]) for s in range(2)]
        ktm = ntm
        v = [sb(f"v{s}", [D, NT, D + HEADS]) for s in range(2)]
        lam = [sb(f"lam{s}", [D, NT, HEADS]) for s in range(2)]
        lam2 = [sb(f"lam2{s}", [D, NT, HEADS]) for s in range(2)]
        logl = [sb(f"logl{s}", [D, NT, HEADS]) for s in range(2)]
        cum = [sb(f"cum{s}", [D, NT, HEADS]) for s in range(2)]
        dk = [sb(f"dk{s}", [D, NT, HEADS]) for s in range(2)]
        dk4 = [sb(f"dk4{s}", [D, NT, HEADS]) for s in range(2)]
        vd = [sb(f"vd{s}", [D, NT, HEADS, HE]) for s in range(2)]
        sm = [sb(f"sm{s}", [D, 4, 2, TOK]) for s in range(2)]
        state = [sb(f"state{s}", [D, NV]) for s in range(2)]
        den = [sb(f"den{s}", [D, TPC, HEADS]) for s in range(2)]
        rden = [sb(f"rden{s}", [D, TPC, HEADS]) for s in range(2)]
        at = [sb(f"at{s}", [D, NT, HEADS, HD]) for s in range(2)]
        atc = k
        o = [t[:, :, :, :].rearrange("p t a b -> p t (a b)") for t in at]
        ss = [sb(f"ss{s}", [D, NT]) for s in range(2)]
        ms = [sb(f"ms{s}", [D, NT]) for s in range(2)]
        rrms = [sb(f"rrms{s}", [D, NT]) for s in range(2)]
        o2 = ntm
        r3 = [sb(f"r3{s}", [D, NT, D]) for s in range(2)]
        gl = sb("gl", [D, 2 * NT, NG])
        gind = sb("gind", [D, 2 * NT, GROUPS])
        rt = [sb(f"rt{i}", [D, 2 * NT, GROUPS, EG]) for i in range(7)]
        rr = [sb(f"rr{i}", [D, 2 * NT * GROUPS]) for i in range(5)]
        q2_flat = [t[:, :, :].rearrange("p a n -> p (a n)") for t in q2]
        npair = 2 * NT * GROUPS * EG * EG
        pair4 = [q2_flat[1][:, i * npair:(i + 1) * npair].rearrange("p (g a b) -> p g a b", a=EG, b=EG)
                 for i in range(2)]
        cmp8 = q2_flat[0][:, 0:2 * npair].rearrange("p (g a b) -> p g a b", a=EG, b=2 * EG)
        comb = sb("comb", [D, 2 * NT, GROUPS, EG])
        cnt9 = sb("cnt9", [D, 2 * NT, EXP + 1])
        cnt_t = sb("cnt_t", [EXP + 1, 2, CH])
        sil = [sb(f"sil{i}", [D, PARTS[0].stop]) for i in range(3)]
        f = y
        f_hi = [sb(f"f_hi{s}", [D, SEQ], F32R) for s in range(2)]
        f_lo = [sb(f"f_lo{s}", [D, SEQ], F32R) for s in range(2)]
        h_shared = [[sb(f"h_shared{s}{hh}", [D, SEQ]) for hh in range(2)] for s in range(2)]
        h_exp = [sb(f"h_exp{i}", [D, PARTS[0].stop]) for i in range(4)]
        h_hi = [[sb(f"h_hi{s}{hh}", [D, SEQ], F32R) for hh in range(2)] for s in range(2)]
        h_lo = [[sb(f"h_lo{s}{hh}", [D, SEQ], F32R) for hh in range(2)] for s in range(2)]
        result = [sb(f"result{s}", [D, NT, D]) for s in range(2)]
        acc2 = [sb(f"acc2{i}", [D, TPC, D]) for i in range(2)]
        w_hi = sb("w_hi", [D, NSPLIT], F32R)
        w_lo = sb("w_lo", [D, NSPLIT], F32R)
        staged = [(q2_flat[0], 0, 2 * SEQ), (q2_flat[1], 2 * SEQ, 4 * SEQ),
                  (h_shared[0][0][:, :], 4 * SEQ, NSPLIT)]
        scratch = sb("scratch", [1, 8])
        PS = ctx.enter_context(nc.psum_tensor("PS", [D, BANKS, BANK], F32))

        S = {n: ctx.enter_context(nc.semaphore(n)) for n in PER_PAIR}
        N = PER_PAIR
        w_first = ctx.enter_context(nc.semaphore("w_first"))
        w_rest = ctx.enter_context(nc.semaphore("w_rest"))
        w_staged = ctx.enter_context(nc.semaphore("w_staged"))
        w_high = ctx.enter_context(nc.semaphore("w_high"))
        w_low = ctx.enter_context(nc.semaphore("w_low"))
        x_in = ctx.enter_context(nc.semaphore("x_in"))
        result_free = ctx.enter_context(nc.semaphore("result_free"))
        cleared = ctx.enter_context(nc.semaphore("cleared"))

        def sc(s, c):
            return 2 * s + c

        def tiles_of(c):
            return range(c * TPC, (c + 1) * TPC)

        def cols(c):
            return slice(c * CH, (c + 1) * CH)

        def tile(i):
            return slice(i * TOK, (i + 1) * TOK)

        def tm_bank(b, width=D, p=TOK):
            return PS[0:p, b, 0:TPC * width].rearrange("p (t n) -> p t n", t=TPC)

        def part(name, half, a, b):
            return (w_hi, w_lo)[half][:, SPLIT[name][0] + a:SPLIT[name][0] + b]

        def hidden_unit(n):
            return n // (4 * len(PARTS)), n // 4 % len(PARTS), n // 2 % 2, n % 2

        def expert_count(n):
            return n // 4 * 2 + max(n % 4 - 2, 0)

        def shared_unit(n):
            m = n - HIDDEN_UNITS
            return (m // 4, m // 2 % 2, m % 2) if 0 <= m < SHARED_UNITS else None

        def expert_unit(n):
            m = n - HIDDEN_UNITS - SHARED_UNITS
            return m // (2 * NT), m // 2 % NT, m % 2

        block = ctx.enter_context(nc.Block())

        @block.sync
        def _(sp):
            sp.dma_start(W[:, 0:W_FIRST], wpack[:, 0:W_FIRST]).then_inc(w_first, 16)


            def load(pair):
                for s in range(2):
                    sp.dma_start(xs[s][:, :], x[:, bass.ds((2 * pair + s) * SEQ, SEQ)]).then_inc(x_in, 16)

            def store(pair):
                for s in range(2):
                    sp.wait_ge(S["chunk_done"], pair * N["chunk_done"] + 2 * s + 2)
                    dst = out[bass.ds(2 * pair + s, 1), :, :].rearrange("o l d -> (o l) d")
                    full = (NT - 1) * TOK
                    sp.dma_start(dst[0:full, :].rearrange("(t p) d -> p t d", p=TOK),
                                 result[s][0:TOK, 0:NT - 1, :]).then_inc(result_free, 16)
                    sp.dma_start(dst[full:OUT_LEN, :], result[s][0:LAST, NT - 1, :]).then_inc(result_free, 16)

            load(0)
            sp.dma_start(W[:, W_FIRST:NW], wpack[:, W_FIRST:NW]).then_inc(w_rest, 16)
            for buffer, lo, hi in staged:
                sp.dma_start(buffer[:, 0:hi - lo], wsplit[:, lo:hi]).then_inc(w_staged, 16)
            with sp.Fori(1, PAIRS) as it:
                sp.wait_ge(S["r1_ready"], it * N["r1_ready"])
                load(it)
                store(it - 1)
            store(PAIRS - 1)
            sp.wait_ge(result_free, (PAIRS + 1) * 4 * 16)

        @block.gpsimd
        def _(pool):
            TT = nc.gpsimd.tensor_tensor
            nc.gpsimd.memset(h1[:, 0:1], 0.0).then_inc(cleared, 1)
            nc.gpsimd.memset(h1[:, SEQ + 1:SEQ + 2], 0.0).then_inc(cleared, 1)
            for s in range(2):
                nc.gpsimd.memset(h[s][:, OUT_LEN:SEQ], 0.0).then_inc(cleared, 1)
            nc.gpsimd.memset(cnt9[0:TOK, :, EXP:EXP + 1], 1.0).then_inc(cleared, 1)
            nc.gpsimd.memset(acc2[0][0:1, 0, 0:1], 0.0).then_inc(result_free, 64)
            pool.wait_ge(w_rest, 16)

            def back(pair, units):
                for n in units:
                    if 0 <= n - 3 < HIDDEN_UNITS and hidden_unit(n - 3)[2]:
                        s, p, _, hh = hidden_unit(n - 3)
                        e = expert_count(n - 3)
                        cs = PARTS[p]
                        pool.wait_ge(S["high_ready"], pair * N["high_ready"] + e + 1)
                        TT(h_lo[s][hh][:, cs], h_exp[e % 4][:, :],
                           h_hi[s][hh][:, cs].bitcast(F32), ALU.subtract).then_inc(S["low_ready"], 1)
                    if n >= HIDDEN_UNITS + SHARED_UNITS:
                        s, i, half = expert_unit(n)
                        if half and i % TPC == TPC - 1:
                            c = i // TPC
                            pool.wait_ge(S["acc"], pair * N["acc"] + 24 * (sc(s, c) + 1))
                            dst = result[s][0:TOK, c * TPC:(c + 1) * TPC, :]
                            TT(dst, dst, acc2[c][0:TOK, :, :], ALU.add).then_inc(S["chunk_done"], 1)

            def front(it, first):
                def fill(stage):
                    if not first:
                        back(it - 1, units_of(stage, lag=2))

                def power(norm, s):
                    pool.wait_ge(S["var_ready"], it * N["var_ready"] + 2 * norm + s + 1)
                    var, eps = mv[s][0:TOK, :, 1], "eps"
                    if norm == 3:
                        TT(ms[s][0:TOK, :], var, w("scale_two", p=TOK), ALU.mult).then_inc(S["scaled"], 1)
                        pool.wait_ge(S["scaled"], it * N["scaled"] + s + 1)
                        var, eps = ms[s][0:TOK, :], "eps_two"
                    TT(ve[s][0:TOK, :], var, w(eps, p=TOK), ALU.add).then_inc(S["eps_added"], 1)
                    pool.wait_ge(S["eps_added"], it * N["eps_added"] + 2 * norm + s + 1)
                    TT(rstd[s][0:TOK, :], ve[s][0:TOK, :], w("halfneg", p=TOK), ALU.pow).then_inc(S["rstd_ready"], 1)

                for stage in ("compress", "conv", "expand0", "expand1", "y_tm00", "y_tm01"):
                    fill(stage)
                power(0, 0)
                fill("y_tm10")
                fill("y_tm11")
                power(0, 1)
                for stage in ("y_wait", "y_cm00", "y_cm01", "y_cm10", "y_cm11"):
                    fill(stage)
                if first:
                    for n, (buffer, lo, hi) in enumerate(staged):
                        pool.wait_ge(w_high, n + 1)
                        TT(w_lo[:, lo:hi], buffer[:, 0:hi - lo], w_hi[:, lo:hi].bitcast(F32),
                           ALU.subtract).then_inc(w_low, 1)
                for stage in ("ff1", "ff20", "ff21", "z_tm0"):
                    fill(stage)
                power(1, 0)
                fill("z_tm1")
                power(1, 1)
                for stage in ("z_wait", "z_cm0", "z_cm1", "pool", "h_tm0"):
                    fill(stage)
                power(2, 0)
                fill("h_tm1")
                power(2, 1)
                fill("n3_cm")
                fill("q")
                if first:
                    pool.wait_ge(w_low, 2)
                for s in range(2):
                    for c in range(NCH):
                        pool.wait_ge(S["q_ready"], it * N["q_ready"] + sc(s, c) + 1)
                        for par in range(2):
                            last = TT(q2[s][:, par, cols(c)], q[s][:, cols(c)],
                                      w("parity", par, par + 1).broadcast_to([D, CH]), ALU.mult)
                        last.then_inc(S["q_split"], 1)
                for stage in ("k", "v", "k_tm0", "k_tm1", "cum"):
                    fill(stage)
                for n in range(2 * NT):
                    fill(f"s{n}")
                    fill(f"a{n}")
                fill("at_cm")
                fill("out")
                for s in range(2):
                    pool.wait_ge(S["sq_ready"], it * N["sq_ready"] + s + 1)
                    TT(ms[s][0:TOK, :], ss[s][0:TOK, :], w("eps_rms", p=TOK), ALU.add).then_inc(S["ms_ready"], 1)
                    pool.wait_ge(S["ms_ready"], it * N["ms_ready"] + s + 1)
                    TT(rrms[s][0:TOK, :], ms[s][0:TOK, :], w("halfneg", p=TOK), ALU.pow).then_inc(S["rms_ready"], 1)
                for s in range(2):
                    power(3, s)
                for stage in ("rms", "h_res", "f_norm"):
                    fill(stage)
                for s in range(2):
                    for c in range(NCH):
                        pool.wait_ge(S["f_high"], it * N["f_high"] + sc(s, c) + 1)
                        TT(f_lo[s][:, cols(c)], f[s][:, cols(c)], f_hi[s][:, cols(c)].bitcast(F32),
                           ALU.subtract).then_inc(S["f_low"], 1)
                fill("f_cm")

            front(0, True)
            with pool.Fori(1, PAIRS) as it:
                front(it, False)
            back(PAIRS - 1, range(BACK))

        @block.tensor
        def _(pe):
            mm = nc.tensor.matmul

            def to_tm(src, s, c, bank):
                for j, i in enumerate(tiles_of(c)):
                    last = nc.tensor.transpose(PS[0:TOK, bank, j * D:(j + 1) * D], src[s][:, tile(i)], w("ident"))
                return last

            def to_cm(src, s, c, bank):
                for j, i in enumerate(tiles_of(c)):
                    last = nc.tensor.transpose(PS[:, bank, tile(j)], src[s][0:TOK, i, :], w("ident", 0, TOK, TOK))
                return last

            def back(pair, units):
                for n in units:
                    bank = 6 + n % 2
                    if n < HIDDEN_UNITS:
                        s, p, expert, hh = hidden_unit(n)
                        cs = PARTS[p]
                        if n == 0:
                            pe.wait_ge(S["f_low"], pair * N["f_low"] + 4)
                            pe.wait_ge(S["gl_ready"], pair * N["gl_ready"] + 2)
                        if n >= 2:
                            pe.wait_ge(S["hidden_ready"], pair * N["hidden_ready"] + n - 1)
                        name = ("shared_in", "expert_in")[expert]
                        for b in range(2):
                            col = b * HID + hh * D
                            dst = PS[:, bank, b * 2 * TOK:(b + 1) * 2 * TOK]
                            mm(dst, part(name, 0, col, col + D), f_hi[s][:, cs], start=True, stop=False)
                            mm(dst, part(name, 0, col, col + D), f_lo[s][:, cs], start=False, stop=False)
                            last = mm(dst, part(name, 1, col, col + D), f_hi[s][:, cs], start=False, stop=True)
                        last.then_inc(S["pe_in"], 1)
                        continue
                    if shared_unit(n):
                        s, c, main = shared_unit(n)
                        n_chunk = sc(s, c)
                        if not main:
                            if n_chunk == 0:
                                pe.wait_ge(S["hidden_ready"], pair * N["hidden_ready"] + HIDDEN_UNITS - 1)
                            else:
                                pe.wait_ge(S["cnt_t"], pair * N["cnt_t"] + n_chunk)
                            for j, i in enumerate(tiles_of(c)):
                                last = nc.tensor.transpose(PS[0:EXP + 1, bank, tile(j)], cnt9[0:TOK, s * NT + i, :],
                                                           w("ident", 0, TOK, TOK))
                            last.then_inc(S["pe_cnt"], 1)
                            continue
                        if n_chunk == 0:
                            pe.wait_ge(S["hidden_ready"], pair * N["hidden_ready"] + HIDDEN_UNITS)
                        else:
                            pe.wait_ge(S["shared_added"], pair * N["shared_added"] + n_chunk)
                        for j, i in enumerate(tiles_of(c)):
                            for hh in range(2):
                                mm(PS[0:TOK, bank, j * D:(j + 1) * D], h_shared[s][hh][:, tile(i)],
                                   w("shared_out", hh * D, (hh + 1) * D), start=j == 0 and hh == 0, stop=False,
                                   skip_group_check=True)
                        pe.wait_ge(S["cnt_t"], pair * N["cnt_t"] + n_chunk + 1)
                        for j in range(TPC):
                            last = mm(PS[0:TOK, bank, j * D:(j + 1) * D], cnt_t[0:EXP + 1, c, tile(j)],
                                      w("bias_rows", p=EXP + 1), start=False, stop=j == TPC - 1,
                                      skip_group_check=True)
                        last.then_inc(S["pe_shared"], 1)
                        continue
                    s, i, half = expert_unit(n)
                    if i == 0 and half == 0:
                        pe.wait_ge(S["low_ready"], pair * N["low_ready"] + (s + 1) * 2 * len(PARTS))
                    before = n - HIDDEN_UNITS - SHARED_UNITS
                    if before >= 2:
                        pe.wait_ge(S["acc"], pair * N["acc"] + EG * (before - 1))
                    elif half:
                        pe.wait_ge(S["shared_added"], pair * N["shared_added"] + 4)
                    dst = PS[0:TOK, bank, :]
                    for hh in range(2):
                        col = hh * EXP * D + half * BANK
                        hi, lo = h_hi[s][hh][:, tile(i)], h_lo[s][hh][:, tile(i)]
                        mm(dst, hi, part("expert_out", 0, col, col + BANK), start=hh == 0, stop=False)
                        mm(dst, hi, part("expert_out", 1, col, col + BANK), start=False, stop=False)
                        last = mm(dst, lo, part("expert_out", 0, col, col + BANK), start=False, stop=hh == 1)
                    last.then_inc(S["pe_exp"], 1)

            def front(it, first):
                def fill(stage):
                    if not first:
                        back(it - 1, units_of(stage))

                pe.wait_ge(x_in, it * 32 + 32)
                for c in range(NCH):
                    for s in range(2):
                        last = mm(PS[HALF * s:HALF * (s + 1), 2 + c, 0:CH], w("compress"), xs[s][:, cols(c)],
                                  start=True, stop=True)
                    last.then_inc(S["pe_compress"], 1)
                fill("compress")
                pe.wait_ge(S["h1_ready"], it * N["h1_ready"] + 2)
                if not first:
                    pe.wait_ge(S["gl_ready"], it * N["gl_ready"])
                for c in range(NCH):
                    for tap in range(3):
                        last = mm(PS[:, c, 0:CH], w("conv", tap * D, (tap + 1) * D),
                                  h1[:, c * CH + tap:c * CH + tap + CH], start=tap == 0, stop=tap == 2)
                    last.then_inc(S["pe_conv"], 1)
                fill("conv")
                pe.wait_ge(S["h2_ready"], it * N["h2_ready"] + 2)
                for s in range(2):
                    for c in range(NCH):
                        rows = slice(HALF * s, HALF * (s + 1))
                        lo, hi = WCOLS["expand"]
                        mm(PS[:, 4 - 2 * s + c, 0:CH], W[rows, lo:hi], h2[rows, cols(c)], start=True,
                           stop=True).then_inc(S["pe_expand"], 1)
                    fill(f"expand{s}")
                for s in range(2):
                    for c in range(NCH):
                        pe.wait_ge(S["r1_ready"], it * N["r1_ready"] + sc(s, c) + 1)
                        to_tm(r, s, c, sc(s, c)).then_inc(S["pe_t"], 1)
                        fill(f"y_tm{s}{c}")
                fill("y_wait")
                for s in range(2):
                    for c in range(NCH):
                        pe.wait_ge(S["norm"], it * N["norm"] + sc(s, c) + 1)
                        to_cm(ntm, s, c, 4 * (1 - s) + c).then_inc(S["pe_back"], 1)
                        fill(f"y_cm{s}{c}")
                pe.wait_ge(S["y_ready"], it * N["y_ready"] + 4)
                for c in range(NCH):
                    for s in range(2):
                        last = mm(PS[HALF * s:HALF * (s + 1), 2 + c, 0:CH], w("ff1"), y[s][:, cols(c)],
                                  start=True, stop=True)
                    last.then_inc(S["pe_ff1"], 1)
                fill("ff1")
                pe.wait_ge(S["g_ready"], it * N["g_ready"] + 2)
                for s in range(2):
                    for c in range(NCH):
                        rows = slice(HALF * s, HALF * (s + 1))
                        lo, hi = WCOLS["ff2"]
                        mm(PS[:, 4 - 2 * s + c, 0:CH], W[rows, lo:hi], g[rows, cols(c)], start=True,
                           stop=True).then_inc(S["pe_ff2"], 1)
                    fill(f"ff2{s}")
                for s in range(2):
                    for c in range(NCH):
                        pe.wait_ge(S["r2_ready"], it * N["r2_ready"] + sc(s, c) + 1)
                        to_tm(r, s, c, sc(s, c)).then_inc(S["pe_t"], 1)
                    fill(f"z_tm{s}")
                fill("z_wait")
                for s in range(2):
                    for c in range(NCH):
                        pe.wait_ge(S["norm"], it * N["norm"] + 4 + sc(s, c) + 1)
                        to_cm(ntm, s, c, 4 * (1 - s) + c).then_inc(S["pe_back"], 1)
                    fill(f"z_cm{s}")
                fill("pool")
                for s in range(2):
                    pe.wait_ge(S["pooled"], it * N["pooled"] + 2 * s + 2)
                    for c in range(NCH):
                        if s == 0:
                            pe.wait_ge(S["z_ready"], it * N["z_ready"] + c + 3)
                        to_tm(h, s, c, sc(s, c)).then_inc(S["pe_t"], 1)
                    fill(f"h_tm{s}")
                fill("n3_cm")
                for s in range(2):
                    for c in range(NCH):
                        pe.wait_ge(S["norm"], it * N["norm"] + 8 + sc(s, c) + 1)
                        to_cm(ntm, s, c, 4 * (1 - s) + c).then_inc(S["pe_back"], 1)
                if first:
                    pe.wait_ge(w_rest, 16)
                for s in range(2):
                    for c in range(NCH):
                        pe.wait_ge(S["n3_ready"], it * N["n3_ready"] + c + 3)
                        mm(PS[:, sc(s, c), 0:CH], w("q"), y[s][:, cols(c)], start=True,
                           stop=True).then_inc(S["pe_q"], 1)
                fill("q")
                for s in range(2):
                    for c in range(NCH):
                        if s:
                            pe.wait_ge(S["in_relu"], it * N["in_relu"] + c + 1)
                        mm(PS[:, 4 * (1 - s) + c, 0:CH], w("k"), y[s][:, cols(c)], start=True,
                           stop=True).then_inc(S["pe_k"], 1)
                fill("k")
                for s in range(2):
                    for c in range(NCH):
                        pe.wait_ge(S["in_relu"], it * N["in_relu"] + 2 + 2 * s + c + 1)
                        for j, i in enumerate(tiles_of(c)):
                            last = mm(PS[0:TOK, 2 + 2 * s + c, j * (D + HEADS):(j + 1) * (D + HEADS)],
                                      y[s][:, tile(i)], w("v"), start=True, stop=True)
                        last.then_inc(S["pe_v"], 1)
                fill("v")
                for s in range(2):
                    for c in range(NCH):
                        pe.wait_ge(S["k_ready"], it * N["k_ready"] + sc(s, c) + 1)
                        if s:
                            pe.wait_ge(S["v_ready"], it * N["v_ready"] + c + 1)
                        else:
                            pe.wait_ge(S["in_relu"], it * N["in_relu"] + 6 + c + 1)
                        to_tm(k, s, c, sc(s, c)).then_inc(S["pe_tk"], 1)
                    fill(f"k_tm{s}")
                for s in range(2):
                    pe.wait_ge(S["log_ready"], it * N["log_ready"] + s + 1)
                    if s == 0:
                        pe.wait_ge(S["v_ready"], it * N["v_ready"] + 4)
                    dst = PS[0:TOK, 4 + s, 0:NT * HEADS].rearrange("p (t n) -> p t n", t=NT)
                    mm(dst, w("tri", p=TOK), logl[s][0:TOK, :, :], start=True, stop=False)
                    for before in range(1, NT):
                        last = mm(dst[:, before:NT, :], w("ones", p=TOK), logl[s][0:TOK, 0:NT - before, :],
                                  start=False, stop=before == NT - 1)
                    last.then_inc(S["pe_cum"], 1)
                fill("cum")

                def scores(n, i, s):
                    for half in range(2):
                        u = 4 * i + 2 * s + half
                        if u == 0:
                            pe.wait_ge(S["q_split"], it * N["q_split"] + 4)
                            pe.wait_ge(S["ktm_ready"], it * N["ktm_ready"] + 4)
                            pe.wait_ge(S["cum_clipped"], it * N["cum_clipped"] + 2)
                        else:
                            pe.wait_ge(S["masked"], it * N["masked"] + u)
                        for b in range(2):
                            hd = 2 * half + b
                            rows = slice(32 * hd, 32 * hd + 32)
                            last = mm(PS[0:TOK, b, 0:2 * TOK].rearrange("p (a n) -> p a n", a=2), k[s][rows, tile(i)],
                                      q2[s][rows, :, tile(i)], start=True, stop=True, tile_position=(32 * hd, 0))
                        last.then_inc(S["pe_s"], 1)
                        if half == 0:
                            fill(f"s{n}")

                def attend(i, s):
                    if i == 0:
                        pe.wait_ge(S["vd_ready"], it * N["vd_ready"] + s + 1)
                    if i == TPC:
                        pe.wait_ge(S["at_ready"], it * N["at_ready"] + s + 1)
                    base = (i % TPC) * NV
                    if i > 0:
                        pe.wait_ge(S["state_copied"], it * N["state_copied"] + 2 * (i - 1) + s + 1)
                        mm(PS[0:TOK, 2 + s, base:base + NV], q[s][:, tile(i)], state[s][:, :],
                           start=True, stop=False, skip_group_check=True)
                    pe.wait_ge(S["masked"], it * N["masked"] + 4 * i + 2 * s + 2)
                    for hd in range(HEADS):
                        last = mm(PS[0:TOK, 2 + s, base + hd * HE:base + (hd + 1) * HE],
                                  sm[s][0:TOK, hd // 2, hd % 2, :], vd[s][0:TOK, i, hd, :],
                                  start=(i == 0 and hd == 0), stop=hd == HEADS - 1, skip_group_check=True)
                    last.then_inc(S["pe_num"], 1)
                    if i < NT - 1:
                        mm(PS[:, 4 + s, 0:NV], ktm[s][0:TOK, i, :], vd[s][0:TOK, i, :, :].rearrange("p a b -> p (a b)"),
                           start=i == 0, stop=True, skip_group_check=True).then_inc(S["pe_state"], 1)

                steps = [(i, s) for i in range(NT) for s in range(2)]
                for n, (i, s) in enumerate(steps):
                    scores(n, i, s)
                    if n:
                        attend(*steps[n - 1])
                    fill(f"a{n}")
                attend(*steps[-1])
                for s in range(2):
                    for c in range(NCH):
                        pe.wait_ge(S["at_ready"], it * N["at_ready"] + 2 * c + s + 1)
                        at_cm = [t[:, :, :, :].rearrange("p t a b -> p t (a b)") for t in at]
                        to_cm(at_cm, s, c, sc(s, c)).then_inc(S["pe_tat"], 1)
                fill("at_cm")
                for s in range(2):
                    for c in range(NCH):
                        pe.wait_ge(S["atc_ready"], it * N["atc_ready"] + sc(s, c) + 1)
                        if s:
                            pe.wait_ge(S["o_ready"], it * N["o_ready"] + c + 1)
                        for j, i in enumerate(tiles_of(c)):
                            last = mm(PS[0:TOK, 4 + c, j * D:(j + 1) * D], atc[s][:, tile(i)], w("out"),
                                      start=True, stop=True)
                        last.then_inc(S["pe_o"], 1)
                fill("out")
                fill("rms")
                for s in range(2):
                    for c in range(NCH):
                        to_tm(h, s, c, sc(s, c)).then_inc(S["pe_t"], 1)
                fill("h_res")
                fill("f_norm")
                for s in range(2):
                    for c in range(NCH):
                        pe.wait_ge(S["norm"], it * N["norm"] + 12 + sc(s, c) + 1)
                        if s:
                            pe.wait_ge(S["f_high"], it * N["f_high"] + c + 1)
                        to_cm(ntm, s, c, 4 + c).then_inc(S["pe_back"], 1)
                fill("f_cm")
                for s in range(2):
                    pe.wait_ge(S["f_ready"], it * N["f_ready"] + 2 * s + 2)
                    for i in range(NT):
                        last = mm(PS[0:TOK, s, i * NG:(i + 1) * NG], f[s][:, tile(i)], w("gate"), start=True,
                                  stop=True)
                    last.then_inc(S["pe_gate"], 1)

            pe.wait_ge(w_first, 16)
            front(0, True)
            pe.wait_ge(w_low, 3)
            with pe.Fori(1, PAIRS) as it:
                front(it, False)
            back(PAIRS - 1, range(BACK))

        @block.scalar
        def _(act):
            A = nc.scalar.activation

            def back(pair, units):
                for n in units:
                    if n < HIDDEN_UNITS:
                        act.wait_ge(S["pe_in"], pair * N["pe_in"] + n + 1)
                        if n >= 3:
                            act.wait_ge(S["hidden_ready"], pair * N["hidden_ready"] + n - 2)
                        A(sil[n % 3][:, :], PS[:, 6 + n % 2, 0:2 * TOK], ACT.Silu).then_inc(S["silu_ready"], 1)
                    if 0 <= n - 2 < HIDDEN_UNITS and hidden_unit(n - 2)[2]:
                        s, p, _, hh = hidden_unit(n - 2)
                        act.wait_ge(S["hidden_ready"], pair * N["hidden_ready"] + n - 1)
                        A(h_hi[s][hh][:, PARTS[p]], h_exp[expert_count(n - 2) % 4][:, :],
                          ACT.Identity).then_inc(S["high_ready"], 1)
                    if shared_unit(n) and not shared_unit(n)[2]:
                        s, c, _ = shared_unit(n)
                        act.wait_ge(S["pe_cnt"], pair * N["pe_cnt"] + sc(s, c) + 1)
                        A(cnt_t[0:EXP + 1, c, :], PS[0:EXP + 1, 6, 0:CH], ACT.Identity).then_inc(S["cnt_t"], 1)

            def front(it, first):
                def fill(stage):
                    if not first:
                        back(it - 1, units_of(stage))

                for c in range(NCH):
                    act.wait_ge(S["pe_compress"], it * N["pe_compress"] + c + 1)
                    A(h1[:, 1 + c * CH:1 + (c + 1) * CH], PS[:, 2 + c, 0:CH], ACT.Silu,
                      bias=vec("compress")).then_inc(S["h1_ready"], 1)
                fill("compress")
                for c in range(NCH):
                    act.wait_ge(S["pe_conv"], it * N["pe_conv"] + c + 1)
                    A(h2[:, cols(c)], PS[:, c, 0:CH], ACT.Silu, bias=vec("main")).then_inc(S["h2_ready"], 1)
                fill("conv")
                if first:
                    for n, (buffer, lo, hi) in enumerate(staged):
                        if n == 0:
                            act.wait_ge(w_staged, 16 * len(staged))
                        A(w_hi[:, lo:hi], buffer[:, 0:hi - lo], ACT.Identity).then_inc(w_high, 1)
                for stage in ("expand0", "expand1", "y_tm00", "y_tm01", "y_tm10", "y_tm11", "y_wait"):
                    fill(stage)
                for s in range(2):
                    for c in range(NCH):
                        act.wait_ge(S["pe_back"], it * N["pe_back"] + sc(s, c) + 1)
                        A(y[s][:, cols(c)], PS[:, 4 * (1 - s) + c, 0:CH], ACT.Identity, bias=vec("conv_b"),
                          scale=vec("conv_g")).then_inc(S["y_ready"], 1)
                        fill(f"y_cm{s}{c}")
                for c in range(NCH):
                    act.wait_ge(S["pe_ff1"], it * N["pe_ff1"] + c + 1)
                    A(g[:, cols(c)], PS[:, 2 + c, 0:CH], ACT.Gelu, bias=vec("ff1")).then_inc(S["g_ready"], 1)
                for stage in ("ff1", "ff20", "ff21", "z_tm0", "z_tm1", "z_wait"):
                    fill(stage)
                for s in range(2):
                    for c in range(NCH):
                        act.wait_ge(S["pe_back"], it * N["pe_back"] + 4 + sc(s, c) + 1)
                        A(z[s][:, cols(c)], PS[:, 4 * (1 - s) + c, 0:CH], ACT.Identity, bias=vec("ff_b"),
                          scale=vec("ff_g")).then_inc(S["z_ready"], 1)
                    fill(f"z_cm{s}")
                nc.scalar.preload_act_table_set("natural_log_exp_and_others")
                for stage in ("pool", "h_tm0", "h_tm1", "n3_cm"):
                    fill(stage)
                for s in range(2):
                    for c in range(NCH):
                        act.wait_ge(S["pe_back"], it * N["pe_back"] + 8 + sc(s, c) + 1)
                        act.wait_ge(S["r2_ready"], it * N["r2_ready"] + 4)
                        A(y[s][:, cols(c)], PS[:, 4 * (1 - s) + c, 0:CH], ACT.Identity).then_inc(S["n3_ready"], 1)
                if first:
                    act.wait_ge(w_rest, 16)
                for n, (name, projected) in enumerate((("q", S["pe_q"]), ("k", S["pe_k"]))):
                    for s in range(2):
                        for c in range(NCH):
                            act.wait_ge(projected, it * N["pe_q"] + sc(s, c) + 1)
                            if n:
                                act.wait_ge(S["q_ready"], it * N["q_ready"] + sc(s, c) + 1)
                            src = PS[:, 4 * (1 - s) + c if n else sc(s, c), 0:CH]
                            A(e_in[sc(s, c)], src, ACT.Exp, bias=vec(name)).then_inc(S["in_exp"], 1)
                            A(r_in[sc(s, c)], src, ACT.Relu, bias=vec(name)).then_inc(S["in_relu"], 1)
                    fill(name)
                fill("v")
                for s in range(2):
                    act.wait_ge(S["v_ready"], it * N["v_ready"] + 2 * s + 2)
                    A(lam[s][0:TOK, :, :], v[s][0:TOK, :, D:D + HEADS], ACT.Exp, scale=-1.0).then_inc(S["lam_exp"], 1)
                for s in range(2):
                    for c in range(NCH):
                        act.wait_ge(S["pe_tk"], it * N["pe_tk"] + sc(s, c) + 1)
                        A(ktm[s][0:TOK, c * TPC:(c + 1) * TPC, :], tm_bank(sc(s, c)),
                          ACT.Identity).then_inc(S["ktm_ready"], 1)
                    fill(f"k_tm{s}")
                for s in range(2):
                    act.wait_ge(S["lam_ready"], it * N["lam_ready"] + s + 1)
                    A(logl[s][0:TOK, :, :], lam[s][0:TOK, :, :], ACT.Ln).then_inc(S["log_ready"], 1)
                for s in range(2):
                    act.wait_ge(S["cum_clipped"], it * N["cum_clipped"] + s + 1)
                    A(dk[s][0:TOK, :, :], cum[s][0:TOK, :, :], ACT.Exp, scale=-1.0).then_inc(S["dk_ready"], 1)
                fill("cum")
                for n in range(2 * NT):
                    fill(f"s{n}")
                    fill(f"a{n}")
                for s in range(2):
                    for c in range(NCH):
                        act.wait_ge(S["pe_tat"], it * N["pe_tat"] + sc(s, c) + 1)
                        A(atc[s][:, cols(c)], PS[:, sc(s, c), 0:CH], ACT.Identity).then_inc(S["atc_ready"], 1)
                fill("at_cm")
                for s in range(2):
                    act.wait_ge(S["o_ready"], it * N["o_ready"] + 2 * s + 2)
                    for i in range(NT):
                        last = A(q2[s][0:TOK].rearrange("p a n -> p (a n)")[:, i * D:(i + 1) * D], o[s][0:TOK, i, :],
                                 ACT.Square, scale=D ** -0.5, accum_out=ss[s][0:TOK, i:i + 1])
                    last.then_inc(S["sq_ready"], 1)
                for stage in ("out", "rms", "h_res", "f_norm"):
                    fill(stage)
                for s in range(2):
                    for c in range(NCH):
                        act.wait_ge(S["pe_back"], it * N["pe_back"] + 12 + sc(s, c) + 1)
                        for dst, done in ((f[s], S["f_ready"]), (f_hi[s], S["f_high"])):
                            A(dst[:, cols(c)], PS[:, 4 + c, 0:CH], ACT.Identity, bias=vec("ln_b"),
                              scale=vec("ln_g")).then_inc(done, 1)
                fill("f_cm")
                act.wait_ge(S["route"], it * N["route"] + 4)
                A(rt[1][0:TOK], rt[0][0:TOK], ACT.Exp).then_inc(S["route_exp"], 1)

            act.wait_ge(w_first, 16)
            act.wait_ge(cleared, 5)
            front(0, True)
            with act.Fori(1, PAIRS) as it:
                front(it, False)
            back(PAIRS - 1, range(BACK))

        @block.vector
        def _(dve):
            V = nc.vector

            def back(pair, units):
                for n in units:
                    if n < HIDDEN_UNITS:
                        s, p, expert, hh = hidden_unit(n)
                        dve.wait_ge(S["silu_ready"], pair * N["silu_ready"] + n + 1)
                        dst = h_shared[s][hh][:, PARTS[p]]
                        if expert:
                            e = expert_count(n)
                            if e >= 4:
                                dve.wait_ge(S["low_ready"], pair * N["low_ready"] + e - 3)
                            dst = h_exp[e % 4][:, :]
                        V.tensor_tensor(dst, sil[n % 3][:, :], PS[:, 6 + n % 2, 2 * TOK:4 * TOK],
                                        ALU.mult).then_inc(S["hidden_ready"], 1)
                        continue
                    if shared_unit(n):
                        s, c, main = shared_unit(n)
                        if main:
                            if sc(s, c) == 0:
                                dve.wait_ge(result_free, 64 * (pair + 1))
                            dve.wait_ge(S["pe_shared"], pair * N["pe_shared"] + sc(s, c) + 1)
                            chunk = slice(c * TPC, (c + 1) * TPC)
                            V.tensor_tensor(result[s][0:TOK, chunk, :], tm_bank(7), r3[s][0:TOK, chunk, :],
                                            ALU.add).then_inc(S["shared_added"], 1)
                        continue
                    s, i, half = expert_unit(n)
                    before = n - HIDDEN_UNITS - SHARED_UNITS
                    dve.wait_ge(S["pe_exp"], pair * N["pe_exp"] + before + 1)
                    if i % TPC == 0 and half == 0:
                        dve.wait_ge(S["shared_added"], pair * N["shared_added"] + sc(s, i // TPC) + 1)
                    sums = result[s][0:TOK, i, :], acc2[i // TPC][0:TOK, i % TPC, :]
                    for e in range(EG):
                        src = PS[0:TOK, 6 + half, e * D:(e + 1) * D]
                        share = comb[0:TOK, s * NT + i, half, e:e + 1]
                        dst = sums[e % 2]
                        if half or e >= 2:
                            dve.wait_ge(S["acc"], pair * N["acc"] + EG * before + e - 1)
                        if half == 0 and e == 1:
                            if s and i % TPC == 0:
                                dve.wait_ge(S["chunk_done"], pair * N["chunk_done"] + i // TPC + 1)
                            V.tensor_scalar(dst, src, share, None, ALU.mult).then_inc(S["acc"], 1)
                        else:
                            V.scalar_tensor_tensor(dst, src, share, dst, ALU.mult, ALU.add).then_inc(S["acc"], 1)

            def front(it, first):
                def fill(stage):
                    if not first:
                        back(it - 1, units_of(stage, lag=1))

                smalls = [0]

                def small(ins):
                    ins.then_inc(S["small"], 1)
                    smalls[0] += 1
                    dve.wait_ge(S["small"], it * N["small"] + smalls[0])

                def statistics(norm, s, c, src):
                    u = 4 * norm + sc(s, c) + 1
                    for j, i in enumerate(tiles_of(c)):
                        last = V.bn_stats(st[s][0:TOK, i, :], src(j, i))
                    last.then_inc(S["stats"], 1)
                    if c == 1:
                        dve.wait_ge(S["stats"], it * N["stats"] + u)
                        n = 2 * norm + s
                        V.memset(scratch[0:1, n:n + 1], 0.0)
                        for i in range(NT):
                            last = V.bn_aggr(mv[s][0:TOK, i, :], st[s][0:TOK, i, :])
                        last.then_inc(S["var_ready"], 1)

                def normalise(norm, s, c, src):
                    if c == 0:
                        dve.wait_ge(S["rstd_ready"], it * N["rstd_ready"] + 2 * norm + s + 1)
                    for j, i in enumerate(tiles_of(c)):
                        last = V.tensor_scalar(ntm[s][0:TOK, i, :], src(j, i), mv[s][0:TOK, i, 0:1],
                                               rstd[s][0:TOK, i:i + 1], ALU.subtract, ALU.mult)
                    last.then_inc(S["norm"], 1)

                def norm_from_psum(norm, tm_stage, wait_stage, cm_stage, by_chunk):
                    for s in range(2):
                        for c in range(NCH):
                            dve.wait_ge(S["pe_t"], it * N["pe_t"] + 4 * norm + sc(s, c) + 1)
                            statistics(norm, s, c, lambda j, i: PS[0:TOK, sc(s, c), j * D:(j + 1) * D])
                            if by_chunk:
                                fill(f"{tm_stage}{s}{c}")
                        if not by_chunk:
                            fill(f"{tm_stage}{s}")
                    fill(wait_stage)
                    for s in range(2):
                        for c in range(NCH):
                            normalise(norm, s, c, lambda j, i: PS[0:TOK, sc(s, c), j * D:(j + 1) * D])
                            if by_chunk:
                                fill(f"{cm_stage}{s}{c}")
                        if not by_chunk and cm_stage:
                            fill(f"{cm_stage}{s}")

                fill("compress")
                fill("conv")
                for s in range(2):
                    for c in range(NCH):
                        dve.wait_ge(S["pe_expand"], it * N["pe_expand"] + sc(s, c) + 1)
                        ins = V.scalar_tensor_tensor(r[s][:, cols(c)], PS[:, 4 - 2 * s + c, 0:CH], vec("expand"),
                                                     xs[s][:, cols(c)], ALU.add, ALU.add)
                        ins.then_inc(S["r1_ready"], 1)
                    fill(f"expand{s}")
                norm_from_psum(0, "y_tm", "y_wait", "y_cm", True)
                fill("ff1")
                for s in range(2):
                    for c in range(NCH):
                        dve.wait_ge(S["pe_ff2"], it * N["pe_ff2"] + sc(s, c) + 1)
                        V.scalar_tensor_tensor(r[s][:, cols(c)], PS[:, 4 - 2 * s + c, 0:CH], vec("ff2"),
                                               y[s][:, cols(c)], ALU.add, ALU.add).then_inc(S["r2_ready"], 1)
                    fill(f"ff2{s}")
                norm_from_psum(1, "z_tm", "z_wait", "z_cm", False)
                fill("pool")
                for s in range(2):
                    dve.wait_ge(S["z_ready"], it * N["z_ready"] + 2 * s + 2)
                    if s:
                        dve.wait_ge(S["pooled"], it * N["pooled"] + 2)
                    V.tensor_tensor(m2[:, 0:SEQ - 1], z[s][:, 0:SEQ - 1], z[s][:, 1:SEQ], ALU.max).then_inc(S["pooled"], 1)
                    dve.wait_ge(S["pooled"], it * N["pooled"] + 2 * s + 1)
                    V.tensor_tensor(h[s][:, 0:OUT_LEN], m2[:, 0:OUT_LEN], z[s][:, 2:SEQ], ALU.max).then_inc(S["pooled"], 1)
                norm_from_psum(2, "h_tm", "n3_cm", None, False)
                for ready, dst, n in ((S["q_ready"], q, 0), (S["k_ready"], k, 4)):
                    for s in range(2):
                        for c in range(NCH):
                            dve.wait_ge(S["in_relu"], it * N["in_relu"] + n + sc(s, c) + 1)
                            V.scalar_tensor_tensor(dst[s][:, cols(c)], e_in[sc(s, c)], 1.0,
                                                       r_in[sc(s, c)], ALU.min, ALU.add).then_inc(ready, 1)
                    fill("k" if n else "q")
                if first:
                    dve.wait_ge(w_rest, 16)
                for s in range(2):
                    for c in range(NCH):
                        dve.wait_ge(S["pe_v"], it * N["pe_v"] + sc(s, c) + 1)
                        bias = w("row_v", p=TOK).unsqueeze(1).broadcast_to([TOK, TPC, D + HEADS])
                        V.tensor_tensor(v[s][0:TOK, c * TPC:(c + 1) * TPC, :], tm_bank(2 + 2 * s + c, D + HEADS),
                                            bias, ALU.add).then_inc(S["v_ready"], 1)
                fill("v")
                for s in range(2):
                    dve.wait_ge(S["lam_exp"], it * N["lam_exp"] + s + 1)
                    small(V.tensor_scalar_add(lam2[s][0:TOK, :, :], lam[s][0:TOK, :, :], 1.0))
                    small(V.reciprocal(lam[s][0:TOK, :, :], lam2[s][0:TOK, :, :]))
                    small(V.tensor_scalar(lam2[s][0:TOK, :, :], lam[s][0:TOK, :, :], 0.1, 0.9, ALU.mult, ALU.add))
                    V.tensor_scalar_max(lam[s][0:TOK, :, :], lam2[s][0:TOK, :, :], 1e-6).then_inc(S["lam_ready"], 1)
                fill("k_tm0")
                fill("k_tm1")
                for s in range(2):
                    dve.wait_ge(S["pe_cum"], it * N["pe_cum"] + s + 1)
                    V.tensor_scalar(cum[s][0:TOK, :, :], PS[0:TOK, 4 + s, 0:NT * HEADS].rearrange(
                        "p (t n) -> p t n", t=NT), 50.0, -50.0, ALU.min, ALU.max).then_inc(S["cum_clipped"], 1)
                for s in range(2):
                    dve.wait_ge(S["dk_ready"], it * N["dk_ready"] + s + 1)
                    small(V.tensor_scalar_mul(dk4[s][0:TOK, :, :], dk[s][0:TOK, :, :], HD ** -0.5))
                    V.tensor_copy(vd[s][0:TOK, :, :, HD:HE], dk4[s][0:TOK, :, :].unsqueeze(3))
                    V.tensor_tensor(vd[s][0:TOK, :, :, 0:HD],
                                        v[s][0:TOK, :, 0:D].rearrange("p t (a b) -> p t a b", a=HEADS),
                                        dk4[s][0:TOK, :, :].unsqueeze(3).broadcast_to([TOK, NT, HEADS, HD]),
                                        ALU.mult).then_inc(S["vd_ready"], 1)

                fill("cum")

                def mask(n, i, s):
                    for half in range(2):
                        dve.wait_ge(S["pe_s"], it * N["pe_s"] + 4 * i + 2 * s + half + 1)
                        if i > 0:
                            dve.wait_ge(S["pe_num"], it * N["pe_num"] + 2 * (i - 1) + s + 1)
                        causal = w("tri", p=TOK).unsqueeze(1).unsqueeze(1).broadcast_to([TOK, 2, 2, TOK])
                        src = PS[0:TOK, 0:2, 0:2 * TOK].rearrange("p b (a n) -> p b a n", a=2)
                        V.tensor_tensor(sm[s][0:TOK, 2 * half:2 * half + 2, :, :], src, causal,
                                        ALU.mult).then_inc(S["masked"], 1)
                        if half == 0:
                            fill(f"s{n}")

                def copy_state(i, s):
                    dve.wait_ge(S["pe_state"], it * N["pe_state"] + 2 * i + s + 1)
                    V.tensor_tensor(state[s][:, :], PS[:, 4 + s, 0:NV], w("blocks"), ALU.mult).then_inc(S["state_copied"], 1)

                def divide(c, s):
                    dve.wait_ge(S["pe_num"], it * N["pe_num"] + 2 * (TPC * (c + 1) - 1) + s + 1)
                    nd = PS[0:TOK, 2 + s, 0:TPC * NV].rearrange("p (t a b) -> p t a b", t=TPC, a=HEADS)
                    small(V.scalar_tensor_tensor(den[s][0:TOK, :, :], dk4[s][0:TOK, c * TPC:(c + 1) * TPC, :],
                                                 1e-6 * HD ** 0.5, nd[:, :, :, HD], ALU.mult, ALU.add))
                    V.reciprocal(rden[s][0:TOK, :, :], den[s][0:TOK, :, :]).then_inc(S["den_ready"], 1)
                    dve.wait_ge(S["den_ready"], it * N["den_ready"] + 2 * c + s + 1)
                    V.tensor_tensor(at[s][0:TOK, c * TPC:(c + 1) * TPC, :, :], nd[:, :, :, 0:HD],
                                        rden[s][0:TOK, :, :].unsqueeze(3).broadcast_to([TOK, TPC, HEADS, HD]),
                                        ALU.mult).then_inc(S["at_ready"], 1)

                steps = [(i, s) for i in range(NT) for s in range(2)]
                for n, (i, s) in enumerate(steps):
                    mask(n, i, s)
                    if n:
                        pi, psq = steps[n - 1]
                        if pi < NT - 1:
                            copy_state(pi, psq)
                        if pi == TPC - 1:
                            divide(0, psq)
                        if pi == NT - 1:
                            divide(1, psq)
                    fill(f"a{n}")
                divide(1, 1)
                fill("at_cm")
                for s in range(2):
                    for c in range(NCH):
                        dve.wait_ge(S["pe_o"], it * N["pe_o"] + sc(s, c) + 1)
                        bias = w("row_out", p=TOK).unsqueeze(1).broadcast_to([TOK, TPC, D])
                        V.tensor_tensor(o[s][0:TOK, c * TPC:(c + 1) * TPC, :], tm_bank(4 + c), bias,
                                            ALU.add).then_inc(S["o_ready"], 1)
                fill("out")
                fill("rms")
                for s in range(2):
                    dve.wait_ge(S["rms_ready"], it * N["rms_ready"] + s + 1)
                    for i in range(NT):
                        last = V.scalar_tensor_tensor(o2[s][0:TOK, i, :], o[s][0:TOK, i, :], rrms[s][0:TOK, i:i + 1],
                                                      w("row_scale", p=TOK), ALU.mult, ALU.mult)
                    last.then_inc(S["o2_ready"], 1)
                    dve.wait_ge(S["o2_ready"], it * N["o2_ready"] + s + 1)
                    for c in range(NCH):
                        dve.wait_ge(S["pe_t"], it * N["pe_t"] + 12 + sc(s, c) + 1)
                        V.tensor_tensor(r3[s][0:TOK, c * TPC:(c + 1) * TPC, :], tm_bank(sc(s, c)),
                                            o2[s][0:TOK, c * TPC:(c + 1) * TPC, :], ALU.add).then_inc(S["r3_ready"], 1)
                    for c in range(NCH):
                        dve.wait_ge(S["r3_ready"], it * N["r3_ready"] + sc(s, c) + 1)
                        statistics(3, s, c, lambda j, i: r3[s][0:TOK, i, :])
                fill("h_res")
                for s in range(2):
                    for c in range(NCH):
                        normalise(3, s, c, lambda j, i: r3[s][0:TOK, i, :])
                fill("f_norm")
                fill("f_cm")

                routes = [0]

                def step(ins):
                    ins.then_inc(S["route"], 1)
                    routes[0] += 1
                    dve.wait_ge(S["route"], it * N["route"] + routes[0])

                G2 = 2 * NT * GROUPS
                for s in range(2):
                    dve.wait_ge(S["pe_gate"], it * N["pe_gate"] + s + 1)
                    src = PS[0:TOK, s, 0:NT * NG].rearrange("p (t n) -> p t n", t=NT)
                    V.tensor_tensor(gl[0:TOK, s * NT:(s + 1) * NT, :], src,
                                        w("row_gate", p=TOK).unsqueeze(1).broadcast_to([TOK, NT, NG]), ALU.add).then_inc(S["gl_ready"], 1)
                dve.wait_ge(S["gl_ready"], it * N["gl_ready"] + 2)
                logits = gl[0:TOK, :, GROUPS:NG].rearrange("p t (a b) -> p t a b", a=GROUPS)
                step(V.tensor_tensor(gind[0:TOK, :, 1:2], gl[0:TOK, :, 1:2], gl[0:TOK, :, 0:1], ALU.is_gt))
                step(V.tensor_scalar(gind[0:TOK, :, 0:1], gind[0:TOK, :, 1:2], -1.0, 1.0, ALU.mult, ALU.add))
                mx = rr[0][0:TOK, :].rearrange("p (t a) -> p t a", a=GROUPS)
                step(V.tensor_reduce(mx, logits, AX.X, ALU.max))
                step(V.tensor_tensor(rt[0][0:TOK], logits, mx.unsqueeze(3).broadcast_to([TOK, 2 * NT, GROUPS, EG]),
                                     ALU.subtract))
                dve.wait_ge(S["route_exp"], it * N["route_exp"] + 1)

                def flat(t):
                    return t[0:TOK].rearrange("p t a b -> p (t a) b")

                def over4(col):
                    return col[0:TOK, :].unsqueeze(2).broadcast_to([TOK, G2, EG])

                step(V.tensor_reduce(rr[1][0:TOK, :], flat(rt[1]), AX.X, ALU.add))
                step(V.reciprocal(rr[2][0:TOK, :], rr[1][0:TOK, :]))
                step(V.tensor_tensor(flat(rt[2]), flat(rt[1]), over4(rr[2]), ALU.mult))
                prob = flat(rt[2])
                other = prob.unsqueeze(2).broadcast_to([TOK, G2, EG, EG])
                own = prob.unsqueeze(3).broadcast_to([TOK, G2, EG, EG])
                step(V.tensor_tensor(pair4[0][0:TOK], other, own, ALU.is_gt))
                step(V.tensor_tensor(pair4[1][0:TOK], other, own, ALU.is_ge))

                def table(name):
                    return w(name, p=TOK).rearrange("p (a b) -> p a b", a=EG).unsqueeze(1).broadcast_to(
                        [TOK, G2, EG, EG])

                step(V.tensor_tensor(cmp8[0:TOK, :, :, 0:EG], pair4[0][0:TOK], table("after"), ALU.mult))
                step(V.tensor_tensor(cmp8[0:TOK, :, :, EG:2 * EG], pair4[1][0:TOK], table("before"), ALU.mult))
                step(V.tensor_reduce(flat(rt[3]), cmp8[0:TOK], AX.X, ALU.add))
                step(V.tensor_scalar(flat(rt[4]), flat(rt[3]), 1.5, None, ALU.is_lt))
                step(V.tensor_tensor(flat(rt[5]), prob, flat(rt[4]), ALU.mult))
                step(V.tensor_reduce(rr[3][0:TOK, :], flat(rt[5]), AX.X, ALU.add))
                step(V.tensor_scalar_add(rr[4][0:TOK, :], rr[3][0:TOK, :], 1e-8))
                step(V.reciprocal(rr[0][0:TOK, :], rr[4][0:TOK, :]))
                step(V.tensor_tensor(flat(rt[6]), flat(rt[5]), over4(rr[0]), ALU.mult))
                chosen = gind[0:TOK].unsqueeze(3).broadcast_to([TOK, 2 * NT, GROUPS, EG])
                step(V.tensor_tensor(comb[0:TOK], rt[6][0:TOK], chosen, ALU.mult))
                V.tensor_tensor(cnt9[0:TOK, :, 0:EXP].rearrange("p t (a b) -> p t a b", a=GROUPS), rt[4][0:TOK],
                                    chosen, ALU.mult).then_inc(S["cnt_ready"], 1)

            dve.wait_ge(w_first, 16)
            dve.wait_ge(cleared, 5)
            front(0, True)
            with dve.Fori(1, PAIRS) as it:
                front(it, False)
            back(PAIRS - 1, range(BACK))


def kernel(**inputs):
    import numpy as np
    import concourse.bacc as bacc
    from concourse.bass_utils import run_bass_kernel_spmd

    a = {n.replace("L0_", ""): np.asarray(t) for n, t in inputs.items()}
    pack = np.zeros((D, NW), np.float32)

    def put(name, block, row=0, col=0):
        block = np.asarray(block, np.float32)
        at = WCOLS[name][0] + col
        pack[row:row + block.shape[0], at:at + block.shape[1]] = block

    put("ident", np.eye(D))
    put("compress", a["tok_w_compress"][:, :, 0].T)
    for tap in range(3):
        for s in range(2):
            put("conv", a["tok_w_main"][:, :, tap].T, HALF * s, tap * D + HALF * s)
    for s in range(2):
        put("expand", a["tok_w_expand"][:, :, 0].T, HALF * s)
        put("ff2", a["tok_w_ff2"].T, HALF * s)
    put("ff1", a["tok_w_ff1"].T)
    for name, source in [("compress", "tok_b_compress"), ("main", "tok_b_main"), ("ff1", "tok_b_ff1")]:
        for s in range(2):
            put("vecs", a[source][:, None], HALF * s, VECS.index(name))
    qkv_b = a["attn_qkv_b"].reshape(3, D)
    for name, column in [("expand", a["tok_b_expand"]), ("conv_g", a["tok_g_conv_norm"]),
                         ("conv_b", a["tok_b_conv_norm"]), ("ff2", a["tok_b_ff2"]), ("ff_g", a["tok_g_ff_norm"]),
                         ("ff_b", a["tok_b_ff_norm"]), ("q", qkv_b[0]), ("k", qkv_b[1]), ("ln_g", a["ffn_ln_scale"]),
                         ("ln_b", a["ffn_ln_bias"])]:
        put("vecs", column[:, None], 0, VECS.index(name))
    qkv_w = a["attn_qkv_w"].reshape(3, D, D)
    put("q", qkv_w[0].T)
    put("k", qkv_w[1].T)
    put("v", qkv_w[2].T)
    put("v", a["attn_decay_w"].T, 0, D)
    put("out", a["attn_out_w"].T)
    put("tri", np.triu(np.ones((TOK, TOK))))
    put("ones", np.ones((TOK, TOK)))
    put("blocks", np.kron(np.eye(HEADS), np.ones((HD, HE))))
    put("parity", np.kron(np.ones((D // (2 * HD), 1)), np.kron(np.eye(2), np.ones((HD, 1)))))
    put("row_v", np.broadcast_to(qkv_b[2], (D, D)))
    put("row_v", np.broadcast_to(a["attn_decay_b"], (D, HEADS)), 0, D)
    put("row_out", np.broadcast_to(a["attn_out_b"], (D, D)))
    put("row_scale", np.broadcast_to(a["attn_norm_scale"], (D, D)))
    put("row_gate", np.broadcast_to(a["ffn_group_bias"], (D, GROUPS)))
    put("row_gate", np.broadcast_to(a["ffn_expert_bias"], (D, EXP)), 0, GROUPS)
    before = np.tril(np.ones((EG, EG)), -1)
    put("before", np.broadcast_to(before.reshape(-1), (D, EG * EG)))
    put("after", np.broadcast_to((1.0 - before).reshape(-1), (D, EG * EG)))
    put("halfneg", np.full((D, NT), -0.5))
    for name, value in [("eps", EPS), ("eps_rms", 1e-8), ("scale_two", 1.0 + EPS), ("eps_two", EPS * EPS)]:
        put(name, np.full((D, NT), value))
    split = np.zeros((D, NSPLIT), np.float32)

    def put_split(name, block, col=0):
        at = SPLIT[name][0] + col
        split[:, at:at + block.shape[1]] = block

    put_split("shared_in", a["ffn_shared_in_w"].T)
    put_split("expert_in", a["ffn_expert_in_w"].T)
    for half in range(2):
        rows = slice(half * D, (half + 1) * D)
        put("shared_out", a["ffn_shared_out_w"].T[rows], 0, half * D)
        put_split("expert_out", a["ffn_expert_out_weight"].transpose(2, 0, 1).reshape(HID, EXP * D)[rows],
                  half * EXP * D)
    put("gate", a["ffn_group_gate_w"].T)
    put("gate", a["ffn_expert_gate_w"].T, 0, GROUPS)
    put("bias_rows", a["ffn_expert_out_bias"])
    put("bias_rows", a["ffn_shared_out_b"][None, :], EXP)

    arrays = {
        "wpack": pack,
        "wsplit": split,
        "x_cm": np.ascontiguousarray(a["x"].transpose(2, 0, 1).reshape(D, NSEQ * SEQ)),
    }
    nc = bacc.Bacc("TRN2", target_bir_lowering=False, num_devices=1)
    args = [nc.dram_tensor(n, t.shape, mybir.dt.from_np(t.dtype), kind="ExternalInput").ap()
            for n, t in arrays.items()]
    args.append(nc.dram_tensor("out", (NSEQ, OUT_LEN, D), F32, kind="ExternalOutput").ap())
    build(nc, *args)
    got = run_bass_kernel_spmd(nc, [arrays], core_ids=[0])
    return got.results[0]["out"]
```

```python
from contextlib import ExitStack

import concourse.bass as bass
from concourse import mybir

F32 = mybir.dt.float32
F32R = mybir.dt.float32r
ALU = mybir.AluOpType
ACT = mybir.ActivationFunctionType
AX = mybir.AxisListType

NSEQ, SEQ, D = 8, 750, 128
POOL = 3
OUT_LEN = SEQ - POOL + 1
PAIRS = NSEQ // 2
TOK = 125
NT = SEQ // TOK
NCH = 2
TPC = NT // NCH
CH = TPC * TOK
LAST = OUT_LEN - (NT - 1) * TOK
HALF = D // 2
HEADS, HD = 8, 16
QH = 4
HE = HD + 1
NV = HEADS * HE
HID = 256
EXP = 8
GROUPS, EG = 2, 4
NG = GROUPS + EXP
BANKS, BANK = 8, 512
EPS = 1e-5

WCOLS = {}


def _layout():
    at = 0
    for name, width in [
        ("ident", D), ("compress", HALF), ("conv", 3 * D), ("expand", D), ("ff1", HALF), ("ff2", D), ("vecs", 16),
        ("q", D), ("k", D), ("v", D + HEADS), ("out", D), ("tri", TOK), ("ones", TOK), ("blocks", NV), ("own", QH),
        ("row_v", D + HEADS), ("row_out", D), ("row_scale", D), ("row_gate", NG), ("gate", NG),
        ("bias_rows", D), ("shared_out", 2 * D), ("before", EG * EG), ("after", EG * EG),
        ("halfneg", NT), ("eps", NT), ("eps_rms", NT), ("scale_two", NT), ("eps_two", NT),
    ]:
        WCOLS[name] = (at, at + width)
        at += width
    return at


NW = _layout()
W_FIRST = WCOLS["q"][0]
VECS = ["compress", "main", "expand", "conv_g", "conv_b", "ff1", "ff2", "ff_g", "ff_b", "q", "k", "ln_g", "ln_b"]

SPLIT = {"shared_in": (0, 2 * HID), "expert_in": (2 * HID, 4 * HID), "expert_out": (4 * HID, 4 * HID + 2 * EXP * D)}
NSPLIT = 4 * HID + 2 * EXP * D

PARTS = [slice(2 * TOK * p, 2 * TOK * (p + 1)) for p in range(NT // 2)]
HIDDEN_UNITS = 2 * len(PARTS) * 4
SHARED_UNITS = 2 * NCH * 2
EXPERT_UNITS = 2 * NT * 2
BACK = HIDDEN_UNITS + SHARED_UNITS + EXPERT_UNITS

FILLS = dict(
    compress=2, conv=2, expand0=0, expand1=2, y_tm00=1, y_tm01=1, y_tm10=1, y_tm11=2, y_wait=2, y_cm00=1, y_cm01=2,
    y_cm10=1, y_cm11=1, ff1=2, ff20=1, ff21=1, z_tm0=0, z_tm1=2, z_wait=0, z_cm0=2, z_cm1=0, pool=1, h_tm0=2,
    h_tm1=0, n3_cm=1, q=1, k=0, v=1, k_tm0=0, k_tm1=1, cum=0, s0=1, a0=0, s1=1, a1=0, s2=1, a2=1, s3=1, a3=3, s4=0,
    a4=0, s5=4, a5=1, s6=1, a6=0, s7=1, a7=0, s8=1, a8=1, s9=0, a9=0, s10=1, a10=0, s11=1, a11=1, at_cm=1, out=1,
    rms=0, h_res=0, f_norm=1, f_cm=0,
)
assert sum(FILLS.values()) == BACK

STAND_INS = dict(k_tm1=8, cum=16, **{f"{x}{n}": count for n in range(2 * NT) for x, count in (("s", 2), ("a", 1))})


def units_of(stage, lag=0):
    names = list(FILLS)
    first = sum(FILLS[n] for n in names[:names.index(stage)])
    last = first + FILLS[stage]
    return range(max(first - lag, 0), BACK if stage == names[-1] else max(last - lag, 0))


PER_PAIR = dict(
    small=12, scaled=2, ms_ready=2, h1_ready=2, h2_ready=2, r1_ready=4, y_ready=4, g_ready=2, r2_ready=4, z_ready=4,
    pooled=4, h_copied=4, n3_ready=4, in_exp=8, in_relu=8, q_ready=4, k_ready=4, q_split=12, v_ready=4, ktm_ready=4, lam_exp=2,
    lam_ready=2, log_ready=2, cum_clipped=2, dk_ready=2, vd_ready=2, masked=24, den_ready=4, at_ready=4,
    atc_ready=4, o_ready=4, sq_ready=2, rms_ready=2, o_scaled=4, r3_ready=4, f_ready=4, f_high=4, f_low=4, gl_ready=2,
    route_exp=1, route=19, cnt_ready=1, cnt_t=4, silu_ready=24, hidden_ready=24, high_ready=12, low_ready=12,
    shared_added=4, acc=96, chunk_done=4, state_copied=10, stats=16, var_ready=8, rstd_ready=8, norm=16, eps_added=8,
    pe_compress=2, pe_conv=2, pe_expand=4, pe_t=12, pe_back=16, pe_ff1=2, pe_ff2=4, pe_q=4, pe_k=4, pe_v=4, pe_tk=4,
    pe_cum=2, pe_s=24, pe_num=12, pe_state=10, pe_tat=4, pe_o=4, pe_gate=2, pe_cnt=4, pe_in=24, pe_shared=4,
    pe_exp=24,
)


def build(nc, wpack, wsplit, x, out):
    with ExitStack() as ctx:
        def sb(name, shape, dtype=F32):
            return ctx.enter_context(nc.sbuf_tensor(name, shape, dtype))

        W = sb("weights", [D, NW])

        def w(name, a=0, b=None, p=D):
            lo, hi = WCOLS[name]
            return W[0:p, lo + a:(hi if b is None else lo + b)]

        def vec(name, p0=0, p1=D):
            c = WCOLS["vecs"][0] + VECS.index(name)
            return W[p0:p1, c:c + 1]

        xs = [sb(f"x{s}", [D, SEQ]) for s in range(2)]
        h1 = sb("conv1", [D, SEQ + 2])
        h2 = sb("conv2", [D, SEQ])
        g = sb("g", [D, SEQ])
        r = [sb(f"r{s}", [D, SEQ]) for s in range(2)]
        ntm = [sb(f"ntm{s}", [D, NT, D]) for s in range(2)]
        y = [sb(f"y{s}", [D, SEQ]) for s in range(2)]
        z = [sb(f"z{s}", [D, SEQ]) for s in range(2)]
        m2 = h2
        h = [sb(f"h{s}", [D, SEQ]) for s in range(2)]
        st = [sb(f"st{s}", [D, NT, 6]) for s in range(2)]
        mv = [sb(f"mv{s}", [D, NT, 2]) for s in range(2)]
        ve = [sb(f"ve{s}", [D, NT]) for s in range(2)]
        rstd = [sb(f"rstd{s}", [D, NT]) for s in range(2)]
        e_in = [z[i // 2][:, (i % 2) * CH:(i % 2 + 1) * CH] for i in range(4)]
        r_in = [(h2, g)[i // 2][:, (i % 2) * CH:(i % 2 + 1) * CH] for i in range(4)]
        q = r
        k = [sb(f"k{s}", [D, SEQ]) for s in range(2)]
        q_own = [sb(f"q_own{i}", [D, QH, TOK]) for i in range(3)]
        ktm = ntm
        v = [sb(f"v{s}", [D, NT, D + HEADS]) for s in range(2)]
        lam = [sb(f"lam{s}", [D, NT, HEADS]) for s in range(2)]
        lam2 = [sb(f"lam2{s}", [D, NT, HEADS]) for s in range(2)]
        logl = [sb(f"logl{s}", [D, NT, HEADS]) for s in range(2)]
        cum = [sb(f"cum{s}", [D, NT, HEADS]) for s in range(2)]
        dk = [sb(f"dk{s}", [D, NT, HEADS]) for s in range(2)]
        dk4 = [sb(f"dk4{s}", [D, NT, HEADS]) for s in range(2)]
        vd = [sb(f"vd{s}", [D, NT, HEADS, HE]) for s in range(2)]
        sm = [sb(f"sm{s}", [D, HEADS, TOK]) for s in range(2)]
        state = [sb(f"state{s}", [D, NV]) for s in range(2)]
        den = [sb(f"den{s}", [D, TPC, HEADS]) for s in range(2)]
        rden = [sb(f"rden{s}", [D, TPC, HEADS]) for s in range(2)]
        at = [sb(f"at{s}", [D, NT, HEADS, HD]) for s in range(2)]
        atc = k
        o = [t[:, :, :, :].rearrange("p t a b -> p t (a b)") for t in at]
        ss = [sb(f"ss{s}", [D, NT]) for s in range(2)]
        ms = [sb(f"ms{s}", [D, NT]) for s in range(2)]
        rrms = [sb(f"rrms{s}", [D, NT]) for s in range(2)]
        o2 = ntm
        h_tm = [sb(f"h_tm{s}", [D, NT, D]) for s in range(2)]
        r3 = [sb(f"r3{s}", [D, NT, D]) for s in range(2)]
        gl = sb("gl", [D, 2 * NT, NG])
        gind = sb("gind", [D, 2 * NT, GROUPS])
        rt = [sb(f"rt{i}", [D, 2 * NT, GROUPS, EG]) for i in range(7)]
        rr = [sb(f"rr{i}", [D, 2 * NT * GROUPS]) for i in range(5)]
        sm_flat = [t[:, :, :].rearrange("p a n -> p (a n)") for t in sm]
        npair = 2 * NT * GROUPS * EG * EG
        pair4 = [sm_flat[1][:, i * npair:(i + 1) * npair].rearrange("p (g a b) -> p g a b", a=EG, b=EG)
                 for i in range(2)]
        cmp8 = sm_flat[0][:, 0:2 * npair].rearrange("p (g a b) -> p g a b", a=EG, b=2 * EG)
        comb = sb("comb", [D, 2 * NT, GROUPS, EG])
        cnt9 = sb("cnt9", [D, 2 * NT, EXP + 1])
        cnt_t = sb("cnt_t", [EXP + 1, 2, CH])
        sil = [sb(f"sil{i}", [D, PARTS[0].stop]) for i in range(3)]
        f = y
        f_hi = [sb(f"f_hi{s}", [D, SEQ], F32R) for s in range(2)]
        f_lo = [sb(f"f_lo{s}", [D, SEQ], F32R) for s in range(2)]
        h_shared = [[sb(f"h_shared{s}{hh}", [D, SEQ]) for hh in range(2)] for s in range(2)]
        h_exp = [sb(f"h_exp{i}", [D, PARTS[0].stop]) for i in range(4)]
        h_hi = [[sb(f"h_hi{s}{hh}", [D, SEQ], F32R) for hh in range(2)] for s in range(2)]
        h_lo = [[sb(f"h_lo{s}{hh}", [D, SEQ], F32R) for hh in range(2)] for s in range(2)]
        result = [sb(f"result{s}", [D, NT, D]) for s in range(2)]
        acc2 = [sb(f"acc2{i}", [D, TPC, D]) for i in range(2)]
        w_hi = sb("w_hi", [D, NSPLIT], F32R)
        w_lo = sb("w_lo", [D, NSPLIT], F32R)
        staged = []
        for buffer in ([t[:, :, :].rearrange("p t n -> p (t n)") for t in result]
                       + [t[:, :] for t in h_shared[0] + h_shared[1]]):
            at_col = staged[-1][2] if staged else 0
            if at_col < NSPLIT:
                staged.append((buffer, at_col, min(at_col + buffer.shape[1], NSPLIT)))
        scratch = sb("scratch", [1, 8])
        PS = ctx.enter_context(nc.psum_tensor("PS", [D, BANKS, BANK], F32))

        S = {n: ctx.enter_context(nc.semaphore(n)) for n in PER_PAIR}
        N = PER_PAIR
        w_first = ctx.enter_context(nc.semaphore("w_first"))
        w_rest = ctx.enter_context(nc.semaphore("w_rest"))
        w_staged = ctx.enter_context(nc.semaphore("w_staged"))
        w_high = ctx.enter_context(nc.semaphore("w_high"))
        w_low = ctx.enter_context(nc.semaphore("w_low"))
        x_in = ctx.enter_context(nc.semaphore("x_in"))
        result_free = ctx.enter_context(nc.semaphore("result_free"))
        cleared = ctx.enter_context(nc.semaphore("cleared"))

        def sc(s, c):
            return 2 * s + c

        def tiles_of(c):
            return range(c * TPC, (c + 1) * TPC)

        def cols(c):
            return slice(c * CH, (c + 1) * CH)

        def tile(i):
            return slice(i * TOK, (i + 1) * TOK)

        def tm_bank(b, width=D, p=TOK):
            return PS[0:p, b, 0:TPC * width].rearrange("p (t n) -> p t n", t=TPC)

        def part(name, half, a, b):
            return (w_hi, w_lo)[half][:, SPLIT[name][0] + a:SPLIT[name][0] + b]

        def hidden_unit(n):
            return n // (4 * len(PARTS)), n // 4 % len(PARTS), n // 2 % 2, n % 2

        def expert_count(n):
            return n // 4 * 2 + max(n % 4 - 2, 0)

        def shared_unit(n):
            m = n - HIDDEN_UNITS
            return (m // 4, m // 2 % 2, m % 2) if 0 <= m < SHARED_UNITS else None

        def expert_unit(n):
            m = n - HIDDEN_UNITS - SHARED_UNITS
            return m // (2 * NT), m // 2 % NT, m % 2

        block = ctx.enter_context(nc.Block())

        @block.sync
        def _(sp):
            sp.dma_start(W[:, 0:W_FIRST], wpack[:, 0:W_FIRST]).then_inc(w_first, 16)

            def load(pair):
                for s in range(2):
                    sp.dma_start(xs[s][:, :], x[:, bass.ds((2 * pair + s) * SEQ, SEQ)]).then_inc(x_in, 16)

            def store(pair):
                for s in range(2):
                    sp.wait_ge(S["chunk_done"], pair * N["chunk_done"] + 2 * s + 2)
                    dst = out[bass.ds(2 * pair + s, 1), :, :].rearrange("o l d -> (o l) d")
                    full = (NT - 1) * TOK
                    sp.dma_start(dst[0:full, :].rearrange("(t p) d -> p t d", p=TOK),
                                 result[s][0:TOK, 0:NT - 1, :]).then_inc(result_free, 16)
                    sp.dma_start(dst[full:OUT_LEN, :], result[s][0:LAST, NT - 1, :]).then_inc(result_free, 16)

            load(0)
            sp.dma_start(W[:, W_FIRST:NW], wpack[:, W_FIRST:NW]).then_inc(w_rest, 16)
            for buffer, lo, hi in staged:
                sp.dma_start(buffer[:, 0:hi - lo], wsplit[:, lo:hi]).then_inc(w_staged, 16)
            sp.wait_ge(S["r1_ready"], N["r1_ready"])
            load(1)
            with sp.Fori(1, PAIRS - 1) as it:
                sp.wait_ge(S["r1_ready"], it * N["r1_ready"] + N["r1_ready"])
                load(it + 1)
                store(it - 1)
            store(PAIRS - 2)
            store(PAIRS - 1)
            sp.wait_ge(result_free, (PAIRS + 1) * 4 * 16)

        @block.gpsimd
        def _(pool):
            TT = nc.gpsimd.tensor_tensor
            nc.gpsimd.memset(h1[:, 0:1], 0.0).then_inc(cleared, 1)
            nc.gpsimd.memset(h1[:, SEQ + 1:SEQ + 2], 0.0).then_inc(cleared, 1)
            for s in range(2):
                nc.gpsimd.memset(h[s][:, OUT_LEN:SEQ], 0.0).then_inc(cleared, 1)
            nc.gpsimd.memset(cnt9[0:TOK, :, EXP:EXP + 1], 1.0).then_inc(cleared, 1)
            nc.gpsimd.memset(acc2[0][0:1, 0, 0:1], 0.0).then_inc(result_free, 64)
            pool.wait_ge(w_rest, 16)

            def back(pair, units):
                for n in units:
                    if 0 <= n - 3 < HIDDEN_UNITS and hidden_unit(n - 3)[2]:
                        s, p, _, hh = hidden_unit(n - 3)
                        e = expert_count(n - 3)
                        cs = PARTS[p]
                        pool.wait_ge(S["high_ready"], pair * N["high_ready"] + e + 1)
                        TT(h_lo[s][hh][:, cs], h_exp[e % 4][:, :],
                           h_hi[s][hh][:, cs].bitcast(F32), ALU.subtract).then_inc(S["low_ready"], 1)
                    if n >= HIDDEN_UNITS + SHARED_UNITS:
                        s, i, half = expert_unit(n)
                        if half and i % TPC == TPC - 1:
                            c = i // TPC
                            pool.wait_ge(S["acc"], pair * N["acc"] + 24 * (sc(s, c) + 1))
                            dst = result[s][0:TOK, c * TPC:(c + 1) * TPC, :]
                            TT(dst, dst, acc2[c][0:TOK, :, :], ALU.add).then_inc(S["chunk_done"], 1)

            def front(it, first):
                def fill(stage):
                    if not first:
                        back(it - 1, units_of(stage, lag=2))

                def power(norm, s):
                    pool.wait_ge(S["var_ready"], it * N["var_ready"] + 2 * norm + s + 1)
                    var, eps = mv[s][0:TOK, :, 1], "eps"
                    if norm == 3:
                        TT(ms[s][0:TOK, :], var, w("scale_two", p=TOK), ALU.mult).then_inc(S["scaled"], 1)
                        pool.wait_ge(S["scaled"], it * N["scaled"] + s + 1)
                        var, eps = ms[s][0:TOK, :], "eps_two"
                    TT(ve[s][0:TOK, :], var, w(eps, p=TOK), ALU.add).then_inc(S["eps_added"], 1)
                    pool.wait_ge(S["eps_added"], it * N["eps_added"] + 2 * norm + s + 1)
                    TT(rstd[s][0:TOK, :], ve[s][0:TOK, :], w("halfneg", p=TOK), ALU.pow).then_inc(S["rstd_ready"], 1)

                for stage in ("compress", "conv", "expand0", "expand1", "y_tm00", "y_tm01"):
                    fill(stage)
                power(0, 0)
                fill("y_tm10")
                fill("y_tm11")
                power(0, 1)
                for stage in ("y_wait", "y_cm00", "y_cm01", "y_cm10", "y_cm11"):
                    fill(stage)
                if first:
                    for n, (buffer, lo, hi) in enumerate(staged):
                        pool.wait_ge(w_high, n + 1)
                        TT(w_lo[:, lo:hi], buffer[:, 0:hi - lo], w_hi[:, lo:hi].bitcast(F32),
                           ALU.subtract).then_inc(w_low, 1)
                for stage in ("ff1", "ff20", "ff21", "z_tm0"):
                    fill(stage)
                power(1, 0)
                fill("z_tm1")
                power(1, 1)
                for stage in ("z_wait", "z_cm0", "z_cm1", "pool", "h_tm0"):
                    fill(stage)
                power(2, 0)
                fill("h_tm1")
                power(2, 1)
                fill("n3_cm")
                fill("q")
                for stage in ("k", "v", "k_tm0", "k_tm1", "cum"):
                    fill(stage)

                def own_heads(n):
                    i, s = n // 2, n % 2
                    if i % TPC == 0:
                        pool.wait_ge(S["q_ready"], it * N["q_ready"] + sc(s, i // TPC) + 1)
                    if n >= 3:
                        pool.wait_ge(S["pe_s"], it * N["pe_s"] + 2 * (n - 2))
                    TT(q_own[n % 3][:, :, :], q[s][:, tile(i)].unsqueeze(1).broadcast_to([D, QH, TOK]),
                       w("own").unsqueeze(2).broadcast_to([D, QH, TOK]), ALU.mult).then_inc(S["q_split"], 1)

                own_heads(0)
                own_heads(1)
                for n in range(2 * NT):
                    if n + 2 < 2 * NT:
                        own_heads(n + 2)
                    fill(f"s{n}")
                    fill(f"a{n}")
                fill("at_cm")
                fill("out")
                for s in range(2):
                    pool.wait_ge(S["sq_ready"], it * N["sq_ready"] + s + 1)
                    TT(ms[s][0:TOK, :], ss[s][0:TOK, :], w("eps_rms", p=TOK), ALU.add).then_inc(S["ms_ready"], 1)
                    pool.wait_ge(S["ms_ready"], it * N["ms_ready"] + s + 1)
                    TT(rrms[s][0:TOK, :], ms[s][0:TOK, :], w("halfneg", p=TOK), ALU.pow).then_inc(S["rms_ready"], 1)
                for s in range(2):
                    power(3, s)
                for stage in ("rms", "h_res", "f_norm"):
                    fill(stage)
                for s in range(2):
                    for c in range(NCH):
                        pool.wait_ge(S["f_high"], it * N["f_high"] + sc(s, c) + 1)
                        TT(f_lo[s][:, cols(c)], f[s][:, cols(c)], f_hi[s][:, cols(c)].bitcast(F32),
                           ALU.subtract).then_inc(S["f_low"], 1)
                fill("f_cm")

            front(0, True)
            with pool.Fori(1, PAIRS) as it:
                front(it, False)
            back(PAIRS - 1, range(BACK))

        @block.tensor
        def _(pe):
            mm = nc.tensor.matmul

            def to_tm(src, s, c, bank):
                for j, i in enumerate(tiles_of(c)):
                    last = nc.tensor.transpose(PS[0:TOK, bank, j * D:(j + 1) * D], src[s][:, tile(i)], w("ident"))
                return last

            def to_cm(src, s, c, bank):
                for j, i in enumerate(tiles_of(c)):
                    last = nc.tensor.transpose(PS[:, bank, tile(j)], src[s][0:TOK, i, :], w("ident", 0, TOK, TOK))
                return last

            def back(pair, units, banks=(6, 7)):
                for n in units:
                    bank = banks[n % len(banks)] if n < HIDDEN_UNITS else 6 + n % 2
                    if n < HIDDEN_UNITS:
                        s, p, expert, hh = hidden_unit(n)
                        cs = PARTS[p]
                        if n == 0:
                            pe.wait_ge(S["f_low"], pair * N["f_low"] + 2)
                            pe.wait_ge(S["gl_ready"], pair * N["gl_ready"] + 2)
                        if n == HIDDEN_UNITS // 2:
                            pe.wait_ge(S["f_low"], pair * N["f_low"] + 4)
                        if n >= len(banks):
                            pe.wait_ge(S["hidden_ready"], pair * N["hidden_ready"] + n - len(banks) + 1)
                        name = ("shared_in", "expert_in")[expert]
                        for b in range(2):
                            col = b * HID + hh * D
                            dst = PS[:, bank, b * 2 * TOK:(b + 1) * 2 * TOK]
                            mm(dst, part(name, 0, col, col + D), f_hi[s][:, cs], start=True, stop=False)
                            mm(dst, part(name, 0, col, col + D), f_lo[s][:, cs], start=False, stop=False)
                            last = mm(dst, part(name, 1, col, col + D), f_hi[s][:, cs], start=False, stop=True)
                        last.then_inc(S["pe_in"], 1)
                        continue
                    if shared_unit(n):
                        s, c, main = shared_unit(n)
                        n_chunk = sc(s, c)
                        if not main:
                            if n_chunk == 0:
                                pe.wait_ge(S["hidden_ready"], pair * N["hidden_ready"] + HIDDEN_UNITS - 1)
                            else:
                                pe.wait_ge(S["cnt_t"], pair * N["cnt_t"] + n_chunk)
                            for j, i in enumerate(tiles_of(c)):
                                last = nc.tensor.transpose(PS[0:EXP + 1, bank, tile(j)], cnt9[0:TOK, s * NT + i, :],
                                                           w("ident", 0, TOK, TOK))
                            last.then_inc(S["pe_cnt"], 1)
                            continue
                        if n_chunk == 0:
                            pe.wait_ge(S["hidden_ready"], pair * N["hidden_ready"] + HIDDEN_UNITS)
                        else:
                            pe.wait_ge(S["shared_added"], pair * N["shared_added"] + n_chunk)
                        for j, i in enumerate(tiles_of(c)):
                            for hh in range(2):
                                mm(PS[0:TOK, bank, j * D:(j + 1) * D], h_shared[s][hh][:, tile(i)],
                                   w("shared_out", hh * D, (hh + 1) * D), start=j == 0 and hh == 0, stop=False,
                                   skip_group_check=True)
                        pe.wait_ge(S["cnt_t"], pair * N["cnt_t"] + n_chunk + 1)
                        for j in range(TPC):
                            last = mm(PS[0:TOK, bank, j * D:(j + 1) * D], cnt_t[0:EXP + 1, c, tile(j)],
                                      w("bias_rows", p=EXP + 1), start=False, stop=j == TPC - 1,
                                      skip_group_check=True)
                        last.then_inc(S["pe_shared"], 1)
                        continue
                    s, i, half = expert_unit(n)
                    if i == 0 and half == 0:
                        pe.wait_ge(S["low_ready"], pair * N["low_ready"] + (s + 1) * 2 * len(PARTS))
                    before = n - HIDDEN_UNITS - SHARED_UNITS
                    if before >= 2:
                        pe.wait_ge(S["acc"], pair * N["acc"] + EG * (before - 1))
                    elif half:
                        pe.wait_ge(S["shared_added"], pair * N["shared_added"] + 4)
                    dst = PS[0:TOK, bank, :]
                    for hh in range(2):
                        col = hh * EXP * D + half * BANK
                        hi, lo = h_hi[s][hh][:, tile(i)], h_lo[s][hh][:, tile(i)]
                        mm(dst, hi, part("expert_out", 0, col, col + BANK), start=hh == 0, stop=False)
                        mm(dst, hi, part("expert_out", 1, col, col + BANK), start=False, stop=False)
                        last = mm(dst, lo, part("expert_out", 0, col, col + BANK), start=False, stop=hh == 1)
                    last.then_inc(S["pe_exp"], 1)

            def front(it, first):
                def fill(stage):
                    if not first:
                        back(it - 1, units_of(stage))
                        return
                    if stage == "y_wait":
                        pe.wait_ge(w_high, len(staged))
                    for _ in range(STAND_INS.get(stage, 0)):
                        mm(PS[:, 6, :], w_hi[:, 0:D], w_hi[:, 0:BANK], start=True, stop=True)

                pe.wait_ge(x_in, it * 32 + 32)
                for c in range(NCH):
                    for s in range(2):
                        last = mm(PS[HALF * s:HALF * (s + 1), 2 + c, 0:CH], w("compress"), xs[s][:, cols(c)],
                                  start=True, stop=True)
                    last.then_inc(S["pe_compress"], 1)
                fill("compress")
                pe.wait_ge(S["h1_ready"], it * N["h1_ready"] + 2)
                if not first:
                    pe.wait_ge(S["gl_ready"], it * N["gl_ready"])
                for c in range(NCH):
                    for tap in range(3):
                        last = mm(PS[:, c, 0:CH], w("conv", tap * D, (tap + 1) * D),
                                  h1[:, c * CH + tap:c * CH + tap + CH], start=tap == 0, stop=tap == 2)
                    last.then_inc(S["pe_conv"], 1)
                fill("conv")
                pe.wait_ge(S["h2_ready"], it * N["h2_ready"] + 2)
                for s in range(2):
                    for c in range(NCH):
                        rows = slice(HALF * s, HALF * (s + 1))
                        lo, hi = WCOLS["expand"]
                        mm(PS[:, 4 - 2 * s + c, 0:CH], W[rows, lo:hi], h2[rows, cols(c)], start=True,
                           stop=True).then_inc(S["pe_expand"], 1)
                    fill(f"expand{s}")
                for s in range(2):
                    for c in range(NCH):
                        pe.wait_ge(S["r1_ready"], it * N["r1_ready"] + sc(s, c) + 1)
                        to_tm(r, s, c, sc(s, c)).then_inc(S["pe_t"], 1)
                        fill(f"y_tm{s}{c}")
                fill("y_wait")
                for s in range(2):
                    for c in range(NCH):
                        pe.wait_ge(S["norm"], it * N["norm"] + sc(s, c) + 1)
                        to_cm(ntm, s, c, 4 * (1 - s) + c).then_inc(S["pe_back"], 1)
                        fill(f"y_cm{s}{c}")
                pe.wait_ge(S["y_ready"], it * N["y_ready"] + 4)
                for c in range(NCH):
                    for s in range(2):
                        last = mm(PS[HALF * s:HALF * (s + 1), 2 + c, 0:CH], w("ff1"), y[s][:, cols(c)],
                                  start=True, stop=True)
                    last.then_inc(S["pe_ff1"], 1)
                fill("ff1")
                pe.wait_ge(S["g_ready"], it * N["g_ready"] + 2)
                for s in range(2):
                    for c in range(NCH):
                        rows = slice(HALF * s, HALF * (s + 1))
                        lo, hi = WCOLS["ff2"]
                        mm(PS[:, 4 - 2 * s + c, 0:CH], W[rows, lo:hi], g[rows, cols(c)], start=True,
                           stop=True).then_inc(S["pe_ff2"], 1)
                    fill(f"ff2{s}")
                for s in range(2):
                    for c in range(NCH):
                        pe.wait_ge(S["r2_ready"], it * N["r2_ready"] + sc(s, c) + 1)
                        to_tm(r, s, c, sc(s, c)).then_inc(S["pe_t"], 1)
                    fill(f"z_tm{s}")
                fill("z_wait")
                for s in range(2):
                    for c in range(NCH):
                        pe.wait_ge(S["norm"], it * N["norm"] + 4 + sc(s, c) + 1)
                        to_cm(ntm, s, c, 4 * (1 - s) + c).then_inc(S["pe_back"], 1)
                    fill(f"z_cm{s}")
                fill("pool")
                for s in range(2):
                    pe.wait_ge(S["pooled"], it * N["pooled"] + 2 * s + 2)
                    for c in range(NCH):
                        if s == 0:
                            pe.wait_ge(S["z_ready"], it * N["z_ready"] + c + 3)
                        to_tm(h, s, c, sc(s, c)).then_inc(S["pe_t"], 1)
                    fill(f"h_tm{s}")
                fill("n3_cm")
                for s in range(2):
                    for c in range(NCH):
                        pe.wait_ge(S["norm"], it * N["norm"] + 8 + sc(s, c) + 1)
                        to_cm(ntm, s, c, 4 * (1 - s) + c).then_inc(S["pe_back"], 1)
                if first:
                    pe.wait_ge(w_rest, 16)
                for s in range(2):
                    for c in range(NCH):
                        pe.wait_ge(S["n3_ready"], it * N["n3_ready"] + c + 3)
                        mm(PS[:, sc(s, c), 0:CH], w("q"), y[s][:, cols(c)], start=True,
                           stop=True).then_inc(S["pe_q"], 1)
                fill("q")
                for s in range(2):
                    for c in range(NCH):
                        if s:
                            pe.wait_ge(S["in_relu"], it * N["in_relu"] + c + 1)
                        mm(PS[:, 4 * (1 - s) + c, 0:CH], w("k"), y[s][:, cols(c)], start=True,
                           stop=True).then_inc(S["pe_k"], 1)
                fill("k")
                for s in range(2):
                    for c in range(NCH):
                        pe.wait_ge(S["in_relu"], it * N["in_relu"] + 2 + 2 * s + c + 1)
                        for j, i in enumerate(tiles_of(c)):
                            last = mm(PS[0:TOK, 2 + 2 * s + c, j * (D + HEADS):(j + 1) * (D + HEADS)],
                                      y[s][:, tile(i)], w("v"), start=True, stop=True)
                        last.then_inc(S["pe_v"], 1)
                fill("v")
                for s in range(2):
                    for c in range(NCH):
                        pe.wait_ge(S["k_ready"], it * N["k_ready"] + sc(s, c) + 1)
                        if s:
                            pe.wait_ge(S["v_ready"], it * N["v_ready"] + c + 1)
                        else:
                            pe.wait_ge(S["in_relu"], it * N["in_relu"] + 6 + c + 1)
                        to_tm(k, s, c, sc(s, c)).then_inc(S["pe_tk"], 1)
                    fill(f"k_tm{s}")
                for s in range(2):
                    pe.wait_ge(S["log_ready"], it * N["log_ready"] + s + 1)
                    if s == 0:
                        pe.wait_ge(S["v_ready"], it * N["v_ready"] + 4)
                    dst = PS[0:TOK, 4 + s, 0:NT * HEADS].rearrange("p (t n) -> p t n", t=NT)
                    mm(dst, w("tri", p=TOK), logl[s][0:TOK, :, :], start=True, stop=False)
                    for before in range(1, NT):
                        last = mm(dst[:, before:NT, :], w("ones", p=TOK), logl[s][0:TOK, 0:NT - before, :],
                                  start=False, stop=before == NT - 1)
                    last.then_inc(S["pe_cum"], 1)
                fill("cum")

                def scores(n, i, s):
                    for b in range(2):
                        u = 2 * n + b
                        if u < 2:
                            pe.wait_ge(S["ktm_ready"], it * N["ktm_ready"] + b + 1)
                        else:
                            pe.wait_ge(S["masked"], it * N["masked"] + u - 1)
                        if b == 0:
                            pe.wait_ge(S["q_split"], it * N["q_split"] + n + 1)
                        rows = slice(b * D // 2, (b + 1) * D // 2)
                        mm(PS[0:TOK, b, 0:QH * TOK].rearrange("p (a n) -> p a n", a=QH), k[s][rows, tile(i)],
                           q_own[n % 3][rows, :, :], start=True, stop=True,
                           tile_position=(b * D // 2, 0)).then_inc(S["pe_s"], 1)
                    fill(f"s{n}")

                def attend(i, s):
                    if i == 0:
                        pe.wait_ge(S["vd_ready"], it * N["vd_ready"] + s + 1)
                    if i == TPC:
                        pe.wait_ge(S["at_ready"], it * N["at_ready"] + s + 1)
                    base = (i % TPC) * NV
                    if i > 0:
                        pe.wait_ge(S["state_copied"], it * N["state_copied"] + 2 * (i - 1) + s + 1)
                        mm(PS[0:TOK, 2 + s, base:base + NV], q[s][:, tile(i)], state[s][:, :],
                           start=True, stop=False, skip_group_check=True)
                    pe.wait_ge(S["masked"], it * N["masked"] + 4 * i + 2 * s + 2)
                    for hd in range(HEADS):
                        last = mm(PS[0:TOK, 2 + s, base + hd * HE:base + (hd + 1) * HE],
                                  sm[s][0:TOK, hd, :], vd[s][0:TOK, i, hd, :],
                                  start=(i == 0 and hd == 0), stop=hd == HEADS - 1, skip_group_check=True)
                    last.then_inc(S["pe_num"], 1)
                    if i < NT - 1:
                        mm(PS[:, 4 + s, 0:NV], ktm[s][0:TOK, i, :], vd[s][0:TOK, i, :, :].rearrange("p a b -> p (a b)"),
                           start=i == 0, stop=True, skip_group_check=True).then_inc(S["pe_state"], 1)

                steps = [(i, s) for i in range(NT) for s in range(2)]
                for n, (i, s) in enumerate(steps):
                    scores(n, i, s)
                    if n:
                        attend(*steps[n - 1])
                    fill(f"a{n}")
                attend(*steps[-1])
                for s in range(2):
                    for c in range(NCH):
                        pe.wait_ge(S["at_ready"], it * N["at_ready"] + 2 * c + s + 1)
                        at_cm = [t[:, :, :, :].rearrange("p t a b -> p t (a b)") for t in at]
                        to_cm(at_cm, s, c, sc(s, c)).then_inc(S["pe_tat"], 1)
                fill("at_cm")
                for s in range(2):
                    for c in range(NCH):
                        pe.wait_ge(S["atc_ready"], it * N["atc_ready"] + sc(s, c) + 1)
                        if s:
                            pe.wait_ge(S["o_ready"], it * N["o_ready"] + c + 1)
                        for j, i in enumerate(tiles_of(c)):
                            last = mm(PS[0:TOK, 4 + c, j * D:(j + 1) * D], atc[s][:, tile(i)], w("out"),
                                      start=True, stop=True)
                        last.then_inc(S["pe_o"], 1)
                fill("out")
                fill("rms")
                fill("h_res")
                fill("f_norm")
                for s in range(2):
                    for c in range(NCH):
                        pe.wait_ge(S["norm"], it * N["norm"] + 12 + sc(s, c) + 1)
                        to_cm(ntm, s, c, 4 - 2 * s + c).then_inc(S["pe_back"], 1)
                fill("f_cm")
                for s in range(2):
                    pe.wait_ge(S["f_ready"], it * N["f_ready"] + 2 * s + 2)
                    for i in range(NT):
                        last = mm(PS[0:TOK, s, i * NG:(i + 1) * NG], f[s][:, tile(i)], w("gate"), start=True,
                                  stop=True)
                    last.then_inc(S["pe_gate"], 1)

            pe.wait_ge(w_first, 16)
            front(0, True)
            pe.wait_ge(w_low, len(staged))
            with pe.Fori(1, PAIRS) as it:
                front(it, False)
            back(PAIRS - 1, range(BACK), banks=(6, 7, 4, 5))

        @block.scalar
        def _(act):
            A = nc.scalar.activation

            def back(pair, units, banks=(6, 7)):
                for n in units:
                    if n < HIDDEN_UNITS:
                        act.wait_ge(S["pe_in"], pair * N["pe_in"] + n + 1)
                        if n >= 3:
                            act.wait_ge(S["hidden_ready"], pair * N["hidden_ready"] + n - 2)
                        A(sil[n % 3][:, :], PS[:, banks[n % len(banks)], 0:2 * TOK], ACT.Silu).then_inc(S["silu_ready"], 1)
                    if 0 <= n - 2 < HIDDEN_UNITS and hidden_unit(n - 2)[2]:
                        s, p, _, hh = hidden_unit(n - 2)
                        act.wait_ge(S["hidden_ready"], pair * N["hidden_ready"] + n - 1)
                        A(h_hi[s][hh][:, PARTS[p]], h_exp[expert_count(n - 2) % 4][:, :],
                          ACT.Identity).then_inc(S["high_ready"], 1)
                    if shared_unit(n) and not shared_unit(n)[2]:
                        s, c, _ = shared_unit(n)
                        act.wait_ge(S["pe_cnt"], pair * N["pe_cnt"] + sc(s, c) + 1)
                        A(cnt_t[0:EXP + 1, c, :], PS[0:EXP + 1, 6, 0:CH], ACT.Identity).then_inc(S["cnt_t"], 1)

            def front(it, first):
                def fill(stage):
                    if not first:
                        back(it - 1, units_of(stage))

                for c in range(NCH):
                    act.wait_ge(S["pe_compress"], it * N["pe_compress"] + c + 1)
                    A(h1[:, 1 + c * CH:1 + (c + 1) * CH], PS[:, 2 + c, 0:CH], ACT.Silu,
                      bias=vec("compress")).then_inc(S["h1_ready"], 1)
                fill("compress")
                for c in range(NCH):
                    act.wait_ge(S["pe_conv"], it * N["pe_conv"] + c + 1)
                    A(h2[:, cols(c)], PS[:, c, 0:CH], ACT.Silu, bias=vec("main")).then_inc(S["h2_ready"], 1)
                fill("conv")
                if first:
                    for n, (buffer, lo, hi) in enumerate(staged):
                        if n == 0:
                            act.wait_ge(w_staged, 16 * len(staged))
                        A(w_hi[:, lo:hi], buffer[:, 0:hi - lo], ACT.Identity).then_inc(w_high, 1)
                for stage in ("expand0", "expand1", "y_tm00", "y_tm01", "y_tm10", "y_tm11", "y_wait"):
                    fill(stage)
                for s in range(2):
                    for c in range(NCH):
                        act.wait_ge(S["pe_back"], it * N["pe_back"] + sc(s, c) + 1)
                        A(y[s][:, cols(c)], PS[:, 4 * (1 - s) + c, 0:CH], ACT.Identity, bias=vec("conv_b"),
                          scale=vec("conv_g")).then_inc(S["y_ready"], 1)
                        fill(f"y_cm{s}{c}")
                for c in range(NCH):
                    act.wait_ge(S["pe_ff1"], it * N["pe_ff1"] + c + 1)
                    A(g[:, cols(c)], PS[:, 2 + c, 0:CH], ACT.Gelu, bias=vec("ff1")).then_inc(S["g_ready"], 1)
                for stage in ("ff1", "ff20", "ff21", "z_tm0", "z_tm1", "z_wait"):
                    fill(stage)
                for s in range(2):
                    for c in range(NCH):
                        act.wait_ge(S["pe_back"], it * N["pe_back"] + 4 + sc(s, c) + 1)
                        A(z[s][:, cols(c)], PS[:, 4 * (1 - s) + c, 0:CH], ACT.Identity, bias=vec("ff_b"),
                          scale=vec("ff_g")).then_inc(S["z_ready"], 1)
                    fill(f"z_cm{s}")
                nc.scalar.preload_act_table_set("natural_log_exp_and_others")
                fill("pool")
                for s in range(2):
                    fill(f"h_tm{s}")
                    for c in range(NCH):
                        act.wait_ge(S["stats"], it * N["stats"] + 8 + sc(s, c) + 1)
                        A(h_tm[s][0:TOK, c * TPC:(c + 1) * TPC, :], tm_bank(sc(s, c)),
                          ACT.Identity).then_inc(S["h_copied"], 1)
                fill("n3_cm")
                for s in range(2):
                    for c in range(NCH):
                        act.wait_ge(S["pe_back"], it * N["pe_back"] + 8 + sc(s, c) + 1)
                        act.wait_ge(S["r2_ready"], it * N["r2_ready"] + 4)
                        A(y[s][:, cols(c)], PS[:, 4 * (1 - s) + c, 0:CH], ACT.Identity).then_inc(S["n3_ready"], 1)
                if first:
                    act.wait_ge(w_rest, 16)
                for n, (name, projected) in enumerate((("q", S["pe_q"]), ("k", S["pe_k"]))):
                    for s in range(2):
                        for c in range(NCH):
                            act.wait_ge(projected, it * N["pe_q"] + sc(s, c) + 1)
                            if n:
                                act.wait_ge(S["q_ready"], it * N["q_ready"] + sc(s, c) + 1)
                            src = PS[:, 4 * (1 - s) + c if n else sc(s, c), 0:CH]
                            A(e_in[sc(s, c)], src, ACT.Exp, bias=vec(name)).then_inc(S["in_exp"], 1)
                            A(r_in[sc(s, c)], src, ACT.Relu, bias=vec(name)).then_inc(S["in_relu"], 1)
                    fill(name)
                fill("v")
                for s in range(2):
                    act.wait_ge(S["v_ready"], it * N["v_ready"] + 2 * s + 2)
                    A(lam[s][0:TOK, :, :], v[s][0:TOK, :, D:D + HEADS], ACT.Exp, scale=-1.0).then_inc(S["lam_exp"], 1)
                for s in range(2):
                    for c in range(NCH):
                        act.wait_ge(S["pe_tk"], it * N["pe_tk"] + sc(s, c) + 1)
                        A(ktm[s][0:TOK, c * TPC:(c + 1) * TPC, :], tm_bank(sc(s, c)),
                          ACT.Identity).then_inc(S["ktm_ready"], 1)
                    fill(f"k_tm{s}")
                for s in range(2):
                    act.wait_ge(S["lam_ready"], it * N["lam_ready"] + s + 1)
                    A(logl[s][0:TOK, :, :], lam[s][0:TOK, :, :], ACT.Ln).then_inc(S["log_ready"], 1)
                for s in range(2):
                    act.wait_ge(S["cum_clipped"], it * N["cum_clipped"] + s + 1)
                    A(dk[s][0:TOK, :, :], cum[s][0:TOK, :, :], ACT.Exp, scale=-1.0).then_inc(S["dk_ready"], 1)
                fill("cum")
                for n in range(2 * NT):
                    fill(f"s{n}")
                    fill(f"a{n}")
                for s in range(2):
                    for c in range(NCH):
                        act.wait_ge(S["pe_tat"], it * N["pe_tat"] + sc(s, c) + 1)
                        A(atc[s][:, cols(c)], PS[:, sc(s, c), 0:CH], ACT.Identity).then_inc(S["atc_ready"], 1)
                fill("at_cm")
                for s in range(2):
                    act.wait_ge(S["o_ready"], it * N["o_ready"] + 2 * s + 2)
                    for i in range(NT):
                        last = A(sm_flat[s][0:TOK, i * D:(i + 1) * D], o[s][0:TOK, i, :],
                                 ACT.Square, scale=D ** -0.5, accum_out=ss[s][0:TOK, i:i + 1])
                    last.then_inc(S["sq_ready"], 1)
                for stage in ("out", "rms", "h_res", "f_norm"):
                    fill(stage)
                for s in range(2):
                    for c in range(NCH):
                        act.wait_ge(S["pe_back"], it * N["pe_back"] + 12 + sc(s, c) + 1)
                        A(f[s][:, cols(c)], PS[:, 4 - 2 * s + c, 0:CH], ACT.Identity, bias=vec("ln_b"),
                          scale=vec("ln_g")).then_inc(S["f_ready"], 1)
                fill("f_cm")
                act.wait_ge(S["route"], it * N["route"] + 4)
                A(rt[1][0:TOK], rt[0][0:TOK], ACT.Exp).then_inc(S["route_exp"], 1)

            act.wait_ge(w_first, 16)
            act.wait_ge(cleared, 5)
            front(0, True)
            with act.Fori(1, PAIRS) as it:
                front(it, False)
            back(PAIRS - 1, range(BACK), banks=(6, 7, 4, 5))

        @block.vector
        def _(dve):
            V = nc.vector
            G2 = 2 * NT * GROUPS

            def flat(t):
                return t[0:TOK].rearrange("p t a b -> p (t a) b")

            def over4(col):
                return col[0:TOK, :].unsqueeze(2).broadcast_to([TOK, G2, EG])

            def table(name):
                return w(name, p=TOK).rearrange("p (a b) -> p a b", a=EG).unsqueeze(1).broadcast_to(
                    [TOK, G2, EG, EG])

            def route_step(pair, n, ins):
                ins.then_inc(S["route"], 1)
                dve.wait_ge(S["route"], pair * N["route"] + n)

            def route(pair, n):
                prob = flat(rt[2])
                if n == 0:
                    dve.wait_ge(S["route_exp"], pair * N["route_exp"] + 1)
                    route_step(pair, 5, V.tensor_reduce(rr[1][0:TOK, :], flat(rt[1]), AX.X, ALU.add))
                    route_step(pair, 6, V.reciprocal(rr[2][0:TOK, :], rr[1][0:TOK, :]))
                    V.tensor_tensor(prob, flat(rt[1]), over4(rr[2]), ALU.mult).then_inc(S["route"], 1)
                if n == 1:
                    other = prob.unsqueeze(2).broadcast_to([TOK, G2, EG, EG])
                    own = prob.unsqueeze(3).broadcast_to([TOK, G2, EG, EG])
                    dve.wait_ge(S["route"], pair * N["route"] + 7)
                    V.tensor_tensor(pair4[0][0:TOK], other, own, ALU.is_gt).then_inc(S["route"], 1)
                    V.tensor_tensor(pair4[1][0:TOK], other, own, ALU.is_ge).then_inc(S["route"], 1)
                if n == 2:
                    dve.wait_ge(S["route"], pair * N["route"] + 9)
                    V.tensor_tensor(cmp8[0:TOK, :, :, 0:EG], pair4[0][0:TOK], table("after"),
                                    ALU.mult).then_inc(S["route"], 1)
                    route_step(pair, 11, V.tensor_tensor(cmp8[0:TOK, :, :, EG:2 * EG], pair4[1][0:TOK],
                                                         table("before"), ALU.mult))
                    V.tensor_reduce(flat(rt[3]), cmp8[0:TOK], AX.X, ALU.add).then_inc(S["route"], 1)
                if n == 3:
                    dve.wait_ge(S["route"], pair * N["route"] + 12)
                    route_step(pair, 13, V.tensor_scalar(flat(rt[4]), flat(rt[3]), 1.5, None, ALU.is_lt))
                    route_step(pair, 14, V.tensor_tensor(flat(rt[5]), prob, flat(rt[4]), ALU.mult))
                    route_step(pair, 15, V.tensor_reduce(rr[3][0:TOK, :], flat(rt[5]), AX.X, ALU.add))
                    V.tensor_scalar_add(rr[4][0:TOK, :], rr[3][0:TOK, :], 1e-8).then_inc(S["route"], 1)
                if n == 4:
                    dve.wait_ge(S["route"], pair * N["route"] + 16)
                    route_step(pair, 17, V.reciprocal(rr[0][0:TOK, :], rr[4][0:TOK, :]))
                    route_step(pair, 18, V.tensor_tensor(flat(rt[6]), flat(rt[5]), over4(rr[0]), ALU.mult))
                    chosen = gind[0:TOK].unsqueeze(3).broadcast_to([TOK, 2 * NT, GROUPS, EG])
                    route_step(pair, 19, V.tensor_tensor(comb[0:TOK], rt[6][0:TOK], chosen, ALU.mult))
                    V.tensor_tensor(cnt9[0:TOK, :, 0:EXP].rearrange("p t (a b) -> p t a b", a=GROUPS), rt[4][0:TOK],
                                    chosen, ALU.mult).then_inc(S["cnt_ready"], 1)

            def back(pair, units, banks=(6, 7)):
                for n in units:
                    if n < HIDDEN_UNITS:
                        s, p, expert, hh = hidden_unit(n)
                        dve.wait_ge(S["silu_ready"], pair * N["silu_ready"] + n + 1)
                        dst = h_shared[s][hh][:, PARTS[p]]
                        if expert:
                            e = expert_count(n)
                            if e >= 4:
                                dve.wait_ge(S["low_ready"], pair * N["low_ready"] + e - 3)
                            dst = h_exp[e % 4][:, :]
                        V.tensor_tensor(dst, sil[n % 3][:, :], PS[:, banks[n % len(banks)], 2 * TOK:4 * TOK],
                                        ALU.mult).then_inc(S["hidden_ready"], 1)
                        route(pair, n)
                        continue
                    if shared_unit(n):
                        s, c, main = shared_unit(n)
                        if main:
                            if sc(s, c) == 0:
                                dve.wait_ge(result_free, 64 * (pair + 1))
                            dve.wait_ge(S["pe_shared"], pair * N["pe_shared"] + sc(s, c) + 1)
                            chunk = slice(c * TPC, (c + 1) * TPC)
                            V.tensor_tensor(result[s][0:TOK, chunk, :], tm_bank(7), r3[s][0:TOK, chunk, :],
                                            ALU.add).then_inc(S["shared_added"], 1)
                        continue
                    s, i, half = expert_unit(n)
                    before = n - HIDDEN_UNITS - SHARED_UNITS
                    dve.wait_ge(S["pe_exp"], pair * N["pe_exp"] + before + 1)
                    if i % TPC == 0 and half == 0:
                        dve.wait_ge(S["shared_added"], pair * N["shared_added"] + sc(s, i // TPC) + 1)
                    sums = result[s][0:TOK, i, :], acc2[i // TPC][0:TOK, i % TPC, :]
                    for e in range(EG):
                        src = PS[0:TOK, 6 + half, e * D:(e + 1) * D]
                        share = comb[0:TOK, s * NT + i, half, e:e + 1]
                        dst = sums[e % 2]
                        if half or e >= 2:
                            dve.wait_ge(S["acc"], pair * N["acc"] + EG * before + e - 1)
                        if half == 0 and e == 1:
                            if s and i % TPC == 0:
                                dve.wait_ge(S["chunk_done"], pair * N["chunk_done"] + i // TPC + 1)
                            V.tensor_scalar(dst, src, share, None, ALU.mult).then_inc(S["acc"], 1)
                        else:
                            V.scalar_tensor_tensor(dst, src, share, dst, ALU.mult, ALU.add).then_inc(S["acc"], 1)

            def front(it, first):
                def fill(stage):
                    if not first:
                        back(it - 1, units_of(stage, lag=1))

                smalls = [0]

                def small(ins):
                    ins.then_inc(S["small"], 1)
                    smalls[0] += 1
                    dve.wait_ge(S["small"], it * N["small"] + smalls[0])

                def statistics(norm, s, c, src):
                    u = 4 * norm + sc(s, c) + 1
                    for j, i in enumerate(tiles_of(c)):
                        last = V.bn_stats(st[s][0:TOK, i, :], src(j, i))
                    last.then_inc(S["stats"], 1)
                    if c == 1:
                        dve.wait_ge(S["stats"], it * N["stats"] + u)
                        n = 2 * norm + s
                        V.memset(scratch[0:1, n:n + 1], 0.0)
                        for i in range(NT):
                            last = V.bn_aggr(mv[s][0:TOK, i, :], st[s][0:TOK, i, :])
                        last.then_inc(S["var_ready"], 1)

                def normalise(norm, s, c, src):
                    if norm == 2:
                        dve.wait_ge(S["h_copied"], it * N["h_copied"] + sc(s, c) + 1)
                    if c == 0:
                        dve.wait_ge(S["rstd_ready"], it * N["rstd_ready"] + 2 * norm + s + 1)
                    for j, i in enumerate(tiles_of(c)):
                        last = V.tensor_scalar(ntm[s][0:TOK, i, :], src(j, i), mv[s][0:TOK, i, 0:1],
                                               rstd[s][0:TOK, i:i + 1], ALU.subtract, ALU.mult)
                    last.then_inc(S["norm"], 1)

                def norm_from_psum(norm, tm_stage, wait_stage, cm_stage, by_chunk):
                    for s in range(2):
                        for c in range(NCH):
                            dve.wait_ge(S["pe_t"], it * N["pe_t"] + 4 * norm + sc(s, c) + 1)
                            statistics(norm, s, c, lambda j, i: PS[0:TOK, sc(s, c), j * D:(j + 1) * D])
                            if by_chunk:
                                fill(f"{tm_stage}{s}{c}")
                        if not by_chunk:
                            fill(f"{tm_stage}{s}")
                    fill(wait_stage)
                    for s in range(2):
                        for c in range(NCH):
                            normalise(norm, s, c, lambda j, i: PS[0:TOK, sc(s, c), j * D:(j + 1) * D])
                            if by_chunk:
                                fill(f"{cm_stage}{s}{c}")
                        if not by_chunk and cm_stage:
                            fill(f"{cm_stage}{s}")

                fill("compress")
                fill("conv")
                for s in range(2):
                    for c in range(NCH):
                        dve.wait_ge(S["pe_expand"], it * N["pe_expand"] + sc(s, c) + 1)
                        V.scalar_tensor_tensor(r[s][:, cols(c)], PS[:, 4 - 2 * s + c, 0:CH], vec("expand"),
                                               xs[s][:, cols(c)], ALU.add, ALU.add).then_inc(S["r1_ready"], 1)
                    fill(f"expand{s}")
                norm_from_psum(0, "y_tm", "y_wait", "y_cm", True)
                fill("ff1")
                for s in range(2):
                    for c in range(NCH):
                        dve.wait_ge(S["pe_ff2"], it * N["pe_ff2"] + sc(s, c) + 1)
                        V.scalar_tensor_tensor(r[s][:, cols(c)], PS[:, 4 - 2 * s + c, 0:CH], vec("ff2"),
                                               y[s][:, cols(c)], ALU.add, ALU.add).then_inc(S["r2_ready"], 1)
                    fill(f"ff2{s}")
                norm_from_psum(1, "z_tm", "z_wait", "z_cm", False)
                fill("pool")
                for s in range(2):
                    dve.wait_ge(S["z_ready"], it * N["z_ready"] + 2 * s + 2)
                    if s:
                        dve.wait_ge(S["pooled"], it * N["pooled"] + 2)
                    V.tensor_tensor(m2[:, 0:SEQ - 1], z[s][:, 0:SEQ - 1], z[s][:, 1:SEQ], ALU.max).then_inc(S["pooled"], 1)
                    dve.wait_ge(S["pooled"], it * N["pooled"] + 2 * s + 1)
                    V.tensor_tensor(h[s][:, 0:OUT_LEN], m2[:, 0:OUT_LEN], z[s][:, 2:SEQ], ALU.max).then_inc(S["pooled"], 1)
                norm_from_psum(2, "h_tm", "n3_cm", None, False)
                for ready, dst, n in ((S["q_ready"], q, 0), (S["k_ready"], k, 4)):
                    for s in range(2):
                        for c in range(NCH):
                            dve.wait_ge(S["in_relu"], it * N["in_relu"] + n + sc(s, c) + 1)
                            V.scalar_tensor_tensor(dst[s][:, cols(c)], e_in[sc(s, c)], 1.0,
                                                       r_in[sc(s, c)], ALU.min, ALU.add).then_inc(ready, 1)
                    fill("k" if n else "q")
                if first:
                    dve.wait_ge(w_rest, 16)
                for s in range(2):
                    for c in range(NCH):
                        dve.wait_ge(S["pe_v"], it * N["pe_v"] + sc(s, c) + 1)
                        bias = w("row_v", p=TOK).unsqueeze(1).broadcast_to([TOK, TPC, D + HEADS])
                        V.tensor_tensor(v[s][0:TOK, c * TPC:(c + 1) * TPC, :], tm_bank(2 + 2 * s + c, D + HEADS),
                                            bias, ALU.add).then_inc(S["v_ready"], 1)
                fill("v")
                for s in range(2):
                    dve.wait_ge(S["lam_exp"], it * N["lam_exp"] + s + 1)
                    small(V.tensor_scalar_add(lam2[s][0:TOK, :, :], lam[s][0:TOK, :, :], 1.0))
                    small(V.reciprocal(lam[s][0:TOK, :, :], lam2[s][0:TOK, :, :]))
                    small(V.tensor_scalar(lam2[s][0:TOK, :, :], lam[s][0:TOK, :, :], 0.1, 0.9, ALU.mult, ALU.add))
                    V.tensor_scalar_max(lam[s][0:TOK, :, :], lam2[s][0:TOK, :, :], 1e-6).then_inc(S["lam_ready"], 1)
                fill("k_tm0")
                fill("k_tm1")
                for s in range(2):
                    dve.wait_ge(S["pe_cum"], it * N["pe_cum"] + s + 1)
                    V.tensor_scalar(cum[s][0:TOK, :, :], PS[0:TOK, 4 + s, 0:NT * HEADS].rearrange(
                        "p (t n) -> p t n", t=NT), 50.0, -50.0, ALU.min, ALU.max).then_inc(S["cum_clipped"], 1)
                for s in range(2):
                    dve.wait_ge(S["dk_ready"], it * N["dk_ready"] + s + 1)
                    small(V.tensor_scalar_mul(dk4[s][0:TOK, :, :], dk[s][0:TOK, :, :], HD ** -0.5))
                    V.tensor_copy(vd[s][0:TOK, :, :, HD:HE], dk4[s][0:TOK, :, :].unsqueeze(3))
                    V.tensor_tensor(vd[s][0:TOK, :, :, 0:HD],
                                        v[s][0:TOK, :, 0:D].rearrange("p t (a b) -> p t a b", a=HEADS),
                                        dk4[s][0:TOK, :, :].unsqueeze(3).broadcast_to([TOK, NT, HEADS, HD]),
                                        ALU.mult).then_inc(S["vd_ready"], 1)

                fill("cum")

                def mask(n, i, s):
                    for half in range(2):
                        dve.wait_ge(S["pe_s"], it * N["pe_s"] + 4 * i + 2 * s + half + 1)
                        if i > 0 and half == 0:
                            dve.wait_ge(S["pe_num"], it * N["pe_num"] + 2 * (i - 1) + s + 1)
                        causal = w("tri", p=TOK).unsqueeze(1).broadcast_to([TOK, QH, TOK])
                        src = PS[0:TOK, half, 0:QH * TOK].rearrange("p (a n) -> p a n", a=QH)
                        V.tensor_tensor(sm[s][0:TOK, QH * half:QH * (half + 1), :], src, causal,
                                        ALU.mult).then_inc(S["masked"], 1)
                    fill(f"s{n}")

                def copy_state(i, s):
                    dve.wait_ge(S["pe_state"], it * N["pe_state"] + 2 * i + s + 1)
                    V.tensor_tensor(state[s][:, :], PS[:, 4 + s, 0:NV], w("blocks"), ALU.mult).then_inc(S["state_copied"], 1)

                def divide(c, s):
                    dve.wait_ge(S["pe_num"], it * N["pe_num"] + 2 * (TPC * (c + 1) - 1) + s + 1)
                    nd = PS[0:TOK, 2 + s, 0:TPC * NV].rearrange("p (t a b) -> p t a b", t=TPC, a=HEADS)
                    small(V.scalar_tensor_tensor(den[s][0:TOK, :, :], dk4[s][0:TOK, c * TPC:(c + 1) * TPC, :],
                                                 1e-6 * HD ** 0.5, nd[:, :, :, HD], ALU.mult, ALU.add))
                    V.reciprocal(rden[s][0:TOK, :, :], den[s][0:TOK, :, :]).then_inc(S["den_ready"], 1)
                    dve.wait_ge(S["den_ready"], it * N["den_ready"] + 2 * c + s + 1)
                    V.tensor_tensor(at[s][0:TOK, c * TPC:(c + 1) * TPC, :, :], nd[:, :, :, 0:HD],
                                        rden[s][0:TOK, :, :].unsqueeze(3).broadcast_to([TOK, TPC, HEADS, HD]),
                                        ALU.mult).then_inc(S["at_ready"], 1)

                steps = [(i, s) for i in range(NT) for s in range(2)]
                for n, (i, s) in enumerate(steps):
                    mask(n, i, s)
                    if n:
                        pi, psq = steps[n - 1]
                        if pi < NT - 1:
                            copy_state(pi, psq)
                        if pi == TPC - 1:
                            divide(0, psq)
                        if pi == NT - 1:
                            divide(1, psq)
                    fill(f"a{n}")
                divide(1, 1)
                fill("at_cm")
                for s in range(2):
                    for c in range(NCH):
                        dve.wait_ge(S["pe_o"], it * N["pe_o"] + sc(s, c) + 1)
                        bias = w("row_out", p=TOK).unsqueeze(1).broadcast_to([TOK, TPC, D])
                        V.tensor_tensor(o[s][0:TOK, c * TPC:(c + 1) * TPC, :], tm_bank(4 + c), bias,
                                            ALU.add).then_inc(S["o_ready"], 1)
                for s in range(2):
                    for c in range(NCH):
                        chunk = slice(c * TPC, (c + 1) * TPC)
                        dve.wait_ge(S["o_ready"], it * N["o_ready"] + sc(s, c) + 1)
                        V.tensor_tensor(o2[s][0:TOK, chunk, :], o[s][0:TOK, chunk, :],
                                        w("row_scale", p=TOK).unsqueeze(1).broadcast_to([TOK, TPC, D]),
                                        ALU.mult).then_inc(S["o_scaled"], 1)
                fill("out")
                fill("rms")
                for s in range(2):
                    dve.wait_ge(S["rms_ready"], it * N["rms_ready"] + s + 1)
                    dve.wait_ge(S["o_scaled"], it * N["o_scaled"] + 2 * s + 2)
                    for c in range(NCH):
                        dve.wait_ge(S["h_copied"], it * N["h_copied"] + sc(s, c) + 1)
                        for i in tiles_of(c):
                            last = V.scalar_tensor_tensor(r3[s][0:TOK, i, :], o2[s][0:TOK, i, :],
                                                          rrms[s][0:TOK, i:i + 1],
                                                          h_tm[s][0:TOK, i, :], ALU.mult, ALU.add)
                        last.then_inc(S["r3_ready"], 1)
                    for c in range(NCH):
                        dve.wait_ge(S["r3_ready"], it * N["r3_ready"] + sc(s, c) + 1)
                        statistics(3, s, c, lambda j, i: r3[s][0:TOK, i, :])
                fill("h_res")
                for s in range(2):
                    for c in range(NCH):
                        normalise(3, s, c, lambda j, i: r3[s][0:TOK, i, :])
                fill("f_norm")
                for s in range(2):
                    for c in range(NCH):
                        dve.wait_ge(S["f_ready"], it * N["f_ready"] + sc(s, c) + 1)
                        V.tensor_copy(f_hi[s][:, cols(c)], f[s][:, cols(c)]).then_inc(S["f_high"], 1)
                fill("f_cm")

                for s in range(2):
                    dve.wait_ge(S["pe_gate"], it * N["pe_gate"] + s + 1)
                    src = PS[0:TOK, s, 0:NT * NG].rearrange("p (t n) -> p t n", t=NT)
                    V.tensor_tensor(gl[0:TOK, s * NT:(s + 1) * NT, :], src,
                                        w("row_gate", p=TOK).unsqueeze(1).broadcast_to([TOK, NT, NG]), ALU.add).then_inc(S["gl_ready"], 1)
                dve.wait_ge(S["gl_ready"], it * N["gl_ready"] + 2)
                logits = gl[0:TOK, :, GROUPS:NG].rearrange("p t (a b) -> p t a b", a=GROUPS)
                route_step(it, 1, V.tensor_tensor(gind[0:TOK, :, 1:2], gl[0:TOK, :, 1:2], gl[0:TOK, :, 0:1],
                                                  ALU.is_gt))
                route_step(it, 2, V.tensor_scalar(gind[0:TOK, :, 0:1], gind[0:TOK, :, 1:2], -1.0, 1.0, ALU.mult,
                                                  ALU.add))
                mx = rr[0][0:TOK, :].rearrange("p (t a) -> p t a", a=GROUPS)
                route_step(it, 3, V.tensor_reduce(mx, logits, AX.X, ALU.max))
                V.tensor_tensor(rt[0][0:TOK], logits, mx.unsqueeze(3).broadcast_to([TOK, 2 * NT, GROUPS, EG]),
                                ALU.subtract).then_inc(S["route"], 1)

            dve.wait_ge(w_first, 16)
            dve.wait_ge(cleared, 5)
            front(0, True)
            with dve.Fori(1, PAIRS) as it:
                front(it, False)
            back(PAIRS - 1, range(BACK), banks=(6, 7, 4, 5))


def kernel(**inputs):
    import numpy as np
    import concourse.bacc as bacc
    from concourse.bass_utils import run_bass_kernel_spmd

    a = {n.replace("L0_", ""): np.asarray(t) for n, t in inputs.items()}
    pack = np.zeros((D, NW), np.float32)

    def put(name, block, row=0, col=0):
        block = np.asarray(block, np.float32)
        at = WCOLS[name][0] + col
        pack[row:row + block.shape[0], at:at + block.shape[1]] = block

    put("ident", np.eye(D))
    put("compress", a["tok_w_compress"][:, :, 0].T)
    for tap in range(3):
        for s in range(2):
            put("conv", a["tok_w_main"][:, :, tap].T, HALF * s, tap * D + HALF * s)
    for s in range(2):
        put("expand", a["tok_w_expand"][:, :, 0].T, HALF * s)
        put("ff2", a["tok_w_ff2"].T, HALF * s)
    put("ff1", a["tok_w_ff1"].T)
    for name, source in [("compress", "tok_b_compress"), ("main", "tok_b_main"), ("ff1", "tok_b_ff1")]:
        for s in range(2):
            put("vecs", a[source][:, None], HALF * s, VECS.index(name))
    qkv_b = a["attn_qkv_b"].reshape(3, D)
    for name, column in [("expand", a["tok_b_expand"]), ("conv_g", a["tok_g_conv_norm"]),
                         ("conv_b", a["tok_b_conv_norm"]), ("ff2", a["tok_b_ff2"]), ("ff_g", a["tok_g_ff_norm"]),
                         ("ff_b", a["tok_b_ff_norm"]), ("q", qkv_b[0]), ("k", qkv_b[1]), ("ln_g", a["ffn_ln_scale"]),
                         ("ln_b", a["ffn_ln_bias"])]:
        put("vecs", column[:, None], 0, VECS.index(name))
    qkv_w = a["attn_qkv_w"].reshape(3, D, D)
    put("q", qkv_w[0].T)
    put("k", qkv_w[1].T)
    put("v", qkv_w[2].T)
    put("v", a["attn_decay_w"].T, 0, D)
    put("out", a["attn_out_w"].T)
    put("tri", np.triu(np.ones((TOK, TOK))))
    put("ones", np.ones((TOK, TOK)))
    put("blocks", np.kron(np.eye(HEADS), np.ones((HD, HE))))
    put("own", np.kron(np.ones((HEADS // QH, 1)), np.kron(np.eye(QH), np.ones((HD, 1)))))
    put("row_v", np.broadcast_to(qkv_b[2], (D, D)))
    put("row_v", np.broadcast_to(a["attn_decay_b"], (D, HEADS)), 0, D)
    put("row_out", np.broadcast_to(a["attn_out_b"], (D, D)))
    put("row_scale", np.broadcast_to(a["attn_norm_scale"], (D, D)))
    put("row_gate", np.broadcast_to(a["ffn_group_bias"], (D, GROUPS)))
    put("row_gate", np.broadcast_to(a["ffn_expert_bias"], (D, EXP)), 0, GROUPS)
    before = np.tril(np.ones((EG, EG)), -1)
    put("before", np.broadcast_to(before.reshape(-1), (D, EG * EG)))
    put("after", np.broadcast_to((1.0 - before).reshape(-1), (D, EG * EG)))
    put("halfneg", np.full((D, NT), -0.5))
    for name, value in [("eps", EPS), ("eps_rms", 1e-8), ("scale_two", 1.0 + EPS), ("eps_two", EPS * EPS)]:
        put(name, np.full((D, NT), value))
    split = np.zeros((D, NSPLIT), np.float32)

    def put_split(name, block, col=0):
        at = SPLIT[name][0] + col
        split[:, at:at + block.shape[1]] = block

    put_split("shared_in", a["ffn_shared_in_w"].T)
    put_split("expert_in", a["ffn_expert_in_w"].T)
    for half in range(2):
        rows = slice(half * D, (half + 1) * D)
        put("shared_out", a["ffn_shared_out_w"].T[rows], 0, half * D)
        put_split("expert_out", a["ffn_expert_out_weight"].transpose(2, 0, 1).reshape(HID, EXP * D)[rows],
                  half * EXP * D)
    put("gate", a["ffn_group_gate_w"].T)
    put("gate", a["ffn_expert_gate_w"].T, 0, GROUPS)
    put("bias_rows", a["ffn_expert_out_bias"])
    put("bias_rows", a["ffn_shared_out_b"][None, :], EXP)

    arrays = {
        "wpack": pack,
        "wsplit": split,
        "x_cm": np.ascontiguousarray(a["x"].transpose(2, 0, 1).reshape(D, NSEQ * SEQ)),
    }
    nc = bacc.Bacc("TRN2", target_bir_lowering=False, num_devices=1)
    args = [nc.dram_tensor(n, t.shape, mybir.dt.from_np(t.dtype), kind="ExternalInput").ap()
            for n, t in arrays.items()]
    args.append(nc.dram_tensor("out", (NSEQ, OUT_LEN, D), F32, kind="ExternalOutput").ap())
    build(nc, *args)
    got = run_bass_kernel_spmd(nc, [arrays], core_ids=[0])
    return got.results[0]["out"]
```
